# Optimizing a Trainium2 kernel written in Bass

```python
import numpy as np
import jax
import jax.numpy as jnp

def _softmax(x, axis=-1):
    return jax.nn.softmax(x, axis=axis)

def _gelu(x):
    return jax.nn.gelu(x, approximate=True)

def _silu(x):
    return jax.nn.silu(x)

def _sigmoid(x):
    return jax.nn.sigmoid(x)

def _layernorm(x, axis=-1, eps=1e-05):
    m = jnp.mean(x, axis=axis, keepdims=True)
    v = jnp.var(x, axis=axis, keepdims=True)
    return (x - m) / jnp.sqrt(v + eps)

def _scatter_add(tgt, idx, src, axis=0):
    return tgt.at[idx].add(src)

def _segment_sum(src, seg, n):
    return jax.ops.segment_sum(src, seg, n)
kernel_name = 'mk_perceiver_d2_seqx_r4_81c5ff'

def setup_inputs(seed: int=0):
    np.random.seed(seed)
    _w = jnp.asarray

    def _rec_inputs():
        import jax
        import jax.numpy as jnp
        _rk = jax.random.key(seed)
        x = 0.0002417 + 0.9998 * jax.random.normal(jax.random.fold_in(_rk, 1), (16, 64, 256), jnp.float32)
        _lenS = 64 - jax.random.randint(jax.random.fold_in(_rk, 7), (16,), 0, max(1, 64 // 4) + 1, jnp.int32)
        _lenS2 = 1601 - jax.random.randint(jax.random.fold_in(_rk, 8), (16,), 0, max(1, 1601 // 4) + 1, jnp.int32)
        _ctx_1024P = jax.random.normal(jax.random.fold_in(_rk, 11), (16, 16, 256), jnp.float32)
        _ctx_1024c = jax.random.dirichlet(jax.random.fold_in(_rk, 511), 0.3 * jnp.ones((16,), jnp.float32), (16, 1601))
        _ctx_1024t = jnp.einsum('bsk,bkd->bsd', _ctx_1024c, _ctx_1024P)
        _ctx_1024t = _ctx_1024t * jax.lax.rsqrt(jnp.mean(jnp.square(_ctx_1024t)) + 1e-12) * 0.953939
        ctx_1024 = 7.22013e-05 + 1.00017 * (_ctx_1024t + 0.3 * jax.random.normal(jax.random.fold_in(_rk, 611), (16, 1601, 256), jnp.float32))
        _validS = jnp.arange(64)[None, :] < _lenS[:, None]
        _validS2 = jnp.arange(1601)[None, :] < _lenS2[:, None]
        _causal = jnp.tril(jnp.ones((64, 64), dtype=bool))
        mask_BxS2_if0 = jnp.where(jnp.ones((16, 1601), dtype=bool), 0, 1).astype(jnp.int32)
        return (x, ctx_1024, mask_BxS2_if0)
    x, ctx_1024, mask_BxS2_if0 = _rec_inputs()

    def _L0_xattn_setup():
        import jax, jax.numpy as jnp
        import numpy as np
        import math
        B, M, D, H, NK = (4, 512, 256, 16, 5)
        HD = D // H

        def _gather_pad0(x, idx):
            Bx, Hx, W, hd = x.shape
            valid = (idx >= 0) & (idx < W)
            idxc = jnp.clip(idx, 0, W - 1).reshape(Bx, Hx, -1)
            g = jnp.take_along_axis(x, idxc[..., None], axis=2)
            g = g.reshape(idx.shape + (hd,))
            return g * valid[..., None].astype(x.dtype)
        key = jax.random.key(seed)
        ks = jax.random.split(key, 9)
        w = lambda k, shape: jax.random.normal(k, shape, jnp.float32) * 0.02
        return {'k': jax.random.normal(ks[0], (B, M, D), jnp.float32), 'v': jax.random.normal(ks[1], (B, M, D), jnp.float32), 'q': jax.random.normal(ks[2], (B, M, D), jnp.float32), 'mask': jnp.zeros((B, M), jnp.int32), 'Wk': w(ks[3], (D, D)), 'bk': jnp.zeros((D,), jnp.float32), 'Wv': w(ks[4], (D, D)), 'bv': jnp.zeros((D,), jnp.float32), 'Wq': w(ks[5], (D, D)), 'bq': jnp.zeros((D,), jnp.float32), 'Woff': w(ks[6], (H * NK, D)), 'boff': jnp.zeros((H * NK,), jnp.float32), 'Wo': w(ks[7], (D, D)), 'bo': jnp.zeros((D,), jnp.float32)}
    _L0_xattn_all = _L0_xattn_setup()
    _L0_xattn_in = {k: v for k, v in _L0_xattn_all.items() if k in ('Wk', 'bk', 'Wv', 'bv', 'Wq', 'bq', 'Woff', 'boff', 'Wo', 'bo')}
    del _L0_xattn_all

    def _L0_attn_setup():
        import jax, jax.numpy as jnp
        import numpy as np
        import math
        D_MODEL = 256
        LN_EPS = 1e-05

        def _layer_norm(x):
            mu = jnp.mean(x, axis=-1, keepdims=True)
            var = jnp.var(x, axis=-1, keepdims=True)
            return (x - mu) * jax.lax.rsqrt(var + LN_EPS)
        key = jax.random.key(seed)
        ks = jax.random.split(key, 5)
        B, S, D = (4, 512, D_MODEL)
        scale = 1.0 / math.sqrt(D)
        x = jax.random.normal(ks[0], (B, S, D), dtype=jnp.float32)
        Wq = jax.random.normal(ks[1], (D, D), dtype=jnp.float32) * scale
        Wk = jax.random.normal(ks[2], (D, D), dtype=jnp.float32) * scale
        Wv = jax.random.normal(ks[3], (D, D), dtype=jnp.float32) * scale
        Wo = jax.random.normal(ks[4], (D, D), dtype=jnp.float32) * scale
        b = jnp.zeros((D,), dtype=jnp.float32)
        layerscale = 0.0001 * jnp.ones((D,), dtype=jnp.float32)
        return {'x': x, 'Wq': Wq, 'bq': b, 'Wk': Wk, 'bk': b, 'Wv': Wv, 'bv': b, 'Wo': Wo, 'bo': b, 'layerscale': layerscale}
    _L0_attn_all = _L0_attn_setup()
    _L0_attn_in = {k: v for k, v in _L0_attn_all.items() if k in ('Wq', 'bq', 'Wk', 'bk', 'Wv', 'bv', 'Wo', 'bo', 'layerscale')}
    del _L0_attn_all

    def _L0_ffn_setup():
        import jax, jax.numpy as jnp
        import numpy as np
        B, L, D = (2, 256, 256)
        HID, E, K = (512, 8, 2)
        key = jax.random.key(seed)
        ks = jax.random.split(key, 4)
        std = 0.02
        return {'x': jax.random.normal(ks[0], (B, L, D), dtype=jnp.float32), 'router_scale': jnp.ones((D,), dtype=jnp.float32), 'router_w': jax.random.normal(ks[1], (D, E), dtype=jnp.float32) * std, 'gating_w': jax.random.normal(ks[2], (E, 2, HID, D), dtype=jnp.float32) * std, 'linear_w': jax.random.normal(ks[3], (E, HID, D), dtype=jnp.float32) * std, 'per_expert_scale': jnp.ones((E,), dtype=jnp.float32)}
    _L0_ffn_all = _L0_ffn_setup()
    _L0_ffn_in = {k: v for k, v in _L0_ffn_all.items() if k in ('router_scale', 'router_w', 'gating_w', 'linear_w', 'per_expert_scale')}
    del _L0_ffn_all

    def _L1_xattn_setup():
        import jax, jax.numpy as jnp
        import numpy as np
        HEADS = 16
        DIM_HEAD = 64
        INNER = HEADS * DIM_HEAD
        QUERY_DIM = 256
        CONTEXT_DIM = 256
        TEXT_LEN = 77
        IMG_SCALE = 1.0
        SCALE = DIM_HEAD ** (-0.5)

        def _attend(q, k, v):
            sim = jnp.einsum('bihd,bjhd->bhij', q, k) * SCALE
            attn = jax.nn.softmax(sim, axis=-1)
            out = jnp.einsum('bhij,bjhd->bihd', attn, v)
            B, N, H, D = out.shape
            return out.reshape(B, N, H * D)
        key = jax.random.key(seed)
        ks = jax.random.split(key, 10)
        B, N, Lc = (16, 512, 333)
        x = jax.random.normal(ks[0], (B, N, QUERY_DIM), dtype=jnp.float32)
        context = jax.random.normal(ks[1], (B, Lc, CONTEXT_DIM), dtype=jnp.float32)

        def w(k, din, dout):
            return jax.random.normal(k, (din, dout), dtype=jnp.float32) * din ** (-0.5)
        Wq = w(ks[2], QUERY_DIM, INNER)
        Wk = w(ks[3], CONTEXT_DIM, INNER)
        Wv = w(ks[4], CONTEXT_DIM, INNER)
        Wk_ip = w(ks[5], CONTEXT_DIM, INNER)
        Wv_ip = w(ks[6], CONTEXT_DIM, INNER)
        Wo = w(ks[7], INNER, QUERY_DIM)
        bo = jnp.zeros((QUERY_DIM,), dtype=jnp.float32)
        return {'x': x, 'context': context, 'Wq': Wq, 'Wk': Wk, 'Wv': Wv, 'Wk_ip': Wk_ip, 'Wv_ip': Wv_ip, 'Wo': Wo, 'bo': bo}
    _L1_xattn_all = _L1_xattn_setup()
    _L1_xattn_in = {k: v for k, v in _L1_xattn_all.items() if k in ('Wq', 'Wk', 'Wv', 'Wk_ip', 'Wv_ip', 'Wo', 'bo')}
    del _L1_xattn_all

    def _L1_attn_setup():
        import jax, jax.numpy as jnp
        import numpy as np
        BATCH, SEQ, D_MODEL = (4, 512, 256)
        D_STATE, D_CONV = (16, 4)

        def _silu(u):
            return u * jax.nn.sigmoid(u)
        key = jax.random.key(seed)
        ks = jax.random.split(key, 6)
        s = 0.02
        x = jax.random.normal(ks[0], (BATCH, SEQ, D_MODEL), jnp.float32)
        in_proj_w = jax.random.normal(ks[1], (2 * D_MODEL, D_MODEL), jnp.float32) * s
        conv_w = jax.random.normal(ks[2], (D_MODEL, D_CONV), jnp.float32) * s
        conv_b = jax.random.normal(ks[3], (D_MODEL,), jnp.float32) * s
        x_proj_w = jax.random.normal(ks[4], (2 * D_STATE + 1, D_MODEL), jnp.float32) * s
        A_log = jnp.log(jnp.broadcast_to(jnp.arange(1, D_STATE + 1, dtype=jnp.float32), (D_MODEL, D_STATE)))
        D_param = jnp.ones((D_MODEL,), jnp.float32)
        out_proj_w = jax.random.normal(ks[5], (D_MODEL, D_MODEL), jnp.float32) * s
        return {'x': x, 'in_proj_w': in_proj_w, 'conv_w': conv_w, 'conv_b': conv_b, 'x_proj_w': x_proj_w, 'A_log': A_log, 'D_param': D_param, 'out_proj_w': out_proj_w}
    _L1_attn_all = _L1_attn_setup()
    _L1_attn_in = {k: v for k, v in _L1_attn_all.items() if k in ('in_proj_w', 'conv_w', 'conv_b', 'x_proj_w', 'A_log', 'D_param', 'out_proj_w')}
    del _L1_attn_all

    def _L1_ffn_setup():
        import jax, jax.numpy as jnp
        import numpy as np
        TOPK = 4
        key = jax.random.key(seed)
        ks = jax.random.split(key, 9)
        B, T, D = (4, 512, 256)
        E, H = (32, 128)
        HS = H * TOPK
        s = lambda k, shape, fan: jax.random.normal(k, shape, dtype=jnp.float32) / np.sqrt(fan)
        return {'x': jax.random.normal(ks[0], (B, T, D), dtype=jnp.float32), 'router_w': s(ks[1], (E, D), D), 'router_bias': jnp.zeros((E,), dtype=jnp.float32), 'gate_w': s(ks[2], (E, H, D), D), 'up_w': s(ks[3], (E, H, D), D), 'down_w': s(ks[4], (E, D, H), H), 'sgate_w': s(ks[5], (HS, D), D), 'sup_w': s(ks[6], (HS, D), D), 'sdown_w': s(ks[7], (D, HS), HS)}
    _L1_ffn_all = _L1_ffn_setup()
    _L1_ffn_in = {k: v for k, v in _L1_ffn_all.items() if k in ('router_w', 'router_bias', 'gate_w', 'up_w', 'down_w', 'sgate_w', 'sup_w', 'sdown_w')}
    del _L1_ffn_all
    return {'x': x, 'ctx_1024': ctx_1024, 'mask_BxS2_if0': mask_BxS2_if0, 'L0_xattn_Wk': _L0_xattn_in['Wk'], 'L0_xattn_bk': _L0_xattn_in['bk'], 'L0_xattn_Wv': _L0_xattn_in['Wv'], 'L0_xattn_bv': _L0_xattn_in['bv'], 'L0_xattn_Wq': _L0_xattn_in['Wq'], 'L0_xattn_bq': _L0_xattn_in['bq'], 'L0_xattn_Woff': _L0_xattn_in['Woff'], 'L0_xattn_boff': _L0_xattn_in['boff'], 'L0_xattn_Wo': _L0_xattn_in['Wo'], 'L0_xattn_bo': _L0_xattn_in['bo'], 'L0_attn_Wq': _L0_attn_in['Wq'], 'L0_attn_bq': _L0_attn_in['bq'], 'L0_attn_Wk': _L0_attn_in['Wk'], 'L0_attn_bk': _L0_attn_in['bk'], 'L0_attn_Wv': _L0_attn_in['Wv'], 'L0_attn_bv': _L0_attn_in['bv'], 'L0_attn_Wo': _L0_attn_in['Wo'], 'L0_attn_bo': _L0_attn_in['bo'], 'L0_attn_layerscale': _L0_attn_in['layerscale'], 'L0_ffn_router_scale': _L0_ffn_in['router_scale'], 'L0_ffn_router_w': _L0_ffn_in['router_w'], 'L0_ffn_gating_w': _L0_ffn_in['gating_w'], 'L0_ffn_linear_w': _L0_ffn_in['linear_w'], 'L0_ffn_per_expert_scale': _L0_ffn_in['per_expert_scale'], 'L1_xattn_Wq': _L1_xattn_in['Wq'], 'L1_xattn_Wk': _L1_xattn_in['Wk'], 'L1_xattn_Wv': _L1_xattn_in['Wv'], 'L1_xattn_Wk_ip': _L1_xattn_in['Wk_ip'], 'L1_xattn_Wv_ip': _L1_xattn_in['Wv_ip'], 'L1_xattn_Wo': _L1_xattn_in['Wo'], 'L1_xattn_bo': _L1_xattn_in['bo'], 'L1_attn_in_proj_w': _L1_attn_in['in_proj_w'], 'L1_attn_conv_w': _L1_attn_in['conv_w'], 'L1_attn_conv_b': _L1_attn_in['conv_b'], 'L1_attn_x_proj_w': _L1_attn_in['x_proj_w'], 'L1_attn_A_log': _L1_attn_in['A_log'], 'L1_attn_D_param': _L1_attn_in['D_param'], 'L1_attn_out_proj_w': _L1_attn_in['out_proj_w'], 'L1_ffn_router_w': _L1_ffn_in['router_w'], 'L1_ffn_router_bias': _L1_ffn_in['router_bias'], 'L1_ffn_gate_w': _L1_ffn_in['gate_w'], 'L1_ffn_up_w': _L1_ffn_in['up_w'], 'L1_ffn_down_w': _L1_ffn_in['down_w'], 'L1_ffn_sgate_w': _L1_ffn_in['sgate_w'], 'L1_ffn_sup_w': _L1_ffn_in['sup_w'], 'L1_ffn_sdown_w': _L1_ffn_in['sdown_w']}

def reference(x, ctx_1024, mask_BxS2_if0, L0_xattn_Wk, L0_xattn_bk, L0_xattn_Wv, L0_xattn_bv, L0_xattn_Wq, L0_xattn_bq, L0_xattn_Woff, L0_xattn_boff, L0_xattn_Wo, L0_xattn_bo, L0_attn_Wq, L0_attn_bq, L0_attn_Wk, L0_attn_bk, L0_attn_Wv, L0_attn_bv, L0_attn_Wo, L0_attn_bo, L0_attn_layerscale, L0_ffn_router_scale, L0_ffn_router_w, L0_ffn_gating_w, L0_ffn_linear_w, L0_ffn_per_expert_scale, L1_xattn_Wq, L1_xattn_Wk, L1_xattn_Wv, L1_xattn_Wk_ip, L1_xattn_Wv_ip, L1_xattn_Wo, L1_xattn_bo, L1_attn_in_proj_w, L1_attn_conv_w, L1_attn_conv_b, L1_attn_x_proj_w, L1_attn_A_log, L1_attn_D_param, L1_attn_out_proj_w, L1_ffn_router_w, L1_ffn_router_bias, L1_ffn_gate_w, L1_ffn_up_w, L1_ffn_down_w, L1_ffn_sgate_w, L1_ffn_sup_w, L1_ffn_sdown_w):
    import jax
    import jax.numpy as jnp

    def _L0_xattn_ref(k, v, q, mask, Wk, bk, Wv, bv, Wq, bq, Woff, boff, Wo, bo):
        import jax, jax.numpy as jnp
        import numpy as np
        import math
        B, M, D, H, NK = (4, 512, 256, 16, 5)
        HD = D // H

        def _gather_pad0(x, idx):
            Bx, Hx, W, hd = x.shape
            valid = (idx >= 0) & (idx < W)
            idxc = jnp.clip(idx, 0, W - 1).reshape(Bx, Hx, -1)
            g = jnp.take_along_axis(x, idxc[..., None], axis=2)
            g = g.reshape(idx.shape + (hd,))
            return g * valid[..., None].astype(x.dtype)
        Bq, Q, _ = q.shape
        key_len = k.shape[1]
        K = jnp.einsum('bmd,ed->bme', k, Wk) + bk
        V = jnp.einsum('bmd,ed->bme', v, Wv) + bv
        Qp = jnp.einsum('bqd,ed->bqe', q, Wq) + bq
        off = jnp.einsum('bqd,ed->bqe', Qp, Woff) + boff
        off = off.reshape(Bq, Q, H, NK).transpose(0, 2, 1, 3)
        Kh = K.reshape(Bq, key_len, H, HD).transpose(0, 2, 1, 3)
        Vh = V.reshape(Bq, key_len, H, HD).transpose(0, 2, 1, 3)
        Qh = Qp.reshape(Bq, Q, H, HD).transpose(0, 2, 1, 3)
        loc = jnp.arange(Q, dtype=jnp.float32)[:, None]
        left = -NK // 2
        ref = jnp.arange(left, NK + left, dtype=jnp.float32)
        sign_lens = (1 - mask).sum(-1).astype(jnp.float32) - 1.0
        loc_x = jnp.mod(ref + off + loc, sign_lens[:, None, None, None])
        xg = loc_x / (key_len - 1) * 2.0 - 1.0
        ix = ((xg + 1.0) * key_len - 1.0) / 2.0
        x0 = jnp.floor(ix)
        dx = ix - x0
        i0 = x0.astype(jnp.int32)
        i1 = i0 + 1
        w0 = (1.0 - dx)[..., None]
        w1 = dx[..., None]
        sk = 0.5 * (w0 * _gather_pad0(Kh, i0) + w1 * _gather_pad0(Kh, i1))
        sv = 0.5 * (w0 * _gather_pad0(Vh, i0) + w1 * _gather_pad0(Vh, i1))
        scores = jnp.einsum('bhqd,bhqkd->bhqk', Qh / math.sqrt(HD), sk)
        attn = jax.nn.softmax(scores, axis=-1)
        ctx = jnp.einsum('bhqk,bhqkd->bhqd', attn, sv)
        ctx = ctx.transpose(0, 2, 1, 3).reshape(Bq, Q, H * HD)
        return jnp.einsum('bqd,ed->bqe', ctx, Wo) + bo

    def _L0_attn_ref(x, Wq, bq, Wk, bk, Wv, bv, Wo, bo, layerscale):
        import jax, jax.numpy as jnp
        import numpy as np
        import math
        D_MODEL = 256
        LN_EPS = 1e-05

        def _layer_norm(x):
            mu = jnp.mean(x, axis=-1, keepdims=True)
            var = jnp.var(x, axis=-1, keepdims=True)
            return (x - mu) * jax.lax.rsqrt(var + LN_EPS)
        B, S, D = x.shape
        q = jnp.einsum('bsd,ed->bse', x, Wq) + bq
        k = jnp.einsum('bsd,ed->bse', x, Wk) + bk
        v = jnp.einsum('bsd,ed->bse', x, Wv) + bv
        qn = _layer_norm(q)
        kn = _layer_norm(k)
        scores = jnp.einsum('bse,bte->bst', qn, kn) / jnp.sqrt(jnp.float32(D))
        attn = jax.nn.sigmoid(scores - jnp.log(jnp.float32(S)))
        out = jnp.einsum('bst,bte->bse', attn, v)
        proj = jnp.einsum('bsd,ed->bse', out, Wo) + bo
        return proj * layerscale

    def _L0_ffn_ref(x, router_scale, router_w, gating_w, linear_w, per_expert_scale):
        import jax, jax.numpy as jnp
        import numpy as np
        B, L, D = (2, 256, 256)
        HID, E, K = (512, 8, 2)
        d = x.shape[-1]
        var = jnp.mean(jnp.square(x), axis=-1, keepdims=True)
        r_in = x * jax.lax.rsqrt(var + 1e-06)
        r_in = r_in * jax.lax.rsqrt(jnp.array(d, dtype=r_in.dtype)) * router_scale
        logits = jnp.dot(r_in, router_w).astype(jnp.float32)
        probs = jax.nn.softmax(logits, axis=-1)
        _, top_k_idx = jax.lax.top_k(logits, K)
        indicator = jax.nn.one_hot(top_k_idx, probs.shape[-1], dtype=probs.dtype)
        gate_weights = indicator.sum(axis=-2) * probs
        renorm = jnp.sum(gate_weights, axis=-1, keepdims=True)
        renorm = jnp.where(renorm > 0.0, renorm, 1.0)
        weights = probs / renorm
        top_k_w = jnp.take_along_axis(weights, top_k_idx, axis=-1)
        combine = jnp.einsum('blke,blk->ble', indicator, top_k_w)
        combine = combine * per_expert_scale
        gate0 = jnp.einsum('bld,ehd->bleh', x, gating_w[:, 0])
        gate1 = jnp.einsum('bld,ehd->bleh', x, gating_w[:, 1])
        act = jax.nn.gelu(gate0) * gate1
        out = jnp.einsum('bleh,ehd,ble->bld', act, linear_w, combine)
        return out.astype(x.dtype)

    def _L1_xattn_ref(x, context, Wq, Wk, Wv, Wk_ip, Wv_ip, Wo, bo):
        import jax, jax.numpy as jnp
        import numpy as np
        HEADS = 16
        DIM_HEAD = 64
        INNER = HEADS * DIM_HEAD
        QUERY_DIM = 256
        CONTEXT_DIM = 256
        TEXT_LEN = 77
        IMG_SCALE = 1.0
        SCALE = DIM_HEAD ** (-0.5)

        def _attend(q, k, v):
            sim = jnp.einsum('bihd,bjhd->bhij', q, k) * SCALE
            attn = jax.nn.softmax(sim, axis=-1)
            out = jnp.einsum('bhij,bjhd->bihd', attn, v)
            B, N, H, D = out.shape
            return out.reshape(B, N, H * D)
        B, N, _ = x.shape
        ctx_txt = context[:, :TEXT_LEN, :]
        ctx_img = context[:, TEXT_LEN:, :]
        q = (x @ Wq).reshape(B, N, HEADS, DIM_HEAD)
        k = (ctx_txt @ Wk).reshape(B, TEXT_LEN, HEADS, DIM_HEAD)
        v = (ctx_txt @ Wv).reshape(B, TEXT_LEN, HEADS, DIM_HEAD)
        out = _attend(q, k, v)
        Li = ctx_img.shape[1]
        k_ip = (ctx_img @ Wk_ip).reshape(B, Li, HEADS, DIM_HEAD)
        v_ip = (ctx_img @ Wv_ip).reshape(B, Li, HEADS, DIM_HEAD)
        out_ip = _attend(q, k_ip, v_ip)
        out = out + IMG_SCALE * out_ip
        return out @ Wo + bo

    def _L1_attn_ref(x, in_proj_w, conv_w, conv_b, x_proj_w, A_log, D_param, out_proj_w):
        import jax, jax.numpy as jnp
        import numpy as np
        BATCH, SEQ, D_MODEL = (4, 512, 256)
        D_STATE, D_CONV = (16, 4)

        def _silu(u):
            return u * jax.nn.sigmoid(u)
        seq_len = x.shape[1]
        d_state = A_log.shape[1]
        xz = jnp.einsum('bld,ed->ble', x, in_proj_w)
        x_ssm, z = jnp.split(xz, 2, axis=-1)
        xpad = jnp.pad(x_ssm, ((0, 0), (D_CONV - 1, 0), (0, 0)))
        x_conv = conv_b
        acc = jnp.zeros_like(x_ssm)
        for k in range(D_CONV):
            acc = acc + xpad[:, k:k + seq_len, :] * conv_w[:, k]
        x_conv = _silu(acc + conv_b)
        ssm_params = jnp.einsum('bld,ed->ble', x_conv, x_proj_w)
        Bm = ssm_params[..., :d_state]
        Cm = ssm_params[..., d_state:2 * d_state]
        delta = jax.nn.softplus(ssm_params[..., -1:])
        A = -jnp.exp(A_log)

        def step(h, inp):
            xt, Bt, Ct, dt = inp
            dA = jnp.exp(dt[:, :, None] * A[None])
            h = dA * h + dt[:, :, None] * Bt[:, None, :] * xt[:, :, None]
            y = jnp.einsum('bdn,bn->bd', h, Ct)
            return (h, y)
        h0 = jnp.zeros((x.shape[0], x.shape[2], d_state), x.dtype)
        xs = (jnp.swapaxes(x_conv, 0, 1), jnp.swapaxes(Bm, 0, 1), jnp.swapaxes(Cm, 0, 1), jnp.swapaxes(delta, 0, 1))
        _, ys = jax.lax.scan(step, h0, xs)
        y = jnp.swapaxes(ys, 0, 1)
        y = y + D_param * x_conv
        y = y * _silu(z)
        return jnp.einsum('bld,ed->ble', y, out_proj_w)

    def _L1_ffn_ref(x, router_w, router_bias, gate_w, up_w, down_w, sgate_w, sup_w, sdown_w):
        import jax, jax.numpy as jnp
        import numpy as np
        TOPK = 4
        B, T, D = x.shape
        flat = x.reshape(B * T, D)
        logits = flat.astype(jnp.float32) @ router_w.T + router_bias
        scores = jax.nn.softmax(logits, axis=-1)
        topk_scores, topk_idx = jax.lax.top_k(scores, TOPK)
        topk_scores = topk_scores / jnp.clip(topk_scores.sum(axis=-1, keepdims=True), 1e-12, None)
        h = jax.nn.silu(jnp.einsum('nd,ehd->neh', flat, gate_w)) * jnp.einsum('nd,ehd->neh', flat, up_w)
        expert_out = jnp.einsum('neh,edh->ned', h, down_w)
        sel = jnp.take_along_axis(expert_out, topk_idx[:, :, None], axis=1)
        out = (sel * topk_scores.astype(flat.dtype)[:, :, None]).sum(axis=1)
        out = out + jax.nn.silu(flat @ sgate_w.T) * (flat @ sup_w.T) @ sdown_w.T
        return out.reshape(B, T, D)
    x = x + _L0_xattn_ref(ctx_1024, ctx_1024, _layernorm(x, axis=-1), mask_BxS2_if0, L0_xattn_Wk, L0_xattn_bk, L0_xattn_Wv, L0_xattn_bv, L0_xattn_Wq, L0_xattn_bq, L0_xattn_Woff, L0_xattn_boff, L0_xattn_Wo, L0_xattn_bo)
    x = x + _L0_attn_ref(_layernorm(x, axis=-1), L0_attn_Wq, L0_attn_bq, L0_attn_Wk, L0_attn_bk, L0_attn_Wv, L0_attn_bv, L0_attn_Wo, L0_attn_bo, L0_attn_layerscale)
    x = x + _L0_ffn_ref(_layernorm(x, axis=-1), L0_ffn_router_scale, L0_ffn_router_w, L0_ffn_gating_w, L0_ffn_linear_w, L0_ffn_per_expert_scale)
    x = x + _L1_xattn_ref(_layernorm(x, axis=-1), ctx_1024, L1_xattn_Wq, L1_xattn_Wk, L1_xattn_Wv, L1_xattn_Wk_ip, L1_xattn_Wv_ip, L1_xattn_Wo, L1_xattn_bo)
    x = x + _L1_attn_ref(_layernorm(x, axis=-1), L1_attn_in_proj_w, L1_attn_conv_w, L1_attn_conv_b, L1_attn_x_proj_w, L1_attn_A_log, L1_attn_D_param, L1_attn_out_proj_w)
    x = x + _L1_ffn_ref(_layernorm(x, axis=-1), L1_ffn_router_w, L1_ffn_router_bias, L1_ffn_gate_w, L1_ffn_up_w, L1_ffn_down_w, L1_ffn_sgate_w, L1_ffn_sup_w, L1_ffn_sdown_w)
    return x

_drawn_inputs = setup_inputs


def setup_inputs(seed=0):
    import zlib

    import numpy as np

    out = dict(_drawn_inputs(seed))
    spreads = {'L0_xattn_bk': (0.0, 2.0),
     'L0_xattn_bv': (0.0, 0.304),
     'L0_xattn_bq': (0.0, 0.8),
     'L0_xattn_boff': (0.0, 0.8),
     'L0_xattn_bo': (0.0, 0.1),
     'L0_attn_bq': (0.0, 2.0),
     'L0_attn_bk': (0.0, 2.0),
     'L0_attn_bv': (0.0, 2.0),
     'L0_attn_bo': (0.0, 2.0),
     'L0_attn_layerscale': (9.999999747378752e-05, 0.6),
     'L0_ffn_router_scale': (1.0, 0.6),
     'L0_ffn_per_expert_scale': (1.0, 0.6),
     'L1_xattn_bo': (0.0, 0.1),
     'L1_attn_D_param': (1.0, 0.6),
     'L1_ffn_router_bias': (0.0, 0.8)}
    factors = {'L0_xattn_Wk': 8.0,
     'L0_xattn_Wq': 7.206,
     'L0_xattn_Woff': 6.481,
     'L0_attn_Wq': 64.0,
     'L0_attn_Wk': 64.0,
     'L0_attn_Wv': 64.0,
     'L0_attn_Wo': 64.0,
     'L1_attn_in_proj_w': 8.0,
     'L1_attn_conv_w': 8.0,
     'L1_attn_conv_b': 8.0,
     'L1_attn_x_proj_w': 8.0,
     'L1_attn_A_log': 8.0,
     'L1_attn_out_proj_w': 8.0,
     'L1_ffn_router_w': 8.0,
     'L1_ffn_gate_w': 8.0,
     'L1_ffn_up_w': 8.0,
     'L1_ffn_down_w': 8.0,
     'L1_ffn_sgate_w': 6.035,
     'L1_ffn_sup_w': 5.638,
     'L1_ffn_sdown_w': 5.651}
    for name, (base, spread) in spreads.items():
        noise = np.random.default_rng([zlib.crc32(name.encode()), seed]).standard_normal(out[name].shape)
        drawn = base * np.exp(spread * noise) if base else spread * noise
        out[name] = jnp.asarray(drawn.astype(out[name].dtype))
    for name, factor in factors.items():
        out[name] = (out[name] * factor).astype(out[name].dtype)
    return out
```

```python
import math
from contextlib import ExitStack

import concourse.bass as bass
from concourse import mybir

ALU = mybir.AluOpType
ACT = mybir.ActivationFunctionType
F32 = mybir.dt.float32
I32 = mybir.dt.int32
AX = mybir.AxisListType.X
BANK = 512

P = 128
D = 256
C = D // P
NB, S = 16, 64
T = NB * S
NT = T // P
M = 1601
EPS = 1e-5

H0, HD0, NK = 16, 16, 5
PAIRS0 = H0 // 2
PK = PAIRS0 * NK
LOW, HIGH = 96, 1569
WN = LOW + M - HIGH
NWIN = 13
MPAD = NWIN * WN
assert WN == P

E0, HID = 8, 512
HC = HID // P

H1, HD1, TXT = 16, 64, 77
PAIRS1 = H1 // 2
INNER = H1 * HD1
IMG = M - TXT
IB, IBLK = 12, 127
SB, SBLK = 3, 508
assert IB * IBLK == IMG and SB * SBLK == IMG
NBLK = IB + 1

NS, KC = 16, 4
NPAR = 2 * NS + 1

E1, TOP1 = 32, 4
GROUPS = E1 // HC

SMALL = {}
_at = 0
for _name, _n in (
    ("ident", P), ("mask8", 8), ("mask2", 2), ("same", P), ("iota", WN), ("iota_all", NWIN * WN), ("ref", PK), ("loc", 1),
    ("boff", PK), ("bq", C), ("bk", C), ("ls", D), ("rscale", C), ("pes", E0), ("rw0", C * E0),
    ("convw", C * KC), ("convb", C), ("alog", C * NS), ("dpar", C), ("rw1", C * E1), ("rb1", E1),
):
    SMALL[_name] = (_at, _n)
    _at += _n
SMALL_N = _at
ROWS = {n: i for i, n in enumerate(("bv0", "bo0", "bqa", "bka", "bva", "boa", "bo1"))}


class Chip:
    pass


def broadcast(ap, dim, n):
    return ap.unsqueeze(dim).broadcast(dim, n)


def small(k, name):
    a, n = SMALL[name]
    return k.small[:, a:a + n]


def clear_semaphores(nc, eng):
    ended = sorted(nc.released_uncleared_semaphores)
    first = 0
    for j in range(1, len(ended) + 1):
        if j == len(ended) or ended[j] != ended[j - 1] + 1:
            eng.sem_clear(range(ended[first], ended[j - 1] + 1))
            first = j


def norm_stage(nc, k, tag, clear=False):
    with ExitStack() as ctx:
        stats = ctx.enter_context(nc.sbuf_tensor(f"stats_{tag}", [P, NT, 6], F32))
        moments = ctx.enter_context(nc.sbuf_tensor(f"moments_{tag}", [P, NT, 2], F32))
        var_eps = ctx.enter_context(nc.sbuf_tensor(f"var_eps_{tag}", [P, NT], F32))
        rstd = ctx.enter_context(nc.sbuf_tensor(f"rstd_{tag}", [P, NT], F32))
        xn = ctx.enter_context(nc.sbuf_tensor(f"xn_{tag}", [P, NT, D], F32))
        turned = ctx.enter_context(nc.psum_tensor(f"turned_{tag}", [P, NT, BANK], F32))
        stats_done = ctx.enter_context(nc.semaphore(f"stats_done_{tag}"))
        moments_done = ctx.enter_context(nc.semaphore(f"moments_done_{tag}"))
        eps_added = ctx.enter_context(nc.semaphore(f"eps_added_{tag}"))
        rstd_done = ctx.enter_context(nc.semaphore(f"rstd_done_{tag}"))
        normed = ctx.enter_context(nc.semaphore(f"normed_{tag}"))
        tile_turned = ctx.enter_context(nc.semaphore(f"tile_turned_{tag}"))
        block = ctx.enter_context(nc.Block())

        if clear:
            @block.sync
            def _(sp):
                clear_semaphores(nc, sp)

        @block.vector
        def _(dve):
            for t in range(NT):
                nc.vector.bn_stats(stats[:, t, :], k.x[:, t, :]).then_inc(stats_done, 1)
            for t in range(NT):
                dve.wait_ge(stats_done, t + 1)
                nc.vector.bn_aggr(moments[:, t, :], stats[:, t, :]).then_inc(moments_done, 1)
            dve.wait_ge(moments_done, NT)
            nc.vector.tensor_scalar(var_eps[:], moments[:, :, 1], EPS, None, ALU.add).then_inc(eps_added, 1)
            dve.wait_ge(rstd_done, 1)
            for t in range(NT):
                nc.vector.tensor_scalar(xn[:, t, :], k.x[:, t, :], moments[:, t, 0:1], rstd[:, t:t + 1],
                                        ALU.subtract, ALU.mult).then_inc(normed, 1)

        @block.gpsimd
        def _(pool):
            pool.wait_ge(eps_added, 1)
            nc.gpsimd.tensor_tensor(rstd[:], var_eps[:], k.minus_half[:, 0:1].broadcast_to([P, NT]),
                                    ALU.pow).then_inc(rstd_done, 1)

        @block.tensor
        def _(pe):
            for t in range(NT):
                pe.wait_ge(normed, t + 1)
                for c in range(C):
                    last = nc.tensor.transpose(turned[:, t, c * P:(c + 1) * P], xn[:, t, c * P:(c + 1) * P], k.ident)
                last.then_inc(tile_turned, 1)

        @block.scalar
        def _(act):
            for t in range(NT):
                act.wait_ge(tile_turned, t + 1)
                nc.scalar.activation(k.h_t[:, :, t * P:(t + 1) * P],
                                     turned[:, t, 0:D].rearrange("p (c n) -> p c n", c=C), ACT.Copy)


def load_stage(nc, k, src):
    with ExitStack() as ctx:
        mask_i = ctx.enter_context(nc.sbuf_tensor("mask_i", [NB, M], I32))
        unmasked = ctx.enter_context(nc.sbuf_tensor("unmasked", [NB, M], F32))
        count = ctx.enter_context(nc.sbuf_tensor("count", [NB, 1], F32))
        last_pos = ctx.enter_context(nc.sbuf_tensor("last_pos", [NB, 1], F32))
        diag = ctx.enter_context(nc.sbuf_tensor("diag", [NB, NB], F32))
        spread = ctx.enter_context(nc.psum_tensor("spread", [P, NB], F32))
        mask_in = ctx.enter_context(nc.semaphore("mask_in"))
        small_in = ctx.enter_context(nc.semaphore("small_in"))
        rest_in = ctx.enter_context(nc.semaphore("rest_in"))
        consts_set = ctx.enter_context(nc.semaphore("consts_set"))
        len_step = ctx.enter_context(nc.semaphore("len_step"))
        len_spread = ctx.enter_context(nc.semaphore("len_spread"))
        block = ctx.enter_context(nc.Block())

        @block.sync
        def _(sp):
            sp.dma_start(mask_i[:], src["mask"]).then_inc(mask_in, 16)
            sp.dma_start(k.small[:], src["small"]).then_inc(small_in, 16)
            sp.dma_start(k.x[:], src["x"].rearrange("(t p) d -> p t d", p=P)).then_inc(rest_in, 16)
            sp.dma_start(k.rows[:], src["rows"]).then_inc(rest_in, 16)
            sp.wait_ge(rest_in, 32)

        @block.vector
        def _(dve):
            nc.vector.memset(k.minus_half[:], -0.5)
            nc.vector.memset(k.ones[:], 1.0).then_inc(consts_set, 1)
            nc.vector.memset(k.log_s[:], -math.log(S))
            dve.wait_ge(mask_in, 16)
            nc.vector.tensor_scalar(unmasked[:], mask_i[:], -1.0, 1.0, ALU.mult, ALU.add).then_inc(len_step, 1)
            dve.wait_ge(len_step, 1)
            nc.vector.tensor_reduce(count[:], unmasked[:], AX, ALU.add).then_inc(len_step, 1)
            dve.wait_ge(len_step, 2)
            nc.vector.tensor_scalar(last_pos[:], count[:], -1.0, None, ALU.add).then_inc(len_step, 1)
            dve.wait_ge(len_step, 3)
            dve.wait_ge(small_in, 16)
            nc.vector.tensor_scalar(diag[:], k.ident[0:NB, 0:NB], last_pos[:, 0:1], None,
                                    ALU.mult).then_inc(len_step, 1)
            dve.wait_ge(len_spread, 1)
            nc.vector.tensor_copy(k.length[:], spread[:])

        @block.tensor
        def _(pe):
            pe.wait_ge(len_step, 4)
            pe.wait_ge(consts_set, 1)
            nc.tensor.matmul(spread[:], k.ones[0:NB, :], diag[:], start=True, stop=True).then_inc(len_spread, 1)


def positions_stage(nc, k, src):

    with ExitStack() as ctx:
        def sb(name, shape, dt=F32):
            return ctx.enter_context(nc.sbuf_tensor(name, shape, dt))

        def sem(name):
            return ctx.enter_context(nc.semaphore(name))

        wq = sb("wq0", [P, C, D])
        woff = sb("woff0", [P, C, 2, PK])
        v = sb("where", [P, NB, PK])
        turns = sb("turns", [P, NB, PK])
        side = sb("side", [P, NB, PK])
        per_len = sb("per_len", [P, NB])
        far = sb("far", [P, NB * PK])
        far_any = sb("far_any", [P, 1])
        q_ps = ctx.enter_context(nc.psum_tensor("q_ps", [P, C, 2, 512], F32))
        off_ps = ctx.enter_context(nc.psum_tensor("off_ps", [P, 2, 512], F32))
        flag_ps = ctx.enter_context(nc.psum_tensor("flag_ps", [1, 1], F32))
        wq_in = sem("wq0_in")
        woff_in = sem("woff0_in")
        q_done = sem("q0_done")
        q_kept = sem("q0_kept")
        off_done = sem("off_done")
        step = sem("where_step")
        side_done = sem("row_step")
        flag_summed = sem("flag_summed")
        block = ctx.enter_context(nc.Block())

        @block.sync
        def _(sp):
            sp.dma_start(wq[:], src["wq0"]).then_inc(wq_in, 16)
            sp.dma_start(woff[:], src["woff0"]).then_inc(woff_in, 16)

        @block.tensor
        def _(pe):
            pe.wait_ge(wq_in, 16)
            for e in range(C):
                for g in range(2):
                    for c in range(C):
                        last = nc.tensor.matmul(q_ps[:, e, g, :], wq[:, c, e * P:(e + 1) * P],
                                                k.h_t[:, c, g * 512:(g + 1) * 512], start=c == 0, stop=c == C - 1)
                    last.then_inc(q_done, 1)
            pe.wait_ge(woff_in, 16)
            pe.wait_ge(q_kept, 4)
            for b in range(NB):
                for r in range(2):
                    for c in range(C):
                        last = nc.tensor.matmul(
                            off_ps[r * S:(r + 1) * S, b // 8, (b % 8) * PK:(b % 8 + 1) * PK],
                            k.q0[:, c, b * S:(b + 1) * S], woff[:, c, r, :], start=c == 0, stop=c == C - 1)
            last.then_inc(off_done, 1)
            pe.wait_ge(step, 13)
            nc.tensor.matmul(flag_ps[:], far_any[:], k.ones[:, 0:1], start=True, stop=True).then_inc(flag_summed, 1)

        @block.scalar
        def _(act):
            for e in range(C):
                for g in range(2):
                    act.wait_ge(q_done, 2 * e + g + 1)
                    nc.scalar.activation(k.q0[:, e, g * 512:(g + 1) * 512], q_ps[:, e, g, :], ACT.Identity,
                                         bias=small(k, "bq")[:, e:e + 1]).then_inc(q_kept, 1)

        @block.vector
        def _(dve):
            def rep(ap):
                return ap.unsqueeze(1).broadcast_to([P, NB, PK])

            def by_batch(ap):
                return ap.unsqueeze(2).broadcast_to([P, NB, PK])

            length = by_batch(k.length[:])
            nc.vector.memset(k.pos[:, NB:NB + 1, :], 0.0)
            nc.vector.reciprocal(per_len[:], k.length[:])
            dve.wait_ge(off_done, 1)
            nc.vector.tensor_tensor(v[:].rearrange("p (a b) n -> p a b n", a=2),
                                    off_ps[:, :, 0:8 * PK].rearrange("p a (b n) -> p a b n", n=PK),
                                    rep(small(k, "boff")).rearrange("p (a b) n -> p a b n", a=2),
                                    ALU.add).then_inc(step, 1)
            dve.wait_ge(step, 1)
            nc.vector.tensor_tensor(v[:], v[:], rep(small(k, "ref")), ALU.add).then_inc(step, 1)
            dve.wait_ge(step, 2)
            nc.vector.tensor_scalar(v[:], v[:], small(k, "loc"), None, ALU.add).then_inc(step, 1)
            dve.wait_ge(step, 3)
            nc.vector.tensor_tensor(turns[:], v[:], by_batch(per_len[:]), ALU.mult).then_inc(step, 1)
            dve.wait_ge(step, 4)
            big = 1.5 * 2.0 ** 23
            nc.vector.tensor_scalar(turns[:], turns[:], big, big, ALU.add, ALU.subtract).then_inc(step, 1)
            dve.wait_ge(step, 5)
            nc.vector.tensor_tensor(turns[:], turns[:], length, ALU.mult).then_inc(step, 1)
            dve.wait_ge(step, 6)
            nc.vector.tensor_tensor(v[:], v[:], turns[:], ALU.subtract).then_inc(step, 1)
            dve.wait_ge(step, 7)
            nc.vector.tensor_tensor(side[:], v[:], length, ALU.mult).then_inc(step, 1)
            dve.wait_ge(step, 8)
            nc.vector.scalar_tensor_tensor(out=side[:], in0=side[:], scalar=0.0, in1=length, op0=ALU.is_lt,
                                           op1=ALU.mult).then_inc(step, 1)
            dve.wait_ge(step, 9)
            nc.vector.tensor_tensor(v[:], v[:], side[:], ALU.add).then_inc(step, 1)
            dve.wait_ge(step, 10)
            nc.vector.tensor_scalar(v[:], v[:], 1.0 / (M - 1), 2.0, ALU.mult, ALU.mult).then_inc(step, 1)
            dve.wait_ge(step, 11)
            nc.vector.tensor_scalar(v[:], v[:], 1.0, 1.0, ALU.subtract, ALU.add).then_inc(step, 1)
            dve.wait_ge(step, 12)
            nc.vector.tensor_scalar(v[:], v[:], float(M), -1.0, ALU.mult, ALU.add).then_inc(side_done, 1)
            dve.wait_ge(side_done, 1)
            nc.vector.tensor_scalar(k.pos[:, 0:NB, :], v[:], 0.5, None, ALU.mult).then_inc(side_done, 1)
            dve.wait_ge(side_done, 2)
            flat = k.pos[:, 0:NB, :].rearrange("p b n -> p (b n)")
            nc.vector.tensor_scalar(far[:], flat, float(LOW - 1), None, ALU.is_gt).then_inc(side_done, 1)
            dve.wait_ge(side_done, 3)
            nc.vector.scalar_tensor_tensor(out=far[:], in0=flat, scalar=float(HIGH), in1=far[:], op0=ALU.is_lt,
                                           op1=ALU.mult).then_inc(side_done, 1)
            dve.wait_ge(side_done, 4)
            nc.vector.tensor_reduce(far_any[:], far[:], AX, ALU.add).then_inc(step, 1)
            dve.wait_ge(flag_summed, 1)
            nc.vector.tensor_copy(k.far_count[:], flag_ps[:])




def near_attention(nc, k, src, ctx):
    def sb(name, shape, dt=F32):
        return ctx.enter_context(nc.sbuf_tensor(name, shape, dt))

    def ps(name, shape):
        return ctx.enter_context(nc.psum_tensor(name, shape, F32))

    def sem(name):
        return ctx.enter_context(nc.semaphore(name))

    wk, wv = sb("wk0", [P, C, D]), sb("wv0", [P, C, D])
    win = [sb(f"win{s}", [P, C, WN]) for s in range(2)]
    kt = [sb(f"kt{s}", [P, C, WN]) for s in range(2)]
    vals = [sb(f"vals{s}", [P, D]) for s in range(2)]
    qblk = [sb(f"qblk{s}", [P, C, 8, S]) for s in range(2)]
    tent = [sb(f"tent{s}", [P, PK, WN]) for s in range(2)]
    hit = sb("hit", [P, PK, WN])
    share = sb("share", [P, PK, WN])
    turned = sb("turned0", [P, 2, 512])
    score = sb("score", [P, PK])
    top = sb("top0", [P, PAIRS0])
    shifted = sb("shifted", [P, PK])
    weight = sb("weight", [P, PK])
    total = sb("total0", [P, PAIRS0])
    inv = sb("inv0", [P, PAIRS0])
    attn = sb("attn0", [P, PK])
    kept = sb("kept", [P, C, 2, S])
    kv_ps = ps("kv_ps", [P, 512])
    s_ps = ps("s_ps", [P, 2, 512])
    w_ps = ps("w_ps", [P, 2, 512])
    o_ps = ps("o_ps", [P, C, P])
    w_in = sem("wkv0_in")
    win_in = [sem(f"win_in{s}") for s in range(2)]
    kv_done, kv_kept, q_masked = sem("kv_done"), sem("kv_kept"), sem("q_masked")
    scored, dist_done, dist_abs, tent_done = sem("scored"), sem("dist_done"), sem("dist_abs"), sem("tent_done")
    hit_done, soft = sem("hit_done"), sem("soft_step")
    shift_done, exp_done = sem("shift_done"), sem("exp_done")
    share_done, turned_done, turned_kept = sem("share_done"), sem("turned_done"), sem("turned_kept")
    out_done, out_masked, out_kept = sem("out_done"), sem("out_masked"), sem("out_kept")
    SOFT = 5
    HALVES = NB // 2
    block = ctx.enter_context(nc.Block())

    def pairs_of_batches(eng, body):
        body(0, True, False)
        with eng.Fori(1, HALVES - 1) as i:
            body(i, False, False)
        body(HALVES - 1, False, True)

    @block.sync
    def _(sp):
        def load(b, s):
            ctx_b = src["ctx_t"][b]
            sp.dma_start(win[s][:, :, 0:LOW], ctx_b[:, :, 0:LOW]).then_inc(win_in[s], 16)
            sp.dma_start(win[s][:, :, LOW:WN], ctx_b[:, :, HIGH:M]).then_inc(win_in[s], 16)

        sp.dma_start(wk[:], src["wk0"]).then_inc(w_in, 16)
        sp.dma_start(wv[:], src["wv0"]).then_inc(w_in, 16)
        load(0, 0)
        load(1, 1)
        with sp.Fori(0, HALVES - 1) as i:
            for s in range(2):
                sp.wait_ge(kv_done, i * 2 + (s + 1))
                load(i * 2 + (s + 2), s)

    @block.tensor
    def _(pe):
        def keys_values(b, s, i):
            pe.wait_ge(win_in[s], i * 32 + 32)
            pe.wait_ge(kv_kept, b)
            for e in range(C):
                for c in range(C):
                    nc.tensor.matmul(kv_ps[:, e * WN:(e + 1) * WN], wk[:, c, e * P:(e + 1) * P], win[s][:, c, :],
                                     start=c == 0, stop=c == C - 1)
            for c in range(C):
                nc.tensor.matmul(kv_ps[:, C * WN:C * WN + D], win[s][:, c, :], wv[:, c, :], start=c == 0, stop=False)
            nc.tensor.matmul(kv_ps[:, C * WN:C * WN + D], k.ones[0:1, :], k.row("bv0"), start=False,
                             stop=True).then_inc(kv_done, 1)

        def scores(b, s):
            pe.wait_ge(kv_kept, b + 1)
            pe.wait_ge(q_masked, b + 1)
            pe.wait_ge(hit_done, b)
            for p in range(PAIRS0):
                c, j = divmod(p, 4)
                last = nc.tensor.matmul(s_ps[:, c, j * WN:(j + 1) * WN],
                                        qblk[s][:, c, 2 * j:2 * j + 2, :].rearrange("p h q -> p (h q)"),
                                        kt[s][:, c, :], start=True, stop=True)
            last.then_inc(scored, 1)

        def turn_shares(b, h, skip_wait):
            pe.wait_ge(share_done, b * 2 + (h + 1))
            if not skip_wait:
                pe.wait_ge(turned_kept, b * 2 + (h - 1))
            for j in range(4):
                for n in range(NK):
                    last = nc.tensor.matmul(w_ps[:, h, j * P:(j + 1) * P], share[:, (4 * h + j) * NK + n, :],
                                            k.ident, start=n == 0, stop=n == NK - 1)
            last.then_inc(turned_done, 1)

        def outputs(b, s):
            pe.wait_ge(out_masked, b)
            for p in range(PAIRS0):
                c, j = divmod(p, 4)
                if j == 0:
                    pe.wait_ge(turned_kept, b * 2 + (c + 1))
                last = nc.tensor.matmul(o_ps[32 * j:32 * j + 32, c, :], vals[s][:, 32 * p:32 * p + 32],
                                        turned[:, c, j * P:(j + 1) * P], start=True, stop=True)
            last.then_inc(out_done, 1)

        pe.wait_ge(w_in, 32)
        keys_values(0, 0, 0)
        scores(0, 0)

        def body(i, first, last):
            for s in range(2):
                b = i * 2 + s
                if not (last and s == 1):
                    keys_values(b + 1, 1 - s, i + s)
                    scores(b + 1, 1 - s)
                for h in range(2):
                    turn_shares(b, h, first and s == 0)
                outputs(b, s)

        pairs_of_batches(pe, body)

    @block.gpsimd
    def _(pool):
        def prepare(b, s, old):
            if old is not None:
                pool.wait_ge(scored, old)
            nc.gpsimd.tensor_tensor(
                qblk[s][:], k.q0[:, :, bass.ds(b * S, S)].unsqueeze(2).broadcast_to([P, C, 8, S]),
                small(k, "mask8").unsqueeze(1).unsqueeze(3).broadcast_to([P, C, 8, S]), ALU.mult).then_inc(q_masked, 1)
            if old is not None:
                pool.wait_ge(share_done, old * 2)
            nc.gpsimd.tensor_tensor(
                tent[s][:], small(k, "iota").unsqueeze(1).broadcast_to([P, PK, WN]),
                k.pos[:, bass.ds(b, 1), :].rearrange("p b n -> p (b n)").unsqueeze(2).broadcast_to([P, PK, WN]),
                ALU.subtract).then_inc(dist_done, 1)

        prepare(0, 0, None)

        def body(i, first, last):
            for s in range(2):
                b = i * 2 + s
                if not (last and s == 1):
                    prepare(b + 1, 1 - s, None if first and s == 0 else b)

        pairs_of_batches(pool, body)

    @block.scalar
    def _(act):
        def make_tent(b, s):
            act.wait_ge(dist_done, b + 1)
            nc.scalar.activation(tent[s][:], tent[s][:], ACT.Abs).then_inc(dist_abs, 1)
            act.wait_ge(dist_abs, b + 1)
            nc.scalar.activation(tent[s][:], tent[s][:], ACT.Relu, bias=1.0, scale=-1.0).then_inc(tent_done, 1)

        def keep_keys_values(b, s):
            act.wait_ge(kv_done, b + 1)
            for c in range(C):
                nc.scalar.activation(kt[s][:, c, :], kv_ps[:, c * WN:(c + 1) * WN], ACT.Identity,
                                     bias=small(k, "bk")[:, c:c + 1])
            nc.scalar.activation(vals[s][:], kv_ps[:, C * WN:C * WN + D], ACT.Copy).then_inc(kv_kept, 1)

        keep_keys_values(0, 0)
        make_tent(0, 0)

        def body(i, first, last):
            for s in range(2):
                b = i * 2 + s
                if not (last and s == 1):
                    keep_keys_values(b + 1, 1 - s)
                    make_tent(b + 1, 1 - s)
                act.wait_ge(shift_done, b + 1)
                nc.scalar.activation(weight[:], shifted[:], ACT.Exp).then_inc(exp_done, 1)
                for h in range(2):
                    act.wait_ge(turned_done, b * 2 + (h + 1))
                    nc.scalar.activation(turned[:, h, :], w_ps[:, h, :], ACT.Copy).then_inc(turned_kept, 1)

        pairs_of_batches(act, body)

    @block.vector
    def _(dve):
        def keep_outputs(b):
            dve.wait_ge(out_done, b + 1)
            nc.vector.tensor_tensor(
                kept[:], o_ps[:].rearrange("p c (r q) -> p c r q", r=2),
                small(k, "mask2").unsqueeze(1).unsqueeze(3).broadcast_to([P, C, 2, S]),
                ALU.mult).then_inc(out_masked, 1)
            dve.wait_ge(out_masked, b + 1)
            nc.vector.tensor_tensor(k.ctx_t[:, :, bass.ds(b * S, S)], kept[:, :, 0, :], kept[:, :, 1, :],
                                    ALU.add).then_inc(out_kept, 1)

        def by_pair(ap):
            return ap.unsqueeze(2).broadcast_to([P, PAIRS0, NK])

        def paired(t):
            return t[:].rearrange("p (a n) -> p a n", n=NK)

        def body(i, first, last):
            for s in range(2):
                b = i * 2 + s
                at = b * SOFT
                dve.wait_ge(tent_done, b + 1)
                dve.wait_ge(scored, b + 1)
                nc.vector.tensor_tensor(
                    hit[:].rearrange("p (a n) m -> p a n m", n=NK), tent[s][:].rearrange("p (a n) m -> p a n m", n=NK),
                    s_ps[:].rearrange("p c (j m) -> p (c j) m", m=WN).unsqueeze(2).broadcast_to([P, PAIRS0, NK, WN]),
                    ALU.mult).then_inc(hit_done, 1)
                dve.wait_ge(hit_done, b + 1)
                nc.vector.tensor_reduce(score[:], hit[:], AX, ALU.add).then_inc(soft, 1)
                if not (first and s == 0):
                    keep_outputs(b - 1)
                dve.wait_ge(soft, at + 1)
                nc.vector.tensor_reduce(top[:], paired(score), AX, ALU.max).then_inc(soft, 1)
                dve.wait_ge(soft, at + 2)
                nc.vector.tensor_tensor(paired(shifted), paired(score), by_pair(top[:]),
                                        ALU.subtract).then_inc(shift_done, 1)
                dve.wait_ge(exp_done, b + 1)
                nc.vector.tensor_reduce(total[:], paired(weight), AX, ALU.add).then_inc(soft, 1)
                dve.wait_ge(soft, at + 3)
                nc.vector.reciprocal(inv[:], total[:]).then_inc(soft, 1)
                dve.wait_ge(soft, at + 4)
                nc.vector.scalar_tensor_tensor(out=paired(attn), in0=paired(weight), scalar=0.5, in1=by_pair(inv[:]),
                                               op0=ALU.mult, op1=ALU.mult).then_inc(soft, 1)
                dve.wait_ge(soft, at + 5)
                for h in range(2):
                    n = PK // 2
                    if not (first and s == 0):
                        dve.wait_ge(turned_done, b * 2 + (h - 1))
                    nc.vector.tensor_tensor(share[:, h * n:(h + 1) * n, :], tent[s][:, h * n:(h + 1) * n, :],
                                            attn[:, h * n:(h + 1) * n].unsqueeze(2).broadcast_to([P, n, WN]),
                                            ALU.mult).then_inc(share_done, 1)

        pairs_of_batches(dve, body)
        keep_outputs(NB - 1)


def far_attention(nc, k, src):
    with ExitStack() as ctx:
        def sb(name, shape, dt=F32):
            return ctx.enter_context(nc.sbuf_tensor(f"far_{name}", shape, dt))

        def ps(name, shape):
            return ctx.enter_context(nc.psum_tensor(f"far_{name}", shape, F32))

        def sem(name):
            return ctx.enter_context(nc.semaphore(f"far_{name}"))

        wk, wv = sb("wk", [P, C, D]), sb("wv", [P, C, D])
        win, win2 = sb("win", [P, C, WN]), sb("win2", [P, C, WN])
        kt, vals = sb("kt", [P, C, WN]), sb("vals", [P, D])
        qblk = sb("qblk", [P, C, 8, S])
        tent, hit = sb("tent", [P, PK, WN]), sb("hit", [P, PK, WN])
        tent2, share = sb("tent2", [P, PK, WN]), sb("share", [P, PK, WN])
        turned = sb("turned", [P, 2, 512])
        part, score, shifted, weight, attn = (sb(n, [P, PK]) for n in ("part", "score", "shifted", "weight", "attn"))
        top, total, inv = (sb(n, [P, PAIRS0]) for n in ("top", "total", "inv"))
        kept, out_part, out_sum = sb("kept", [P, C, 2, S]), sb("out_part", [P, C, S]), sb("out_sum", [P, C, S])
        k_ps, v_ps, s_ps = ps("k_ps", [P, C, WN]), ps("v_ps", [P, D]), ps("s_ps", [P, 2, BANK])
        w_ps, o_ps = ps("w_ps", [P, 2, BANK]), ps("o_ps", [P, C, P])
        w_in, win_in, win2_in = sem("w_in"), sem("win_in"), sem("win2_in")
        k_done, k_kept, q_masked, scored = sem("k_done"), sem("k_kept"), sem("q_masked"), sem("scored")
        dist, dist_abs, tent_done, hit_done = sem("dist"), sem("dist_abs"), sem("tent_done"), sem("hit_done")
        part_done, score_done, soft, shift, exp_done = (
            sem(n) for n in ("part_done", "score_done", "soft", "shift", "exp_done"))
        attn_done, v_done, v_kept, dist2, dist2_abs, tent2_done = (
            sem(n) for n in ("attn_done", "v_done", "v_kept", "dist2", "dist2_abs", "tent2_done"))
        share_done, turned_done, turned_kept, out_done, masked, out_step, out_added, batch_out = (
            sem(n) for n in ("share_done", "turned_done", "turned_kept", "out_done", "masked", "out_step",
                             "out_added", "batch_out"))
        block = ctx.enter_context(nc.Block())

        def windows(eng, b, body):
            with eng.Fori(0, NWIN) as j:
                body(j, b * NWIN + j)

        @block.sync
        def _(sp):
            sp.dma_start(wk[:], src["wk0"]).then_inc(w_in, 16)
            sp.dma_start(wv[:], src["wv0"]).then_inc(w_in, 16)
            with sp.Fori(0, NB) as b:
                def for_keys(j, n):
                    sp.wait_ge(k_done, n + 1)
                    sp.dma_start(win[:], src["ctx_t"][b][:, :, bass.ds(j * WN, WN)]).then_inc(win_in, 16)

                def for_values(j, n):
                    sp.wait_ge(v_done, n + 1)
                    sp.dma_start(win2[:], src["ctx_t"][b][:, :, bass.ds(j * WN, WN)]).then_inc(win2_in, 16)

                windows(sp, b, for_keys)
                windows(sp, b, for_values)

        @block.tensor
        def _(pe):
            for first in (k_done, scored, v_done, turned_done, out_done):
                pe.sem_inc(first, 1)
            pe.wait_ge(w_in, 32)
            with pe.Fori(0, NB) as b:
                def scores(j, n):
                    pe.wait_ge(win_in, n * 16 + 16)
                    for e in range(C):
                        for c in range(C):
                            last = nc.tensor.matmul(k_ps[:, e, :], wk[:, c, e * P:(e + 1) * P], win[:, c, :],
                                                    start=c == 0, stop=c == C - 1)
                    last.then_inc(k_done, 1)
                    pe.wait_ge(k_kept, n + 1)
                    pe.wait_ge(q_masked, b + 1)
                    pe.wait_ge(hit_done, n + 1)
                    for p in range(PAIRS0):
                        c, i = divmod(p, 4)
                        last = nc.tensor.matmul(s_ps[:, c, i * WN:(i + 1) * WN],
                                                qblk[:, c, 2 * i:2 * i + 2, :].rearrange("p h q -> p (h q)"),
                                                kt[:, c, :], start=True, stop=True)
                    last.then_inc(scored, 1)

                def outputs(j, n):
                    pe.wait_ge(win2_in, n * 16 + 16)
                    for c in range(C):
                        nc.tensor.matmul(v_ps[:], win2[:, c, :], wv[:, c, :], start=c == 0, stop=False)
                    nc.tensor.matmul(v_ps[:], k.ones[0:1, :], k.row("bv0"), start=False, stop=True).then_inc(v_done, 1)
                    pe.wait_ge(share_done, n + 2)
                    for p in range(PAIRS0):
                        for i in range(NK):
                            last = nc.tensor.matmul(w_ps[:, p // 4, (p % 4) * P:(p % 4 + 1) * P],
                                                    share[:, p * NK + i, :], k.ident, start=i == 0, stop=i == NK - 1)
                    last.then_inc(turned_done, 1)
                    pe.wait_ge(v_kept, n + 1)
                    pe.wait_ge(turned_kept, n + 1)
                    pe.wait_ge(masked, n + 1)
                    for p in range(PAIRS0):
                        c, i = divmod(p, 4)
                        last = nc.tensor.matmul(o_ps[32 * i:32 * i + 32, c, :], vals[:, 32 * p:32 * p + 32],
                                                turned[:, c, i * P:(i + 1) * P], start=True, stop=True)
                    last.then_inc(out_done, 1)

                windows(pe, b, scores)
                windows(pe, b, outputs)

        @block.gpsimd
        def _(pool):
            with pool.Fori(0, NB) as b:
                def distances(out, j, done):
                    nc.gpsimd.tensor_tensor(
                        out[:], small(k, "iota_all")[:, bass.ds(j * WN, WN)].unsqueeze(1).broadcast_to([P, PK, WN]),
                        k.pos[:, bass.ds(b, 1), :].rearrange("p b n -> p (b n)").unsqueeze(2).broadcast_to([P, PK, WN]),
                        ALU.subtract).then_inc(done, 1)

                def for_scores(j, n):
                    pool.wait_ge(hit_done, n + 1)
                    distances(tent, j, dist)

                def for_outputs(j, n):
                    pool.wait_ge(share_done, n + 1)
                    distances(tent2, j, dist2)

                pool.wait_ge(scored, b * NWIN + 1)
                nc.gpsimd.tensor_tensor(
                    qblk[:], k.q0[:, :, bass.ds(b * S, S)].unsqueeze(2).broadcast_to([P, C, 8, S]),
                    small(k, "mask8").unsqueeze(1).unsqueeze(3).broadcast_to([P, C, 8, S]),
                    ALU.mult).then_inc(q_masked, 1)
                windows(pool, b, for_scores)
                windows(pool, b, for_outputs)

        @block.scalar
        def _(act):
            with act.Fori(0, NB) as b:
                def for_scores(j, n):
                    act.wait_ge(k_done, n + 2)
                    for c in range(C):
                        last = nc.scalar.activation(kt[:, c, :], k_ps[:, c, :], ACT.Identity,
                                                    bias=small(k, "bk")[:, c:c + 1])
                    last.then_inc(k_kept, 1)
                    act.wait_ge(dist, n + 1)
                    nc.scalar.activation(tent[:], tent[:], ACT.Abs).then_inc(dist_abs, 1)
                    act.wait_ge(dist_abs, n + 1)
                    nc.scalar.activation(tent[:], tent[:], ACT.Relu, bias=1.0, scale=-1.0).then_inc(tent_done, 1)

                def for_outputs(j, n):
                    act.wait_ge(v_done, n + 2)
                    act.wait_ge(out_done, n + 1)
                    nc.scalar.activation(vals[:], v_ps[:], ACT.Copy).then_inc(v_kept, 1)
                    act.wait_ge(dist2, n + 1)
                    nc.scalar.activation(tent2[:], tent2[:], ACT.Abs).then_inc(dist2_abs, 1)
                    act.wait_ge(dist2_abs, n + 1)
                    nc.scalar.activation(tent2[:], tent2[:], ACT.Relu, bias=1.0, scale=-1.0).then_inc(tent2_done, 1)
                    act.wait_ge(turned_done, n + 2)
                    nc.scalar.activation(turned[:], w_ps[:], ACT.Copy).then_inc(turned_kept, 1)

                windows(act, b, for_scores)
                act.wait_ge(shift, b + 1)
                nc.scalar.activation(weight[:], shifted[:], ACT.Exp).then_inc(exp_done, 1)
                windows(act, b, for_outputs)

        @block.vector
        def _(dve):
            def paired(t):
                return t[:].rearrange("p (a n) -> p a n", n=NK)

            def by_pair(t):
                return t[:].unsqueeze(2).broadcast_to([P, PAIRS0, NK])

            for first in (hit_done, part_done, share_done, masked):
                dve.sem_inc(first, 1)
            nc.vector.memset(score[:], 0.0).then_inc(score_done, 1)
            nc.vector.memset(out_sum[:], 0.0).then_inc(out_added, 1)
            with dve.Fori(0, NB) as b:
                def scores(j, n):
                    dve.wait_ge(tent_done, n + 1)
                    dve.wait_ge(scored, n + 2)
                    dve.wait_ge(part_done, n + 1)
                    nc.vector.tensor_tensor(
                        hit[:].rearrange("p (a n) m -> p a n m", n=NK), tent[:].rearrange("p (a n) m -> p a n m", n=NK),
                        s_ps[:].rearrange("p c (i m) -> p (c i) m", m=WN).unsqueeze(2).broadcast_to(
                            [P, PAIRS0, NK, WN]), ALU.mult).then_inc(hit_done, 1)
                    dve.wait_ge(hit_done, n + 2)
                    nc.vector.tensor_reduce(part[:], hit[:], AX, ALU.add).then_inc(part_done, 1)
                    dve.wait_ge(part_done, n + 2)
                    dve.wait_ge(score_done, n + (b + 1))
                    nc.vector.tensor_tensor(score[:], score[:], part[:], ALU.add).then_inc(score_done, 1)

                def outputs(j, n):
                    dve.wait_ge(soft, b * 5 + 4)
                    dve.wait_ge(tent2_done, n + 1)
                    dve.wait_ge(turned_done, n + 1)
                    nc.vector.tensor_tensor(share[:], tent2[:], attn[:].unsqueeze(2).broadcast_to([P, PK, WN]),
                                            ALU.mult).then_inc(share_done, 1)
                    dve.wait_ge(out_done, n + 2)
                    nc.vector.tensor_tensor(
                        kept[:], o_ps[:].rearrange("p c (r q) -> p c r q", r=2),
                        small(k, "mask2").unsqueeze(1).unsqueeze(3).broadcast_to([P, C, 2, S]),
                        ALU.mult).then_inc(masked, 1)
                    dve.wait_ge(masked, n + 2)
                    nc.vector.tensor_tensor(out_part[:], kept[:, :, 0, :], kept[:, :, 1, :],
                                            ALU.add).then_inc(out_step, 1)
                    dve.wait_ge(out_step, n + 1)
                    dve.wait_ge(out_added, n + (b + 1))
                    nc.vector.tensor_tensor(out_sum[:], out_sum[:], out_part[:], ALU.add).then_inc(out_added, 1)

                windows(dve, b, scores)
                at = b * 5
                dve.wait_ge(score_done, b * (NWIN + 1) + (NWIN + 1))
                nc.vector.tensor_reduce(top[:], paired(score), AX, ALU.max).then_inc(soft, 1)
                dve.wait_ge(soft, at + 1)
                nc.vector.tensor_tensor(paired(shifted), paired(score), by_pair(top), ALU.subtract).then_inc(shift, 1)
                dve.wait_ge(shift, b + 1)
                nc.vector.memset(score[:], 0.0).then_inc(score_done, 1)
                dve.wait_ge(exp_done, b + 1)
                nc.vector.tensor_reduce(total[:], paired(weight), AX, ALU.add).then_inc(soft, 1)
                dve.wait_ge(soft, at + 2)
                nc.vector.reciprocal(inv[:], total[:]).then_inc(soft, 1)
                dve.wait_ge(soft, at + 3)
                nc.vector.scalar_tensor_tensor(out=paired(attn), in0=paired(weight), scalar=0.5, in1=by_pair(inv),
                                               op0=ALU.mult, op1=ALU.mult).then_inc(soft, 1)
                windows(dve, b, outputs)
                dve.wait_ge(out_added, b * (NWIN + 1) + (NWIN + 1))
                nc.vector.tensor_copy(k.ctx_t[:, :, bass.ds(b * S, S)], out_sum[:]).then_inc(soft, 1)
                dve.wait_ge(soft, at + 5)
                nc.vector.memset(out_sum[:], 0.0).then_inc(out_added, 1)


def local_attention(nc, k, src):
    far = nc.values_load(k.far_count[0:1, 0:1], min_val=0, max_val=1 << 23)
    with nc.If(far < 1):
        with ExitStack() as ctx:
            near_attention(nc, k, src, ctx)
    with nc.Else():
        far_attention(nc, k, src)


def after_local(nc, k, src):
    with ExitStack() as ctx:
        wo = ctx.enter_context(nc.sbuf_tensor("wo0", [P, C, D], F32))
        y_ps = ctx.enter_context(nc.psum_tensor("y0_ps", [P, NT, BANK], F32))
        wo_in = ctx.enter_context(nc.semaphore("wo0_in"))
        y_done = ctx.enter_context(nc.semaphore("y0_done"))
        block = ctx.enter_context(nc.Block())

        @block.sync
        def _(sp):
            sp.dma_start(wo[:], src["wo0"]).then_inc(wo_in, 16)

        @block.tensor
        def _(pe):
            pe.wait_ge(wo_in, 16)
            for t in range(NT):
                for c in range(C):
                    nc.tensor.matmul(y_ps[:, t, 0:D], k.ctx_t[:, c, t * P:(t + 1) * P], wo[:, c, :],
                                     start=c == 0, stop=False)
                nc.tensor.matmul(y_ps[:, t, 0:D], k.ones[0:1, :], k.row("bo0"), start=False,
                                 stop=True).then_inc(y_done, 1)

        @block.vector
        def _(dve):
            for t in range(NT):
                dve.wait_ge(y_done, t + 1)
                nc.vector.tensor_tensor(k.x[:, t, :], k.x[:, t, :], y_ps[:, t, 0:D], ALU.add)


def store_stage(nc, k, out):
    with ExitStack() as ctx:
        stored = ctx.enter_context(nc.semaphore("stored"))
        block = ctx.enter_context(nc.Block())

        @block.sync
        def _(sp):
            sp.dma_start(out.rearrange("(t p) d -> p t d", p=P), k.x[:]).then_inc(stored, 16)
            sp.wait_ge(stored, 16)


def self_attention(nc, k, src):
    with ExitStack() as ctx:
        def sb(name, shape, dt=F32):
            return ctx.enter_context(nc.sbuf_tensor(name, shape, dt))

        def bank(name):
            return [ctx.enter_context(nc.psum_tensor(f"{name}{s}", [P, BANK], F32)) for s in range(2)]

        def sem(name):
            return ctx.enter_context(nc.semaphore(name))

        w = {n: sb(f"{n}a_w", [P, C, D]) for n in ("q", "k", "v", "o")}
        h = [sb(f"ha{s}", [P, C, P]) for s in range(2)]
        stats = [sb(f"stats_qk{s}", [P, 2, 6]) for s in range(2)]
        moments = [sb(f"moments_qk{s}", [P, 2, 2]) for s in range(2)]
        var_eps = [sb(f"var_eps_qk{s}", [P, 2]) for s in range(2)]
        rstd = [sb(f"rstd_qk{s}", [P, 2]) for s in range(2)]
        qkn = [sb(f"qkn{s}", [P, 2, D]) for s in range(2)]
        qkt = [sb(f"qkt{s}", [P, 2, C, P]) for s in range(2)]
        v = [sb(f"va{s}", [P, D]) for s in range(2)]
        attn = [sb(f"attn_a{s}", [P, P]) for s in range(2)]
        own = [sb(f"own{s}", [P, P]) for s in range(2)]
        ot = [sb(f"ot_a{s}", [P, C, P]) for s in range(2)]
        scaled = [sb(f"scaled{s}", [P, D]) for s in range(2)]
        spare = sb("spare", [P, 1])
        qk_ps, vy_ps, t_ps, s_ps = bank("qk_ps"), bank("vy_ps"), bank("t_ps"), bank("sa_ps")
        w_in = sem("wa_in")
        h_copied, qk_done, v_done = sem("h_copied"), sem("qk_done"), sem("va_done")
        stat, aggr, eps_added, rstd_done, normed = (sem(f"{n}_qk") for n in ("stat", "aggr", "eps", "rstd", "normed"))
        v_kept, qk_turned, qk_kept, scored = sem("va_kept"), sem("qk_turned"), sem("qk_kept"), sem("a_scored")
        gated, masked, o_done, o_kept = sem("a_gated"), sem("a_masked"), sem("a_o_done"), sem("a_o_kept")
        y_done, y_scaled, x_added = sem("a_y_done"), sem("a_y_scaled"), sem("a_x_added")
        block = ctx.enter_context(nc.Block())

        @block.sync
        def _(sp):
            for n, a in (("q", src["wqa"]), ("k", src["wka"]), ("v", src["wva"]), ("o", src["woa"])):
                sp.dma_start(w[n][:], a).then_inc(w_in, 16)

        @block.gpsimd
        def _(pool):
            with pool.Fori(0, NT // 2) as i:
                for s in range(2):
                    pool.wait_ge(x_added, i * 2 + 2)
                    nc.gpsimd.tensor_copy(h[s][:], k.h_t[:, :, bass.ds(i * 2 * P + s * P, P)]).then_inc(h_copied, 1)
                for s in range(2):
                    pool.wait_ge(eps_added, i * 2 + (s + 1))
                    nc.gpsimd.tensor_tensor(rstd[s][:], var_eps[s][:], k.minus_half[:, 0:1].broadcast_to([P, 2]),
                                            ALU.pow).then_inc(rstd_done, 1)

        @block.tensor
        def _(pe):
            pe.wait_ge(w_in, 64)
            with pe.Fori(0, NT // 2) as i:
                for s in range(2):
                    pe.wait_ge(h_copied, i * 2 + (s + 1))
                    for j, n in enumerate("qk"):
                        for c in range(C):
                            nc.tensor.matmul(qk_ps[s][:, j * D:(j + 1) * D], h[s][:, c, :], w[n][:, c, :],
                                             start=c == 0, stop=False)
                        last = nc.tensor.matmul(qk_ps[s][:, j * D:(j + 1) * D], k.ones[0:1, :], k.row(f"b{n}a"),
                                                start=False, stop=True)
                    last.then_inc(qk_done, 1)
                    for c in range(C):
                        nc.tensor.matmul(vy_ps[s][:, 0:D], h[s][:, c, :], w["v"][:, c, :], start=c == 0, stop=False)
                    nc.tensor.matmul(vy_ps[s][:, 0:D], k.ones[0:1, :], k.row("bva"), start=False,
                                     stop=True).then_inc(v_done, 1)
                for s in range(2):
                    pe.wait_ge(normed, i * 2 + (s + 1))
                    for j in range(2):
                        for c in range(C):
                            last = nc.tensor.transpose(t_ps[s][:, (j * C + c) * P:(j * C + c + 1) * P],
                                                       qkn[s][:, j, c * P:(c + 1) * P], k.ident)
                    last.then_inc(qk_turned, 1)
                for s in range(2):
                    pe.wait_ge(qk_kept, i * 2 + (s + 1))
                    for c in range(C):
                        last = nc.tensor.matmul(s_ps[s][:, 0:P], qkt[s][:, 1, c, :], qkt[s][:, 0, c, :],
                                                start=c == 0, stop=c == C - 1)
                    last.then_inc(scored, 1)
                for s in range(2):
                    pe.wait_ge(masked, i * 2 + (s + 1))
                    pe.wait_ge(v_kept, i * 2 + (s + 1))
                    for c in range(C):
                        last = nc.tensor.matmul(t_ps[s][:, c * P:(c + 1) * P], v[s][:, c * P:(c + 1) * P], own[s][:],
                                                start=True, stop=True)
                    last.then_inc(o_done, 1)
                for s in range(2):
                    pe.wait_ge(o_kept, i * 2 + (s + 1))
                    for c in range(C):
                        nc.tensor.matmul(vy_ps[s][:, 0:D], ot[s][:, c, :], w["o"][:, c, :], start=c == 0, stop=False)
                    nc.tensor.matmul(vy_ps[s][:, 0:D], k.ones[0:1, :], k.row("boa"), start=False,
                                     stop=True).then_inc(y_done, 1)

        @block.scalar
        def _(act):
            with act.Fori(0, NT // 2) as i:
                for s in range(2):
                    act.wait_ge(v_done, i * 2 + (s + 1))
                    nc.scalar.activation(v[s][:], vy_ps[s][:, 0:D], ACT.Copy).then_inc(v_kept, 1)
                for s in range(2):
                    act.wait_ge(qk_turned, i * 2 + (s + 1))
                    nc.scalar.activation(qkt[s][:].rearrange("p j c n -> p (j c n)"), t_ps[s][:],
                                         ACT.Copy).then_inc(qk_kept, 1)
                for s in range(2):
                    act.wait_ge(scored, i * 2 + (s + 1))
                    nc.scalar.activation(attn[s][:], s_ps[s][:, 0:P], ACT.Sigmoid, bias=k.log_s[:, 0:1],
                                         scale=1.0 / math.sqrt(D)).then_inc(gated, 1)
                for s in range(2):
                    act.wait_ge(o_done, i * 2 + (s + 1))
                    nc.scalar.activation(ot[s][:].rearrange("p c n -> p (c n)"), t_ps[s][:, 0:D],
                                         ACT.Copy).then_inc(o_kept, 1)

        @block.vector
        def _(dve):
            dve.sem_inc(x_added, 2)
            with dve.Fori(0, NT // 2) as i:
                for s in range(2):
                    dve.wait_ge(qk_done, i * 2 + (s + 1))
                    for j in range(2):
                        nc.vector.bn_stats(stats[s][:, j, :], qk_ps[s][:, j * D:(j + 1) * D]).then_inc(stat, 1)
                dve.wait_ge(stat, i * 4 + 4)
                nc.vector.memset(spare[:], 0.0)
                for s in range(2):
                    for j in range(2):
                        nc.vector.bn_aggr(moments[s][:, j, :], stats[s][:, j, :]).then_inc(aggr, 1)
                for s in range(2):
                    dve.wait_ge(aggr, i * 4 + (2 * s + 2))
                    nc.vector.tensor_scalar(var_eps[s][:], moments[s][:, :, 1], EPS, None,
                                            ALU.add).then_inc(eps_added, 1)
                for s in range(2):
                    dve.wait_ge(rstd_done, i * 2 + (s + 1))
                    for j in range(2):
                        last = nc.vector.tensor_scalar(qkn[s][:, j, :], qk_ps[s][:, j * D:(j + 1) * D],
                                                       moments[s][:, j, 0:1], rstd[s][:, j:j + 1],
                                                       ALU.subtract, ALU.mult)
                    last.then_inc(normed, 1)
                for s in range(2):
                    dve.wait_ge(gated, i * 2 + (s + 1))
                    nc.vector.tensor_tensor(own[s][:], attn[s][:], small(k, "same"), ALU.mult).then_inc(masked, 1)
                for s in range(2):
                    dve.wait_ge(y_done, i * 2 + (s + 1))
                    nc.vector.tensor_tensor(scaled[s][:], vy_ps[s][:, 0:D], small(k, "ls"),
                                            ALU.mult).then_inc(y_scaled, 1)
                for s in range(2):
                    dve.wait_ge(y_scaled, i * 2 + (s + 1))
                    xt = k.x[:, bass.ds(i * 2 + s, 1), :].rearrange("p a d -> p (a d)")
                    nc.vector.tensor_tensor(xt, xt, scaled[s][:], ALU.add).then_inc(x_added, 1)


def route(nc, k, layer):
    n, top_n = (E0, 2) if layer == 0 else (E1, TOP1)
    PAD, MARK = -1e30, 1e30
    with ExitStack() as ctx:
        def sb(name, shape, dt=F32):
            return ctx.enter_context(nc.sbuf_tensor(f"{name}_r{layer}", shape, dt))

        def sem(name):
            return ctx.enter_context(nc.semaphore(f"{name}_r{layer}"))

        square = sb("square", [P, C, T]) if layer == 0 else None
        w = sb("w", [P, C, n])
        mean_sq, rms = sb("mean_sq", [P, NT]), sb("rms", [P, NT])
        logit = sb("logit", [P, NT, n])
        top, total, inv = sb("top", [P, NT]), sb("total", [P, NT]), sb("inv", [P, NT])
        shifted, weight, prob = sb("shifted", [P, NT, n]), sb("weight", [P, NT, n]), sb("prob", [P, NT, n])
        ranked, marked = sb("ranked", [P, NT, n + 8]), sb("marked", [P, NT, n + 8])
        largest = sb("largest", [P, NT, 8])
        chosen, none, kept = sb("chosen", [P, NT, n]), sb("none", [P, NT]), sb("kept", [P, NT, n])
        l_ps = ctx.enter_context(nc.psum_tensor(f"l_ps_r{layer}", [P, NT, 64], F32))
        squared, w_scaled, logits_done = sem("squared"), sem("w_scaled"), sem("logits_done")
        rms_in, rms_done, step, shift_done, exp_done = (sem(x) for x in ("rms_in", "rms_done", "step", "shift", "exp"))
        padded, maxed, cut, marked_done = sem("padded"), sem("maxed"), sem("cut"), sem("marked")
        block = ctx.enter_context(nc.Block())

        @block.scalar
        def _(act):
            if layer == 0:
                nc.scalar.activation(square[:], k.h_t[:], ACT.Square).then_inc(squared, 1)
            act.wait_ge(shift_done, 1)
            nc.scalar.activation(weight[:], shifted[:], ACT.Exp).then_inc(exp_done, 1)

        @block.gpsimd
        def _(pool):
            if layer == 0:
                pool.wait_ge(rms_in, 1)
                nc.gpsimd.tensor_tensor(rms[:], mean_sq[:], k.minus_half[:, 0:1].broadcast_to([P, NT]),
                                        ALU.pow).then_inc(rms_done, 1)

        @block.tensor
        def _(pe):
            rw = w if layer == 0 else small(k, "rw1").rearrange("p (c e) -> p c e", c=C)
            if layer == 0:
                pe.wait_ge(w_scaled, 1)
                pe.wait_ge(squared, 1)
            for t in range(NT):
                for c in range(C):
                    last = nc.tensor.matmul(l_ps[:, t, 0:n], k.h_t[:, c, t * P:(t + 1) * P], rw[:, c, :],
                                            start=c == 0, stop=c == C - 1)
                if layer == 0:
                    for c in range(C):
                        last = nc.tensor.matmul(l_ps[:, t, n:n + 1], square[:, c, t * P:(t + 1) * P],
                                                k.ones[:, 0:1], start=c == 0, stop=c == C - 1)
            last.then_inc(logits_done, 1)

        @block.vector
        def _(dve):
            def over(ap):
                return ap.unsqueeze(2).broadcast_to([P, NT, n])

            nc.vector.memset(ranked[:, :, n:n + 8], PAD).then_inc(padded, 1)
            if layer == 0:
                nc.vector.tensor_tensor(w[:], small(k, "rw0").rearrange("p (c e) -> p c e", c=C),
                                        small(k, "rscale").unsqueeze(2).broadcast_to([P, C, n]),
                                        ALU.mult).then_inc(w_scaled, 1)
                dve.wait_ge(logits_done, 1)
                nc.vector.tensor_scalar(mean_sq[:], l_ps[:, :, n], 1.0 / D, 1e-6, ALU.mult,
                                        ALU.add).then_inc(rms_in, 1)
                dve.wait_ge(rms_done, 1)
                nc.vector.scalar_tensor_tensor(out=logit[:], in0=l_ps[:, :, 0:n], scalar=1.0 / math.sqrt(D),
                                               in1=over(rms[:]), op0=ALU.mult, op1=ALU.mult).then_inc(step, 1)
            else:
                dve.wait_ge(logits_done, 1)
                nc.vector.tensor_tensor(logit[:], l_ps[:, :, 0:n],
                                        small(k, "rb1").unsqueeze(1).broadcast_to([P, NT, n]),
                                        ALU.add).then_inc(step, 1)
            dve.wait_ge(step, 1)
            nc.vector.tensor_reduce(top[:], logit[:], AX, ALU.max).then_inc(step, 1)
            dve.wait_ge(step, 2)
            nc.vector.tensor_tensor(shifted[:], logit[:], over(top[:]), ALU.subtract).then_inc(shift_done, 1)
            dve.wait_ge(exp_done, 1)
            nc.vector.tensor_reduce(total[:], weight[:], AX, ALU.add).then_inc(step, 1)
            dve.wait_ge(step, 3)
            nc.vector.reciprocal(inv[:], total[:]).then_inc(step, 1)
            dve.wait_ge(step, 4)
            nc.vector.tensor_tensor(prob[:], weight[:], over(inv[:]), ALU.mult).then_inc(step, 1)
            dve.wait_ge(step, 5)
            nc.vector.tensor_copy(ranked[:, :, 0:n], logit[:] if layer == 0 else prob[:]).then_inc(step, 1)
            dve.wait_ge(step, 6)
            dve.wait_ge(padded, 1)
            for t in range(NT):
                nc.vector.max(largest[:, t, :], ranked[:, t, :]).then_inc(maxed, 1)
            dve.wait_ge(maxed, NT)
            nc.vector.memset(largest[:, :, top_n:8], PAD).then_inc(cut, 1)
            dve.wait_ge(cut, 1)
            for t in range(NT):
                nc.vector.match_replace(marked[:, t, :], largest[:, t, :], ranked[:, t, :],
                                        MARK).then_inc(marked_done, 1)
            dve.wait_ge(marked_done, NT)
            nc.vector.tensor_scalar(chosen[:], marked[:, :, 0:n], MARK, None, ALU.is_equal).then_inc(step, 1)
            dve.wait_ge(step, 7)
            nc.vector.tensor_tensor(kept[:], prob[:], chosen[:], ALU.mult).then_inc(step, 1)
            dve.wait_ge(step, 8)
            nc.vector.tensor_reduce(total[:], kept[:], AX, ALU.add).then_inc(step, 1)
            dve.wait_ge(step, 9)
            if layer == 0:
                nc.vector.tensor_scalar(none[:], total[:], 0.0, None, ALU.is_le).then_inc(step, 1)
                dve.wait_ge(step, 10)
                nc.vector.tensor_tensor(total[:], total[:], none[:], ALU.add).then_inc(step, 1)
            else:
                nc.vector.tensor_scalar(none[:], total[:], 1e-12, None, ALU.max).then_inc(step, 1)
                dve.wait_ge(step, 10)
                nc.vector.tensor_copy(total[:], none[:]).then_inc(step, 1)
            dve.wait_ge(step, 11)
            nc.vector.reciprocal(inv[:], total[:]).then_inc(step, 1)
            dve.wait_ge(step, 12)
            nc.vector.tensor_tensor(k.combine[:, :, 0:n], kept[:], over(inv[:]), ALU.mult).then_inc(step, 1)
            if layer == 0:
                dve.wait_ge(step, 13)
                nc.vector.tensor_tensor(k.combine[:, :, 0:n], k.combine[:, :, 0:n],
                                        small(k, "pes").unsqueeze(1).broadcast_to([P, NT, n]), ALU.mult)


def experts(nc, k, layer, up_w, down_w, func):
    GR, UNITS = 8, 4
    per_expert = layer == 1
    Y = 8 if per_expert else 4
    HALF = T // 2
    with ExitStack() as ctx:
        def sb(name, shape, dt=F32):
            return ctx.enter_context(nc.sbuf_tensor(f"{name}_e{layer}", shape, dt))

        def bank(name, n):
            return [ctx.enter_context(nc.psum_tensor(f"{name}{j}_e{layer}", [P, BANK], F32)) for j in range(n)]

        def sem(name):
            return ctx.enter_context(nc.semaphore(f"{name}_e{layer}"))

        up = [sb(f"up{s}", [P, C, 2, HID]) for s in range(2)]
        down = [sb(f"down{s}", [P, HC, D]) for s in range(2)]
        gate = [sb(f"gate{s}", [P, HALF]) for s in range(2)]
        hidden = [sb(f"hidden{s}", [P, HC, HALF]) for s in range(2)]
        g_ps, u_ps, y_ps = bank("g_ps", 2), bank("u_ps", 2), bank("y_ps", 4)
        up_in = [sem(f"up_in{s}") for s in range(2)]
        down_in = [sem(f"down_in{s}") for s in range(2)]
        up_done, gate_done, y_done = sem("up_done"), sem("gate_done"), sem("y_done")
        gated = sem("gated")
        x_added = sem("x_added")
        first_added = sem("first_added")
        block = ctx.enter_context(nc.Block())

        @block.sync
        def _(sp):
            def load(g, s):
                sp.dma_start(up[s][:], up_w[g].rearrange("p c (j h) -> p c j h", j=2)).then_inc(up_in[s], 16)
                sp.dma_start(down[s][:], down_w[g]).then_inc(down_in[s], 16)

            load(0, 0)
            load(1, 1)
            with sp.Fori(0, GR // 2 - 1) as i:
                for s in range(2):
                    sp.wait_ge(y_done, i * (UNITS * Y) + (2 * s + 2) * Y)
                    load(i * 2 + (s + 2), s)
            if per_expert:
                sp.wait_ge(y_done, GR // 2 * UNITS * Y - 2 * Y)
                load(GR, 0)

        @block.tensor
        def _(pe):
            def ups(s, half, unit, loads):
                pe.wait_ge(up_in[s], loads)
                for hc in range(HC):
                    b = hc % 2
                    pe.wait_ge(gated, unit * HC + (hc + 1))
                    for ps, j in ((g_ps[b], 0), (u_ps[b], 1)):
                        for c in range(C):
                            last = nc.tensor.matmul(ps[:], up[s][:, c, j, hc * P:(hc + 1) * P],
                                                    k.h_t[:, c, half * HALF:(half + 1) * HALF],
                                                    start=c == 0, stop=c == C - 1)
                    last.then_inc(up_done, 1)

            def downs(s, u, unit, loads, y0, by_expert):
                pe.wait_ge(down_in[s], loads)
                pe.wait_ge(gated, unit * HC + (HC + 2))
                hid = hidden[u % 2]
                m = 0
                for t in range(4):
                    rows = slice(t * P, (t + 1) * P)
                    for pair in range(2 if by_expert else 1):
                        y = y_ps[m % 4]
                        pe.wait_ge(x_added, y0 + (m + 1))
                        if by_expert:
                            for j in range(2):
                                last = nc.tensor.matmul(y[:, j * D:(j + 1) * D], hid[:, 2 * pair + j, rows],
                                                        down[s][:, 2 * pair + j, :], start=True, stop=True)
                        else:
                            for hc in range(HC):
                                last = nc.tensor.matmul(y[:, 0:D], hid[:, hc, rows], down[s][:, hc, :],
                                                        start=hc == 0, stop=hc == HC - 1)
                        last.then_inc(y_done, 1)
                        m += 1

            with pe.Fori(0, GR // 2) as i:
                def up_unit(u):
                    ups(u // 2, u % 2, i * UNITS + u, i * 16 + 16)

                def down_unit(u):
                    downs(u // 2, u, i * UNITS + u, i * 16 + 16, i * (UNITS * Y) + u * Y, per_expert)

                up_unit(0)
                for u in range(1, UNITS):
                    up_unit(u)
                    down_unit(u - 1)
                down_unit(UNITS - 1)
            if per_expert:
                done, loads = GR // 2 * UNITS, 16 * (GR // 2 + 1)
                ups(0, 0, done, loads)
                ups(0, 1, done + 1, loads)
                downs(0, 0, done, loads, done * Y, False)
                downs(0, 1, done + 1, loads, done * Y + 4, False)

        @block.scalar
        def _(act):
            def gates(unit):
                for hc in range(HC):
                    act.wait_ge(up_done, unit * HC + (hc + 1))
                    nc.scalar.activation(gate[hc % 2][:], g_ps[hc % 2][:], func).then_inc(gate_done, 1)

            with act.Fori(0, GR // 2) as i:
                for u in range(UNITS):
                    gates(i * UNITS + u)
            if per_expert:
                for u in range(2):
                    gates(GR // 2 * UNITS + u)

        @block.vector
        def _(dve):
            def gatings(u, unit):
                for hc in range(HC):
                    dve.wait_ge(gate_done, unit * HC + (hc + 1))
                    nc.vector.tensor_tensor(hidden[u % 2][:, hc, :], gate[hc % 2][:], u_ps[hc % 2][:],
                                            ALU.mult).then_inc(gated, 1)

            def adds(half, y0, g, by_expert):
                m = 0
                for t in range(4 * half, 4 * half + 4):
                    for pair in range(2 if by_expert else 1):
                        y = y_ps[m % 4]
                        dve.wait_ge(y_done, y0 + (m + 1))
                        dve.wait_ge(x_added, y0 + (m + 4))
                        if by_expert:
                            for j in range(2):
                                if j:
                                    dve.wait_ge(first_added, y0 + (m + 1))
                                nc.vector.scalar_tensor_tensor(
                                    out=k.x[:, t, :], in0=y[:, j * D:(j + 1) * D],
                                    scalar=k.combine[:, t, bass.ds(g * 4 + (2 * pair + j), 1)], in1=k.x[:, t, :],
                                    op0=ALU.mult, op1=ALU.add).then_inc(x_added if j else first_added, 1)
                        elif g is None:
                            nc.vector.tensor_tensor(k.x[:, t, :], k.x[:, t, :], y[:, 0:D],
                                                    ALU.add).then_inc(x_added, 1)
                        else:
                            nc.vector.scalar_tensor_tensor(
                                out=k.x[:, t, :], in0=y[:, 0:D], scalar=k.combine[:, t, bass.ds(g, 1)],
                                in1=k.x[:, t, :], op0=ALU.mult, op1=ALU.add).then_inc(x_added, 1)
                        m += 1

            dve.sem_inc(gated, 2)
            dve.sem_inc(x_added, 4)
            with dve.Fori(0, GR // 2) as i:
                def add_unit(u):
                    adds(u % 2, i * (UNITS * Y) + u * Y, i * 2 + u // 2, per_expert)

                gatings(0, i * UNITS)
                for u in range(1, UNITS):
                    gatings(u, i * UNITS + u)
                    add_unit(u - 1)
                add_unit(UNITS - 1)
            if per_expert:
                done = GR // 2 * UNITS
                gatings(0, done)
                gatings(1, done + 1)
                adds(0, done * Y, None, False)
                adds(1, done * Y + 4, None, False)


class Ring:

    def __init__(self, before):
        self.before, self.n = before, 0

    def next(self):
        bank, use = self.n % 2, self.n // 2 + 1
        self.n += 1
        return bank, self.before + use

    def had(self, bank):
        return self.before + (self.n + 1 - bank) // 2


def cross_attention(nc, k, src):
    STEPS = 2 * PAIRS1
    Q_USES, A_USES = 2, 16
    AHEAD = (Q_USES + A_USES) // 2
    PER_TILE = (STEPS * 5 + Q_USES + A_USES) // 2
    SCALE = HD1 ** -0.5
    M_USES = STEPS + 1
    with ExitStack() as ctx:
        def sb(name, shape, dt=F32):
            return ctx.enter_context(nc.sbuf_tensor(name, shape, dt))

        def ps(name, shape):
            return ctx.enter_context(nc.psum_tensor(name, shape, F32))

        def sem(name):
            return ctx.enter_context(nc.semaphore(name))

        wq, wo = sb("wq1", [P, C, INNER]), sb("wo1", [P, PAIRS1, D])
        wk, wv = sb("wk1", [P, 2, PAIRS1, D]), sb("wv1", [P, 2, C, INNER])
        ct = [sb(f"ct{b}", [P, C, M]) for b in range(2)]
        cn = [sb(f"cn{b}", [P, NBLK, D]) for b in range(2)]
        q = sb("q1", [P, PAIRS1, 2, P])
        a = sb("a1", [P, 2, C, 2, H1, S])
        prob = [sb(f"prob1{s}", [P, M]) for s in range(2)]
        pt = sb("pt1", [P, NBLK, P])
        top = [sb(f"top1{s}", [P, 2]) for s in range(2)]
        bias = [sb(f"bias1{s}", [P, 2]) for s in range(2)]
        total = [sb(f"total1{s}", [P, 2]) for s in range(2)]
        inv = [sb(f"inv1{s}", [P, 2]) for s in range(2)]
        o = sb("o1", [P, 2, D])
        ot = sb("ot1", [P, 4, P])
        head_out = sb("head_out", [P, PAIRS1, P])
        s_ps = ps("s1_ps", [P, 4, BANK])
        t_ps = [ps(f"t1_ps{j}", [P, BANK]) for j in range(2)]
        o_ps, m_ps = ps("o1_ps", [P, BANK]), ps("m1_ps", [P, BANK])
        w_in = sem("w1_in")
        ct_in = [sem(f"ct_in{b}") for b in range(2)]
        cn_in = [sem(f"cn_in{b}") for b in range(2)]
        scored, topped, bias_done, exp_done = sem("scored1"), sem("topped1"), sem("bias1_done"), sem("exp1_done")
        t_done = [sem(f"t1_done{j}") for j in range(2)]
        t_kept = [sem(f"t1_kept{j}") for j in range(2)]
        summed, inv_done, sums_kept = sem("summed1"), sem("inv1_done"), sem("sums1_kept")
        m_done, m_kept = sem("m1_done"), sem("m1_kept")
        q_zeroed = sem("q_zeroed")
        block = ctx.enter_context(nc.Block())

        def tiles(eng, body):
            with eng.Fori(0, NT - 1) as i:
                body(i, False)
            body(NT - 1, True)

        @block.sync
        def _(sp):
            sp.dma_start(wq[:], src["wq1"]).then_inc(w_in, 16)
            sp.dma_start(wk[:], src["wk1"]).then_inc(w_in, 16)
            for b in range(2):
                sp.dma_start(ct[b][:], src["ctx_t"][b, :, :, 0:M]).then_inc(ct_in[b], 16)
                sp.dma_start(cn[b][:], src["ctx_n"][b]).then_inc(cn_in[b], 16)
            sp.dma_start(wv[:], src["wv1"]).then_inc(w_in, 16)
            sp.dma_start(wo[:], src["wo1"]).then_inc(w_in, 16)
            with sp.Fori(0, NT - 1) as i:
                for b in range(2):
                    sp.wait_ge(scored, i * STEPS + (b + 1) * PAIRS1)
                    sp.dma_start(ct[b][:], src["ctx_t"][i * 2 + (b + 2)][:, :, 0:M]).then_inc(ct_in[b], 16)
                    sp.wait_ge(summed, i * STEPS + (b + 1) * PAIRS1)
                    sp.dma_start(cn[b][:], src["ctx_n"][i * 2 + (b + 2)]).then_inc(cn_in[b], 16)


        @block.tensor
        def _(pe):
            def use(ring):
                bank, count = ring.next()
                pe.wait_ge(t_kept[bank], count - 1)
                return bank

            def queries(ring, t):
                for half in range(2):
                    bank = use(ring)
                    for j in range(4):
                        p = 4 * half + j
                        for c in range(C):
                            last = nc.tensor.matmul(t_ps[bank][:, j * P:(j + 1) * P], wq[:, c, p * P:(p + 1) * P],
                                                    k.h_t[:, c, bass.ds(t * P, P)], start=c == 0, stop=c == C - 1)
                    last.then_inc(t_done[bank], 1)

            def key_side(ring):
                for bank in range(2):
                    pe.wait_ge(t_kept[bank], ring.had(bank))
                for quad in range(4):
                    for kind in range(2):
                        for c in range(C):
                            bank = use(ring)
                            for j in range(2):
                                p = 2 * quad + j
                                last = nc.tensor.matmul(
                                    t_ps[bank][:, j * 2 * P:(j + 1) * 2 * P], wk[:, kind, p, c * P:(c + 1) * P],
                                    q[:, p, :, :].rearrange("p r n -> p (r n)"), start=True, stop=True)
                            last.then_inc(t_done[bank], 1)

            def scores(n, part):
                b, p = divmod(n, PAIRS1)
                first, width = (0, TXT) if part == 0 else (TXT + (part - 1) * SBLK, SBLK)
                for c in range(C):
                    last = nc.tensor.matmul(
                        s_ps[:, part, 0:width],
                        a[:, min(part, 1), c, b, 2 * p:2 * p + 2, :].rearrange("p h q -> p (h q)"),
                        ct[b][:, c, first:first + width], start=c == 0, stop=c == C - 1)
                return last

            def turn(ring, n, g):
                bank = use(ring)
                for j in range(1 if g == 0 else 4):
                    blk = 0 if g == 0 else 4 * (g - 1) + j
                    first, width = (0, TXT) if g == 0 else (TXT + blk * IBLK, IBLK)
                    last = nc.tensor.transpose(t_ps[bank][0:width, j * P:(j + 1) * P],
                                               prob[n % 2][:, first:first + width], k.ident)
                last.then_inc(t_done[bank], 1)

            def sums(n, base, done):
                b = n // PAIRS1
                for bank in range(2):
                    pe.wait_ge(t_kept[bank], done[bank])
                pe.wait_ge(sums_kept, base + n + 1)
                nc.tensor.matmul(o_ps[:, 0:D], pt[0:TXT, 0, :], cn[b][0:TXT, 0, :], start=True, stop=True)
                for j in range(IB):
                    last = nc.tensor.matmul(o_ps[:, D:2 * D], pt[0:IBLK, 1 + j, :], cn[b][0:IBLK, 1 + j, :],
                                            start=j == 0, stop=j == IB - 1)
                last.then_inc(summed, 1)

            def turn_sums(ring, n, base):
                pe.wait_ge(sums_kept, base + n + 2)
                bank = use(ring)
                for j in range(4):
                    last = nc.tensor.transpose(t_ps[bank][:, j * P:(j + 1) * P],
                                               o[:, j // 2, (j % 2) * P:(j % 2 + 1) * P], k.ident)
                last.then_inc(t_done[bank], 1)
                return bank, ring.had(bank)

            def value_side(n, m_base, kept):
                pe.wait_ge(t_kept[kept[0]], kept[1])
                pe.wait_ge(m_kept, m_base + n + 1)
                for r in range(2):
                    h = 2 * (n % PAIRS1) + r
                    for j in range(4):
                        last = nc.tensor.matmul(m_ps[r * S:(r + 1) * S, 0:S],
                                                wv[:, j // 2, j % 2, h * HD1:(h + 1) * HD1],
                                                ot[:, j, r * S:(r + 1) * S], start=j == 0, stop=j == 3)
                last.then_inc(m_done, 1)

            def project(m_base):
                pe.wait_ge(m_kept, m_base + STEPS + 1)
                for p in range(PAIRS1):
                    nc.tensor.matmul(m_ps[:, 0:D], head_out[:, p, :], wo[:, p, :], start=p == 0, stop=False)
                nc.tensor.matmul(m_ps[:, 0:D], k.ones[0:1, :], k.row("bo1"), start=False,
                                 stop=True).then_inc(m_done, 1)

            pe.wait_ge(w_in, 64)
            start = Ring(0)
            queries(start, 0)
            key_side(start)

            def body(i, last_tile):
                ring = Ring(i * PER_TILE + AHEAD)
                base, m_base = i * STEPS, i * M_USES
                for bank in range(2):
                    pe.wait_ge(t_kept[bank], ring.had(bank))
                for n in range(STEPS + 2):
                    if n % PAIRS1 == 0 and n < STEPS:
                        pe.wait_ge(ct_in[n // PAIRS1], i * 16 + 16)
                        pe.wait_ge(cn_in[n // PAIRS1], i * 16 + 16)
                    if n <= STEPS:
                        pe.wait_ge(exp_done, base + n + 1)
                    for g in range(4):
                        if 1 <= n <= STEPS:
                            turn(ring, n - 1, g)
                        if n < STEPS:
                            last = scores(n, g)
                    if n < STEPS:
                        last.then_inc(scored, 1)
                    turned = [ring.had(bank) for bank in range(2)]
                    if n >= 2:
                        kept = turn_sums(ring, n - 2, base)
                    if 1 <= n <= STEPS:
                        sums(n - 1, base, turned)
                    if n >= 2:
                        value_side(n - 2, m_base, kept)
                    if not last_tile and n == PAIRS1:
                        queries(ring, i + 1)
                    if not last_tile and n == STEPS:
                        key_side(ring)
                project(m_base)

            tiles(pe, body)

        def keep(eng, copy, mine, ring, out, rows=P, cols=BANK):
            bank, count = ring.next()
            if bank == mine:
                eng.wait_ge(t_done[bank], count)
                copy(out, t_ps[bank][0:rows, 0:cols]).then_inc(t_kept[bank], 1)

        def keep_turn(eng, copy, mine, ring, g):
            if g == 0:
                keep(eng, copy, mine, ring, pt[0:TXT, 0, :], TXT, P)
            else:
                keep(eng, copy, mine, ring, pt[0:IBLK, 4 * g - 3:4 * g + 1, :].rearrange("p j n -> p (j n)"), IBLK)

        def keep_queries(eng, copy, mine, ring):
            for half in range(2):
                bank, count = ring.next()
                if bank == mine:
                    eng.wait_ge(t_done[bank], count)
                    for r in range(2):
                        rows = slice(r * HD1, (r + 1) * HD1)
                        last = copy(q[rows, 4 * half:4 * half + 4, r, :],
                                    t_ps[bank][rows, :].rearrange("p (j n) -> p j n", j=4))
                    last.then_inc(t_kept[bank], 1)

        def keep_key_side(eng, copy, mine, ring):
            for quad in range(4):
                for kind in range(2):
                    for c in range(C):
                        bank, count = ring.next()
                        if bank == mine:
                            eng.wait_ge(t_done[bank], count)
                            copy(a[:, kind, c, :, 4 * quad:4 * quad + 4, :],
                                 t_ps[bank][:].rearrange("p (h b q) -> p b h q", h=4, b=2)).then_inc(t_kept[bank], 1)

        @block.scalar
        def _(act):
            def copy(out, in_):
                return nc.scalar.activation(out, in_, ACT.Copy)

            act.sem_inc(exp_done, 1)
            act.wait_ge(q_zeroed, 1)
            start = Ring(0)
            keep_queries(act, copy, 0, start)
            keep_key_side(act, copy, 0, start)

            def body(i, last_tile):
                ring = Ring(i * PER_TILE + AHEAD)
                for n in range(STEPS + 2):
                    s = n % 2
                    if 1 <= n <= STEPS:
                        for g in range(4):
                            keep_turn(act, copy, 0, ring, g)
                    if n >= 2:
                        keep(act, copy, 0, ring, ot[:].rearrange("p j n -> p (j n)"))
                    if n < STEPS:
                        act.wait_ge(bias_done, i * STEPS + n + 1)
                        nc.scalar.activation(prob[s][:, TXT:M].rearrange("p (j m) -> p j m", j=SB),
                                             s_ps[:, 1:4, 0:SBLK], ACT.Exp, bias=bias[s][:, 1:2], scale=SCALE,
                                             accum_out=total[s][:, 1:2])
                        nc.scalar.activation(prob[s][:, 0:TXT], s_ps[:, 0, 0:TXT], ACT.Exp, bias=bias[s][:, 0:1],
                                             scale=SCALE, accum_out=total[s][:, 0:1]).then_inc(exp_done, 1)
                    if not last_tile and n == PAIRS1:
                        keep_queries(act, copy, 0, ring)
                    if not last_tile and n == STEPS:
                        keep_key_side(act, copy, 0, ring)

            tiles(act, body)

        @block.vector
        def _(dve):
            def copy(out, in_):
                return nc.vector.tensor_copy(out, in_)

            dve.sem_inc(sums_kept, 1)
            dve.sem_inc(m_kept, 1)
            nc.vector.memset(q[:], 0.0).then_inc(q_zeroed, 1)
            dve.wait_ge(q_zeroed, 1)
            start = Ring(0)
            keep_queries(dve, copy, 1, start)
            keep_key_side(dve, copy, 1, start)

            def body(i, last_tile):
                ring = Ring(i * PER_TILE + AHEAD)
                base = i * STEPS
                for n in range(STEPS + 2):
                    s = n % 2
                    if 1 <= n <= STEPS:
                        for g in range(4):
                            keep_turn(dve, copy, 1, ring, g)
                    if n < STEPS:
                        dve.wait_ge(scored, base + n + 1)
                        nc.vector.tensor_reduce(top[s][:, 0:1], s_ps[:, 0, 0:TXT], AX, ALU.max)
                        nc.vector.tensor_reduce(top[s][:, 1:2], s_ps[:, 1:4, 0:SBLK], mybir.AxisListType.XY,
                                                ALU.max).then_inc(topped, 1)
                        dve.wait_ge(topped, base + n + 1)
                        nc.vector.tensor_scalar(bias[s][:], top[s][:], -SCALE, None, ALU.mult).then_inc(bias_done, 1)
                    if n >= 2:
                        keep(dve, copy, 1, ring, ot[:].rearrange("p j n -> p (j n)"))
                    if 1 <= n <= STEPS:
                        dve.wait_ge(exp_done, base + n + 1)
                        nc.vector.reciprocal(inv[1 - s][:], total[1 - s][:]).then_inc(inv_done, 1)
                        dve.wait_ge(summed, base + n)
                        dve.wait_ge(inv_done, base + n)
                        for kind in range(2):
                            last = nc.vector.tensor_scalar(o[:, kind, :], o_ps[:, kind * D:(kind + 1) * D],
                                                           inv[1 - s][:, kind:kind + 1], None, ALU.mult)
                        last.then_inc(sums_kept, 1)
                    if n >= 2:
                        b, p = divmod(n - 2, PAIRS1)
                        dve.wait_ge(m_done, i * M_USES + n - 1)
                        nc.vector.tensor_copy(head_out[:, p, b * S:(b + 1) * S], m_ps[:, 0:S]).then_inc(m_kept, 1)
                    if not last_tile and n == PAIRS1:
                        keep_queries(dve, copy, 1, ring)
                    if not last_tile and n == STEPS:
                        keep_key_side(dve, copy, 1, ring)
                dve.wait_ge(m_done, (i + 1) * M_USES)
                xt = k.x[:, bass.ds(i, 1), :].rearrange("p a d -> p (a d)")
                nc.vector.tensor_tensor(xt, xt, m_ps[:, 0:D], ALU.add).then_inc(m_kept, 1)

            tiles(dve, body)


def scan_layer(nc, k, src):
    HALF = T // 2
    HB = NB // 2
    with ExitStack() as outer:
        def keep(name, shape, dt=F32):
            return outer.enter_context(nc.sbuf_tensor(name, shape, dt))

        gate = keep("gate_z", [P, C, T])
        xc = keep("xc", [P, C, T])
        u = keep("u", [P, C, T])
        dt = keep("dt", [P, T])
        a_neg = keep("a_neg", [P, C * NS])
        par = keep("par", [NPAR, T])
        diag = keep("diag_d", [P, C, P])
        w_out = keep("w_out", [P, C, D])
        gated = keep("gated_y", [P, C, T])
        w_out_in = outer.enter_context(nc.semaphore("w_out_in"))

        with ExitStack() as ctx:
            w_in_proj = ctx.enter_context(nc.sbuf_tensor("w_in_proj", [P, C, 2 * D], F32))
            xpad = ctx.enter_context(nc.sbuf_tensor("xpad", [P, C, NB, S + KC - 1], F32))
            acc = [ctx.enter_context(nc.sbuf_tensor(f"conv_acc{c}", [P, NB, S], F32)) for c in range(C)]
            ps = ctx.enter_context(nc.psum_tensor("xz_ps", [P, 2 * C, 2, BANK], F32))
            proj_in = ctx.enter_context(nc.semaphore("proj_in"))
            projected = ctx.enter_context(nc.semaphore("projected"))
            x_kept = ctx.enter_context(nc.semaphore("x_kept"))
            pad_zeroed = ctx.enter_context(nc.semaphore("pad_zeroed"))
            tap_done = ctx.enter_context(nc.semaphore("tap_done"))
            block = ctx.enter_context(nc.Block())

            @block.sync
            def _(sp):
                sp.dma_start(w_in_proj[:], src["win"]).then_inc(proj_in, 16)
                sp.dma_start(w_out[:], src["wout"]).then_inc(w_out_in, 16)

            @block.tensor
            def _(pe):
                pe.wait_ge(proj_in, 16)
                for e in range(2 * C):
                    for g in range(2):
                        for c in range(C):
                            last = nc.tensor.matmul(ps[:, e, g, :], w_in_proj[:, c, e * P:(e + 1) * P],
                                                    k.h_t[:, c, g * HALF:(g + 1) * HALF],
                                                    start=c == 0, stop=c == C - 1)
                        last.then_inc(projected, 1)

            @block.scalar
            def _(act):
                for e in range(C):
                    for g in range(2):
                        act.wait_ge(projected, 2 * e + g + 1)
                        nc.scalar.activation(xpad[:, e, g * HB:(g + 1) * HB, KC - 1:],
                                             ps[:, e, g, :].rearrange("p (b l) -> p b l", l=S),
                                             ACT.Copy).then_inc(x_kept, 1)
                for e in range(C):
                    for g in range(2):
                        act.wait_ge(projected, 2 * (C + e) + g + 1)
                        nc.scalar.activation(gate[:, e, g * HALF:(g + 1) * HALF], ps[:, C + e, g, :], ACT.Silu)
                for c in range(C):
                    act.wait_ge(tap_done, KC * C - C + c + 1)
                    nc.scalar.activation(xc[:, c, :], acc[c][:].rearrange("p b l -> p (b l)"), ACT.Silu,
                                         bias=small(k, "convb")[:, c:c + 1])

            @block.vector
            def _(dve):
                nc.vector.memset(xpad[:, :, :, 0:KC - 1], 0.0).then_inc(pad_zeroed, 1)
                dve.wait_ge(pad_zeroed, 1)
                w = small(k, "convw")
                for tap in range(KC):
                    for c in range(C):
                        seen = xpad[:, c, :, tap:tap + S]
                        if tap == 0:
                            dve.wait_ge(x_kept, 2 * c + 2)
                            nc.vector.tensor_scalar(acc[c][:], seen, w[:, c * KC:c * KC + 1], None,
                                                    ALU.mult).then_inc(tap_done, 1)
                        else:
                            dve.wait_ge(tap_done, C * (tap - 1) + c + 1)
                            nc.vector.scalar_tensor_tensor(
                                out=acc[c][:], in0=seen, scalar=w[:, c * KC + tap:c * KC + tap + 1], in1=acc[c][:],
                                op0=ALU.mult, op1=ALU.add).then_inc(tap_done, 1)

        with ExitStack() as ctx:
            w_par = ctx.enter_context(nc.sbuf_tensor("w_par", [P, C, NPAR], F32))
            pick_dt = ctx.enter_context(nc.sbuf_tensor("pick_dt", [NPAR, P], F32))
            mag = ctx.enter_context(nc.sbuf_tensor("mag", [NPAR, T], F32))
            pos = ctx.enter_context(nc.sbuf_tensor("pos_part", [NPAR, T], F32))
            exp_a = ctx.enter_context(nc.sbuf_tensor("exp_a", [P, C * NS], F32))
            p_ps = ctx.enter_context(nc.psum_tensor("par_ps", [P, 2, BANK], F32))
            d_ps = ctx.enter_context(nc.psum_tensor("dt_ps", [P, 2, BANK], F32))
            par_in, par_done, par_kept = (ctx.enter_context(nc.semaphore(n)) for n in ("par_in", "par_done", "par_kept"))
            soft, soft_kept = (ctx.enter_context(nc.semaphore(n)) for n in ("softplus_step", "softplus_kept"))
            pos_done, pick_set, dt_done, dt_kept = (
                ctx.enter_context(nc.semaphore(n)) for n in ("pos_done", "pick_set", "dt_done", "dt_kept"))
            exp_done = ctx.enter_context(nc.semaphore("exp_a_done"))
            block = ctx.enter_context(nc.Block())
            row = slice(NPAR - 1, NPAR)

            @block.sync
            def _(sp):
                sp.dma_start(w_par[:], src["wpar"]).then_inc(par_in, 16)

            @block.tensor
            def _(pe):
                pe.wait_ge(par_in, 16)
                for g in range(2):
                    for c in range(C):
                        last = nc.tensor.matmul(p_ps[0:NPAR, g, :], w_par[:, c, :], xc[:, c, g * HALF:(g + 1) * HALF],
                                                start=c == 0, stop=c == C - 1)
                last.then_inc(par_done, 1)
                pe.wait_ge(soft_kept, 1)
                pe.wait_ge(pick_set, 2)
                for g in range(2):
                    last = nc.tensor.matmul(d_ps[:, g, :], pick_dt[:], par[:, g * HALF:(g + 1) * HALF],
                                            start=True, stop=True)
                last.then_inc(dt_done, 1)

            @block.scalar
            def _(act):
                nc.scalar.activation(exp_a[:], small(k, "alog"), ACT.Exp).then_inc(exp_done, 1)
                act.wait_ge(par_done, 1)
                nc.scalar.activation(par[:], p_ps[0:NPAR].rearrange("p g n -> p (g n)"), ACT.Copy).then_inc(par_kept, 1)
                act.wait_ge(par_kept, 1)
                nc.scalar.activation(mag[row], par[row], ACT.Abs).then_inc(soft, 1)
                act.wait_ge(soft, 1)
                nc.scalar.activation(mag[row], mag[row], ACT.Exp, scale=-1.0).then_inc(soft, 1)
                act.wait_ge(soft, 2)
                nc.scalar.activation(mag[row], mag[row], ACT.Ln, bias=1.0).then_inc(soft, 1)
                act.wait_ge(dt_done, 1)
                nc.scalar.activation(dt[:], d_ps[:].rearrange("p g n -> p (g n)"), ACT.Copy).then_inc(dt_kept, 1)

            @block.vector
            def _(dve):
                nc.vector.memset(pick_dt[:], 0.0).then_inc(pick_set, 1)
                dve.wait_ge(pick_set, 1)
                nc.vector.memset(pick_dt[row], 1.0).then_inc(pick_set, 1)
                dve.wait_ge(exp_done, 1)
                nc.vector.tensor_scalar(a_neg[:], exp_a[:], -1.0, None, ALU.mult)
                for c in range(C):
                    nc.vector.tensor_scalar(diag[:, c, :], k.ident, small(k, "dpar")[:, c:c + 1], None, ALU.mult)
                dve.wait_ge(par_kept, 1)
                nc.vector.tensor_scalar(pos[row], par[row], 0.0, None, ALU.max).then_inc(pos_done, 1)
                dve.wait_ge(pos_done, 1)
                dve.wait_ge(soft, 3)
                nc.vector.tensor_tensor(par[row], pos[row], mag[row], ALU.add).then_inc(soft_kept, 1)
                dve.wait_ge(dt_kept, 1)
                for c in range(C):
                    nc.vector.tensor_tensor(u[:, c, :], xc[:, c, :], dt[:], ALU.mult)

        with ExitStack() as ctx:
            def sb(name, shape):
                return ctx.enter_context(nc.sbuf_tensor(name, shape, F32))

            def sem(name):
                return ctx.enter_context(nc.semaphore(name))

            ones = sb("ones33", [NPAR, P])
            row_b, row_c = sb("row_b", [NPAR, T]), sb("row_c", [NPAR, T])
            decay = [sb(f"decay{c}", [P, NB, S]) for c in range(C)]
            drive = [sb(f"drive{c}", [P, T]) for c in range(C)]
            state = [sb(f"state{c}", [P, T]) for c in range(C)]
            read = [sb(f"read{c}", [P, T]) for c in range(C)]
            c_row = sb("c_row", [P, T])
            b_ps = ctx.enter_context(nc.psum_tensor("b_ps", [P, 2, BANK], F32))
            c_ps = ctx.enter_context(nc.psum_tensor("c_ps", [P, 2, BANK], F32))
            y_ps = ctx.enter_context(nc.psum_tensor("scan_y_ps", [P, C, 2, BANK], F32))
            set_up, rows_masked, b_done, c_done = sem("scan_set_up"), sem("rows_masked"), sem("b_done"), sem("c_done")
            c_kept, decayed, driven, scanned = sem("c_kept"), sem("decayed"), sem("driven"), sem("scanned")
            read_done, y_added = sem("read_done"), sem("scan_y_added")
            block = ctx.enter_context(nc.Block())


            @block.scalar
            def _(act):
                def rows(n):
                    nc.scalar.activation(row_b[:], par[:], ACT.Identity, scale=small(k, "ident")[0:NPAR, bass.ds(n, 1)])
                    nc.scalar.activation(row_c[:], par[:], ACT.Identity,
                                         scale=small(k, "ident")[0:NPAR, bass.ds(n + NS, 1)]).then_inc(rows_masked, 1)

                def decays(n):
                    for c in range(C):
                        nc.scalar.activation(decay[c][:, :, 1:], dt[:].rearrange("p (b l) -> p b l", l=S)[:, :, 1:],
                                             ACT.Exp, scale=a_neg[:, bass.ds(n + c * NS, 1)]).then_inc(decayed, 1)

                rows(0)
                act.wait_ge(set_up, 1)
                decays(0)
                act.wait_ge(c_done, 1)
                nc.scalar.activation(c_row[:], c_ps[:].rearrange("p g n -> p (g n)"), ACT.Copy).then_inc(c_kept, 1)
                with act.Fori(0, NS - 1) as n:
                    act.wait_ge(c_done, n + 1)
                    rows(n + 1)
                    for c in range(C):
                        act.wait_ge(scanned, n * 2 + (c + 3))
                        nc.scalar.activation(decay[c][:, :, 1:], dt[:].rearrange("p (b l) -> p b l", l=S)[:, :, 1:],
                                             ACT.Exp, scale=a_neg[:, bass.ds(n + (c * NS + 1), 1)]).then_inc(decayed, 1)
                    act.wait_ge(c_done, n + 2)
                    act.wait_ge(read_done, n * 2 + 4)
                    nc.scalar.activation(c_row[:], c_ps[:].rearrange("p g n -> p (g n)"), ACT.Copy).then_inc(c_kept, 1)

            @block.tensor
            def _(pe):
                def spread(out, row_):
                    for g in range(2):
                        last = nc.tensor.matmul(out[:, g, :], ones[:], row_[:, g * HALF:(g + 1) * HALF],
                                                start=True, stop=True)
                    return last

                def add(c, final):
                    for g in range(2):
                        last = nc.tensor.matmul(y_ps[:, c, g, :], k.ident, read[c][:, g * HALF:(g + 1) * HALF],
                                                start=False, stop=final, skip_group_check=True)
                    last.then_inc(y_added, 1)

                pe.sem_inc(y_added, 2)
                for c in range(C):
                    for g in range(2):
                        nc.tensor.matmul(y_ps[:, c, g, :], diag[:, c, :], xc[:, c, g * HALF:(g + 1) * HALF],
                                         start=True, stop=False, skip_group_check=True)
                pe.wait_ge(set_up, 1)
                pe.wait_ge(rows_masked, 1)
                spread(b_ps, row_b).then_inc(b_done, 1)
                spread(c_ps, row_c).then_inc(c_done, 1)
                with pe.Fori(0, NS - 1) as n:
                    pe.wait_ge(rows_masked, n + 2)
                    pe.wait_ge(driven, n * 2 + 2)
                    spread(b_ps, row_b).then_inc(b_done, 1)
                    pe.wait_ge(c_kept, n + 1)
                    spread(c_ps, row_c).then_inc(c_done, 1)
                    for c in range(C):
                        pe.wait_ge(read_done, n * 2 + (c + 3))
                        add(c, False)
                for c in range(C):
                    pe.wait_ge(read_done, (NS - 1) * 2 + c + 3)
                    add(c, True)

            @block.gpsimd
            def _(pool):
                pool.sem_inc(read_done, 2)
                with pool.Fori(0, NS) as n:
                    pool.wait_ge(c_kept, n + 1)
                    for c in range(C):
                        pool.wait_ge(scanned, n * 2 + (c + 3))
                        pool.wait_ge(y_added, n * 2 + 2)
                        nc.gpsimd.tensor_tensor(read[c][:], state[c][:], c_row[:], ALU.mult).then_inc(read_done, 1)

            @block.vector
            def _(dve):
                dve.sem_inc(scanned, 2)
                nc.vector.memset(ones[:], 1.0)
                for c in range(C):
                    last = nc.vector.memset(decay[c][:], 0.0)
                last.then_inc(set_up, 1)
                with dve.Fori(0, NS) as n:
                    dve.wait_ge(scanned, n * 2 + 2)
                    dve.wait_ge(b_done, n + 1)
                    for c in range(C):
                        nc.vector.tensor_tensor(drive[c][:], u[:, c, :], b_ps[:].rearrange("p g n -> p (g n)"),
                                                ALU.mult).then_inc(driven, 1)
                    for c in range(C):
                        dve.wait_ge(driven, n * 2 + (c + 1))
                        dve.wait_ge(decayed, n * 2 + (c + 1))
                        dve.wait_ge(read_done, n * 2 + 2)
                        nc.vector.tensor_tensor_scan(state[c][:], decay[c][:].rearrange("p b l -> p (b l)"),
                                                     drive[c][:], 0.0, ALU.mult, ALU.add).then_inc(scanned, 1)
                for c in range(C):
                    dve.wait_ge(y_added, (NS - 1) * 2 + c + 3)
                    nc.vector.tensor_tensor(gated[:, c, :], y_ps[:, c].rearrange("p g n -> p (g n)"), gate[:, c, :],
                                            ALU.mult)

        with ExitStack() as ctx:
            o_ps = ctx.enter_context(nc.psum_tensor("scan_o_ps", [P, NT, BANK], F32))
            o_done = ctx.enter_context(nc.semaphore("scan_o_done"))
            block = ctx.enter_context(nc.Block())

            @block.tensor
            def _(pe):
                pe.wait_ge(w_out_in, 16)
                for t in range(NT):
                    for c in range(C):
                        last = nc.tensor.matmul(o_ps[:, t, 0:D], gated[:, c, t * P:(t + 1) * P], w_out[:, c, :],
                                                start=c == 0, stop=c == C - 1)
                    last.then_inc(o_done, 1)

            @block.vector
            def _(dve):
                for t in range(NT):
                    dve.wait_ge(o_done, t + 1)
                    nc.vector.tensor_tensor(k.x[:, t, :], k.x[:, t, :], o_ps[:, t, 0:D], ALU.add)


def perceiver_program(nc, src, out):
    with ExitStack() as ctx:
        def sb(name, shape, dt=F32):
            return ctx.enter_context(nc.sbuf_tensor(name, shape, dt))

        k = Chip()
        k.x = sb("x_sb", [P, NT, D])
        k.h_t = sb("h_t", [P, C, T])
        k.small = sb("small", [P, SMALL_N])
        rows = k.rows = sb("rows", [1, len(ROWS), D])
        k.row = lambda name: rows[:, ROWS[name], :]
        k.ident = small(k, "ident")
        k.ones = sb("ones", [P, P])
        k.minus_half = sb("minus_half", [P, 1])
        k.log_s = sb("log_s", [P, 1])
        k.length = sb("length", [P, NB])
        k.far_count = sb("far_count", [1, 1], I32)
        k.combine = sb("combine", [P, NT, E1])
        load_stage(nc, k, src)
        with ExitStack() as inner:
            k.q0 = inner.enter_context(nc.sbuf_tensor("q0", [P, C, T], F32))
            k.pos = inner.enter_context(nc.sbuf_tensor("pos", [P, NB + 1, PK], F32))
            k.ctx_t = inner.enter_context(nc.sbuf_tensor("ctx_out_t", [P, C, T], F32))
            norm_stage(nc, k, "a")
            positions_stage(nc, k, src)
            local_attention(nc, k, src)
            after_local(nc, k, src)
        norm_stage(nc, k, "b")
        self_attention(nc, k, src)
        norm_stage(nc, k, "c")
        route(nc, k, 0)
        experts(nc, k, 0, src["up0"], src["down0"], ACT.Gelu_apprx_tanh)
        norm_stage(nc, k, "d", clear=True)
        cross_attention(nc, k, src)
        norm_stage(nc, k, "e")
        scan_layer(nc, k, src)
        norm_stage(nc, k, "f")
        route(nc, k, 1)
        experts(nc, k, 1, src["up1"], src["down1"], ACT.Silu)
        store_stage(nc, k, out)


def _small_arrays(np, a):
    part = np.arange(P)
    near = np.concatenate([np.arange(LOW), np.arange(HIGH, M)])
    rows = np.arange(NWIN * WN)
    loc = (part % S)[:, None]
    ref = np.tile(np.arange(NK) + (-NK // 2), PAIRS0)

    def rep(v):
        return np.broadcast_to(np.asarray(v).reshape(1, -1), (P, np.asarray(v).size))

    def cols(v):
        v = np.asarray(v).reshape(C, P, -1)
        return v.transpose(1, 0, 2).reshape(P, -1)

    boff = np.asarray(a["L0_xattn_boff"]).reshape(PAIRS0, 2, NK).transpose(1, 0, 2).reshape(2, PK)
    parts = dict(
        ident=np.eye(P), mask8=(part[:, None] // HD0 == np.arange(8)[None]) * 0.125,
        mask2=((part[:, None] % 32) // HD0 == np.arange(2)[None]), same=(part[:, None] // S == part[None] // S),
        iota=rep(near), iota_all=rep(np.where(rows < M, rows, 1 << 20)), ref=rep(ref), loc=loc,
        boff=np.repeat(boff, S, axis=0), bq=cols(a["L0_xattn_bq"]), bk=cols(a["L0_xattn_bk"]),
        ls=rep(a["L0_attn_layerscale"]), rscale=cols(a["L0_ffn_router_scale"]), pes=rep(a["L0_ffn_per_expert_scale"]),
        rw0=cols(a["L0_ffn_router_w"]), convw=cols(a["L1_attn_conv_w"]), convb=cols(a["L1_attn_conv_b"]),
        alog=cols(a["L1_attn_A_log"]), dpar=cols(a["L1_attn_D_param"]),
        rw1=cols(np.asarray(a["L1_ffn_router_w"]).T), rb1=rep(a["L1_ffn_router_bias"]),
    )
    assert list(parts) == list(SMALL) and all(v.shape == (P, SMALL[n][1]) for n, v in parts.items())
    return np.concatenate([np.asarray(v, dtype=np.float32) for v in parts.values()], axis=1)


def _laid_out(np, a):
    def chunks(w):
        w = np.asarray(w)
        return w.reshape(w.shape[0] // P, P, -1).transpose(1, 0, 2)

    ctx = np.asarray(a["ctx_1024"])
    ctx_t = np.zeros((NB, P, C, MPAD), ctx.dtype)
    ctx_t[..., :M] = ctx.transpose(0, 2, 1).reshape(NB, C, P, M).transpose(0, 2, 1, 3)
    ctx_n = np.zeros((NB, NBLK, P, D), ctx.dtype)
    ctx_n[:, 0, :TXT] = ctx[:, :TXT]
    ctx_n[:, 1:, :IBLK] = ctx[:, TXT:].reshape(NB, IB, IBLK, D)
    woff = np.asarray(a["L0_xattn_Woff"]).reshape(PAIRS0, 2, NK, D).transpose(1, 0, 2, 3).reshape(2 * PK, D)
    up0 = np.asarray(a["L0_ffn_gating_w"]).reshape(E0, 2 * HID, C, P)
    up1 = np.stack([np.asarray(a["L1_ffn_gate_w"]).reshape(GROUPS, HID, D),
                    np.asarray(a["L1_ffn_up_w"]).reshape(GROUPS, HID, D)], axis=1)
    shared = np.stack([np.asarray(a["L1_ffn_sgate_w"]), np.asarray(a["L1_ffn_sup_w"])])[None]
    up1 = np.concatenate([up1, shared], axis=0).reshape(GROUPS + 1, 2 * HID, C, P)
    down1 = np.asarray(a["L1_ffn_down_w"]).reshape(GROUPS, HC, D, P).transpose(0, 3, 1, 2)
    sdown = np.asarray(a["L1_ffn_sdown_w"]).T.reshape(1, HC, P, D).transpose(0, 2, 1, 3)
    laid = dict(
        x=np.asarray(a["x"]).reshape(T, D), mask=a["mask_BxS2_if0"], small=_small_arrays(np, a),
        rows=np.stack([np.asarray(a[n]) for n in ("L0_xattn_bv", "L0_xattn_bo", "L0_attn_bq", "L0_attn_bk",
                                                  "L0_attn_bv", "L0_attn_bo", "L1_xattn_bo")])[None],
        ctx_t=ctx_t, ctx_n=ctx_n.transpose(0, 2, 1, 3),
        wq0=chunks(np.asarray(a["L0_xattn_Wq"]).T), wk0=chunks(np.asarray(a["L0_xattn_Wk"]).T),
        wv0=chunks(np.asarray(a["L0_xattn_Wv"]).T), wo0=chunks(np.asarray(a["L0_xattn_Wo"]).T),
        woff0=chunks(woff.T).reshape(P, C, 2, PK),
        wqa=chunks(np.asarray(a["L0_attn_Wq"]).T), wka=chunks(np.asarray(a["L0_attn_Wk"]).T),
        wva=chunks(np.asarray(a["L0_attn_Wv"]).T), woa=chunks(np.asarray(a["L0_attn_Wo"]).T),
        up0=up0.transpose(0, 3, 2, 1), down0=np.asarray(a["L0_ffn_linear_w"]).reshape(E0, HC, P, D).transpose(0, 2, 1, 3),
        wq1=chunks(a["L1_xattn_Wq"]),
        wk1=np.stack([chunks(np.asarray(a[n]).T) for n in ("L1_xattn_Wk", "L1_xattn_Wk_ip")], axis=1),
        wv1=np.stack([chunks(a[n]) for n in ("L1_xattn_Wv", "L1_xattn_Wv_ip")], axis=1),
        wo1=chunks(a["L1_xattn_Wo"]),
        win=chunks(np.asarray(a["L1_attn_in_proj_w"]).T), wpar=chunks(np.asarray(a["L1_attn_x_proj_w"]).T),
        wout=chunks(np.asarray(a["L1_attn_out_proj_w"]).T),
        up1=up1.transpose(0, 3, 2, 1), down1=np.concatenate([down1, sdown], axis=0),
    )
    return {n: np.ascontiguousarray(v) for n, v in laid.items()}


def kernel(**inputs):
    import numpy as np
    import concourse.bacc as bacc
    from concourse.bass_utils import run_bass_kernel_spmd

    nc = bacc.Bacc("TRN2", target_bir_lowering=False, num_devices=1)
    laid = _laid_out(np, inputs)
    arrays = {f"in_{n}": v for n, v in laid.items()}
    aps = {n: nc.dram_tensor(f"in_{n}", v.shape, mybir.dt.from_np(v.dtype), kind="ExternalInput").ap()
           for n, v in laid.items()}
    out = nc.dram_tensor("out_x", (T, D), F32, kind="ExternalOutput").ap()
    perceiver_program(nc, aps, out)
    r = run_bass_kernel_spmd(nc, [arrays], core_ids=[0])
    return r.results[0]["out_x"].reshape(NB, S, D)
```

```python
import math
from contextlib import ExitStack

import concourse.bass as bass
from concourse import mybir

ALU = mybir.AluOpType
ACT = mybir.ActivationFunctionType
F32 = mybir.dt.float32
F32R = mybir.dt.float32r
I32 = mybir.dt.int32
AX = mybir.AxisListType.X
BANK = 512

P = 128
D = 256
C = D // P
NB, S = 16, 64
T = NB * S
NT = T // P
M = 1601
EPS = 1e-5

H0, HD0, NK = 16, 16, 5
PAIRS0 = H0 // 2
PK = PAIRS0 * NK
LOW, HIGH = 96, 1569
WN = LOW + M - HIGH
NWIN = 13
MPAD = NWIN * WN
assert WN == P

E0, HID = 8, 512
HC = HID // P

H1, HD1, TXT = 16, 64, 77
PAIRS1 = H1 // 2
INNER = H1 * HD1
IMG = M - TXT
IB, IBLK = 12, 127
SB, SBLK = 3, 508
assert IB * IBLK == IMG and SB * SBLK == IMG
NBLK = IB + 1

NS, KC = 16, 4
NPAR = 2 * NS + 1

E1, TOP1 = 32, 4
GROUPS = E1 // HC

SMALL = {}
_at = 0
for _name, _n in (
    ("ident", P), ("mask8", 8), ("mask2", 2), ("ref", PK), ("loc", 1),
    ("boff", PK), ("bq", C), ("bk", C), ("rscale", C), ("pes", E0), ("rw0", C * E0),
    ("convw", C * KC), ("convb", C), ("alog", C * NS), ("dpar", C), ("rw1", C * E1), ("rb1", E1),
):
    SMALL[_name] = (_at, _n)
    _at += _n
SMALL_N = _at
EARLY = {"same": (0, P), "iota": (P, WN), "ls": (P + WN, D)}
EARLY_N = P + WN + D
ROWS = {n: i for i, n in enumerate(("bv0", "bo0", "bqa", "bka", "bva", "boa"))}


class Chip:
    pass


def broadcast(ap, dim, n):
    return ap.unsqueeze(dim).broadcast(dim, n)


def small(k, name):
    a, n = SMALL[name] if name in SMALL else EARLY[name]
    return (k.small if name in SMALL else k.early)[:, a:a + n]


def clear_semaphores(nc, eng):
    ended = sorted(nc.released_uncleared_semaphores)
    first = 0
    for j in range(1, len(ended) + 1):
        if j == len(ended) or ended[j] != ended[j - 1] + 1:
            eng.sem_clear(range(ended[first], ended[j - 1] + 1))
            first = j


def norm_stage(nc, k, tag, clear=False):
    with ExitStack() as ctx:
        stats = ctx.enter_context(nc.sbuf_tensor(f"stats_{tag}", [P, NT, 6], F32))
        moments = ctx.enter_context(nc.sbuf_tensor(f"moments_{tag}", [P, NT, 2], F32))
        var_eps = ctx.enter_context(nc.sbuf_tensor(f"var_eps_{tag}", [P, NT], F32))
        rstd = ctx.enter_context(nc.sbuf_tensor(f"rstd_{tag}", [P, NT], F32))
        xn = ctx.enter_context(nc.sbuf_tensor(f"xn_{tag}", [P, NT, D], F32))
        turned = ctx.enter_context(nc.psum_tensor(f"turned_{tag}", [P, NT, BANK], F32))
        stats_done = ctx.enter_context(nc.semaphore(f"stats_done_{tag}"))
        moments_done = ctx.enter_context(nc.semaphore(f"moments_done_{tag}"))
        eps_added = ctx.enter_context(nc.semaphore(f"eps_added_{tag}"))
        rstd_done = ctx.enter_context(nc.semaphore(f"rstd_done_{tag}"))
        normed = ctx.enter_context(nc.semaphore(f"normed_{tag}"))
        tile_turned = ctx.enter_context(nc.semaphore(f"tile_turned_{tag}"))
        block = ctx.enter_context(nc.Block())

        if clear:
            @block.sync
            def _(sp):
                clear_semaphores(nc, sp)

        @block.vector
        def _(dve):
            for t in range(NT):
                nc.vector.bn_stats(stats[:, t, :], k.x[:, t, :]).then_inc(stats_done, 1)
            for t in range(NT):
                dve.wait_ge(stats_done, t + 1)
                nc.vector.bn_aggr(moments[:, t, :], stats[:, t, :]).then_inc(moments_done, 1)
            dve.wait_ge(moments_done, NT)
            nc.vector.tensor_scalar(var_eps[:], moments[:, :, 1], EPS, None, ALU.add).then_inc(eps_added, 1)
            dve.wait_ge(rstd_done, 1)
            for t in range(NT):
                nc.vector.tensor_scalar(xn[:, t, :], k.x[:, t, :], moments[:, t, 0:1], rstd[:, t:t + 1],
                                        ALU.subtract, ALU.mult).then_inc(normed, 1)

        @block.gpsimd
        def _(pool):
            pool.wait_ge(eps_added, 1)
            nc.gpsimd.tensor_tensor(rstd[:], var_eps[:], k.minus_half[:, 0:1].broadcast_to([P, NT]),
                                    ALU.pow).then_inc(rstd_done, 1)

        @block.tensor
        def _(pe):
            for t in range(NT):
                pe.wait_ge(normed, t + 1)
                for c in range(C):
                    last = nc.tensor.transpose(turned[:, t, c * P:(c + 1) * P], xn[:, t, c * P:(c + 1) * P], k.ident)
                last.then_inc(tile_turned, 1)

        @block.scalar
        def _(act):
            for t in range(NT):
                act.wait_ge(tile_turned, t + 1)
                nc.scalar.activation(k.h_t[:, :, t * P:(t + 1) * P],
                                     turned[:, t, 0:D].rearrange("p (c n) -> p c n", c=C), ACT.Copy)


def load_stage(nc, k, src):
    with ExitStack() as ctx:
        mask_i = ctx.enter_context(nc.sbuf_tensor("mask_i", [NB, M], I32))
        unmasked = ctx.enter_context(nc.sbuf_tensor("unmasked", [NB, M], F32))
        count = ctx.enter_context(nc.sbuf_tensor("count", [NB, 1], F32))
        last_pos = ctx.enter_context(nc.sbuf_tensor("last_pos", [NB, 1], F32))
        diag = ctx.enter_context(nc.sbuf_tensor("diag", [NB, NB], F32))
        spread = ctx.enter_context(nc.psum_tensor("spread", [P, NB], F32))
        mask_in = ctx.enter_context(nc.semaphore("mask_in"))
        small_in = ctx.enter_context(nc.semaphore("small_in"))
        rest_in = ctx.enter_context(nc.semaphore("rest_in"))
        consts_set = ctx.enter_context(nc.semaphore("consts_set"))
        len_step = ctx.enter_context(nc.semaphore("len_step"))
        len_spread = ctx.enter_context(nc.semaphore("len_spread"))
        block = ctx.enter_context(nc.Block())

        @block.sync
        def _(sp):
            sp.dma_start(mask_i[:], src["mask"]).then_inc(mask_in, 16)
            sp.dma_start(k.small[:], src["small"]).then_inc(small_in, 16)
            sp.dma_start(k.x[:], src["x"].rearrange("(t p) d -> p t d", p=P)).then_inc(rest_in, 16)
            sp.dma_start(k.rows[:], src["rows"]).then_inc(rest_in, 16)
            sp.dma_start(k.iota_all[:], src["iota_all"]).then_inc(rest_in, 16)
            sp.dma_start(k.early[:], src["early"]).then_inc(rest_in, 16)
            sp.dma_start(k.bo1[:], src["bo1"]).then_inc(rest_in, 16)
            sp.wait_ge(rest_in, 80)

        @block.vector
        def _(dve):
            nc.vector.memset(k.minus_half[:], -0.5)
            nc.vector.memset(k.ones[:], 1.0).then_inc(consts_set, 1)
            nc.vector.memset(k.log_s[:], -math.log(S))
            dve.wait_ge(mask_in, 16)
            nc.vector.tensor_scalar(unmasked[:], mask_i[:], -1.0, 1.0, ALU.mult, ALU.add).then_inc(len_step, 1)
            dve.wait_ge(len_step, 1)
            nc.vector.tensor_reduce(count[:], unmasked[:], AX, ALU.add).then_inc(len_step, 1)
            dve.wait_ge(len_step, 2)
            nc.vector.tensor_scalar(last_pos[:], count[:], -1.0, None, ALU.add).then_inc(len_step, 1)
            dve.wait_ge(len_step, 3)
            dve.wait_ge(small_in, 16)
            nc.vector.tensor_scalar(diag[:], k.ident[0:NB, 0:NB], last_pos[:, 0:1], None,
                                    ALU.mult).then_inc(len_step, 1)
            dve.wait_ge(len_spread, 1)
            nc.vector.tensor_copy(k.length[:], spread[:])

        @block.tensor
        def _(pe):
            pe.wait_ge(len_step, 4)
            pe.wait_ge(consts_set, 1)
            nc.tensor.matmul(spread[:], k.ones[0:NB, :], diag[:], start=True, stop=True).then_inc(len_spread, 1)


def positions_stage(nc, k, src):

    with ExitStack() as ctx:
        def sb(name, shape, dt=F32):
            return ctx.enter_context(nc.sbuf_tensor(name, shape, dt))

        def sem(name):
            return ctx.enter_context(nc.semaphore(name))

        wq = sb("wq0", [P, C, D])
        woff = sb("woff0", [P, C, 2, PK])
        v = sb("where", [P, NB, PK])
        turns = sb("turns", [P, NB, PK])
        side = sb("side", [P, NB, PK])
        per_len = sb("per_len", [P, NB])
        far = sb("far", [P, NB * PK])
        far_any = sb("far_any", [P, 1])
        q_ps = ctx.enter_context(nc.psum_tensor("q_ps", [P, C, 2, 512], F32))
        off_ps = ctx.enter_context(nc.psum_tensor("off_ps", [P, 2, 512], F32))
        flag_ps = ctx.enter_context(nc.psum_tensor("flag_ps", [1, 1], F32))
        wq_in = sem("wq0_in")
        woff_in = sem("woff0_in")
        q_done = sem("q0_done")
        q_kept = sem("q0_kept")
        off_done = sem("off_done")
        step = sem("where_step")
        side_done = sem("row_step")
        flag_summed = sem("flag_summed")
        block = ctx.enter_context(nc.Block())

        @block.sync
        def _(sp):
            sp.dma_start(wq[:], src["wq0"]).then_inc(wq_in, 16)
            sp.dma_start(woff[:], src["woff0"]).then_inc(woff_in, 16)

        @block.tensor
        def _(pe):
            pe.wait_ge(wq_in, 16)
            for e in range(C):
                for g in range(2):
                    for c in range(C):
                        last = nc.tensor.matmul(q_ps[:, e, g, :], wq[:, c, e * P:(e + 1) * P],
                                                k.h_t[:, c, g * 512:(g + 1) * 512], start=c == 0, stop=c == C - 1)
                    last.then_inc(q_done, 1)
            pe.wait_ge(woff_in, 16)
            pe.wait_ge(q_kept, 4)
            for b in range(NB):
                for r in range(2):
                    for c in range(C):
                        last = nc.tensor.matmul(
                            off_ps[r * S:(r + 1) * S, b // 8, (b % 8) * PK:(b % 8 + 1) * PK],
                            k.q0[:, c, b * S:(b + 1) * S], woff[:, c, r, :], start=c == 0, stop=c == C - 1)
            last.then_inc(off_done, 1)
            pe.wait_ge(step, 13)
            nc.tensor.matmul(flag_ps[:], far_any[:], k.ones[:, 0:1], start=True, stop=True).then_inc(flag_summed, 1)

        @block.scalar
        def _(act):
            for e in range(C):
                for g in range(2):
                    act.wait_ge(q_done, 2 * e + g + 1)
                    nc.scalar.activation(k.q0[:, e, g * 512:(g + 1) * 512], q_ps[:, e, g, :], ACT.Identity,
                                         bias=small(k, "bq")[:, e:e + 1]).then_inc(q_kept, 1)

        @block.vector
        def _(dve):
            def rep(ap):
                return ap.unsqueeze(1).broadcast_to([P, NB, PK])

            def by_batch(ap):
                return ap.unsqueeze(2).broadcast_to([P, NB, PK])

            length = by_batch(k.length[:])
            nc.vector.memset(k.pos[:, NB:NB + 1, :], 0.0)
            nc.vector.reciprocal(per_len[:], k.length[:])
            dve.wait_ge(off_done, 1)
            nc.vector.tensor_tensor(v[:].rearrange("p (a b) n -> p a b n", a=2),
                                    off_ps[:, :, 0:8 * PK].rearrange("p a (b n) -> p a b n", n=PK),
                                    rep(small(k, "boff")).rearrange("p (a b) n -> p a b n", a=2),
                                    ALU.add).then_inc(step, 1)
            dve.wait_ge(step, 1)
            nc.vector.tensor_tensor(v[:], v[:], rep(small(k, "ref")), ALU.add).then_inc(step, 1)
            dve.wait_ge(step, 2)
            nc.vector.tensor_scalar(v[:], v[:], small(k, "loc"), None, ALU.add).then_inc(step, 1)
            dve.wait_ge(step, 3)
            nc.vector.tensor_tensor(turns[:], v[:], by_batch(per_len[:]), ALU.mult).then_inc(step, 1)
            dve.wait_ge(step, 4)
            big = 1.5 * 2.0 ** 23
            nc.vector.tensor_scalar(turns[:], turns[:], big, big, ALU.add, ALU.subtract).then_inc(step, 1)
            dve.wait_ge(step, 5)
            nc.vector.tensor_tensor(turns[:], turns[:], length, ALU.mult).then_inc(step, 1)
            dve.wait_ge(step, 6)
            nc.vector.tensor_tensor(v[:], v[:], turns[:], ALU.subtract).then_inc(step, 1)
            dve.wait_ge(step, 7)
            nc.vector.tensor_tensor(side[:], v[:], length, ALU.mult).then_inc(step, 1)
            dve.wait_ge(step, 8)
            nc.vector.scalar_tensor_tensor(out=side[:], in0=side[:], scalar=0.0, in1=length, op0=ALU.is_lt,
                                           op1=ALU.mult).then_inc(step, 1)
            dve.wait_ge(step, 9)
            nc.vector.tensor_tensor(v[:], v[:], side[:], ALU.add).then_inc(step, 1)
            dve.wait_ge(step, 10)
            nc.vector.tensor_scalar(v[:], v[:], 1.0 / (M - 1), 2.0, ALU.mult, ALU.mult).then_inc(step, 1)
            dve.wait_ge(step, 11)
            nc.vector.tensor_scalar(v[:], v[:], 1.0, 1.0, ALU.subtract, ALU.add).then_inc(step, 1)
            dve.wait_ge(step, 12)
            nc.vector.tensor_scalar(v[:], v[:], float(M), -1.0, ALU.mult, ALU.add).then_inc(side_done, 1)
            dve.wait_ge(side_done, 1)
            nc.vector.tensor_scalar(k.pos[:, 0:NB, :], v[:], 0.5, None, ALU.mult).then_inc(side_done, 1)
            dve.wait_ge(side_done, 2)
            flat = k.pos[:, 0:NB, :].rearrange("p b n -> p (b n)")
            nc.vector.tensor_scalar(far[:], flat, float(LOW - 1), None, ALU.is_gt).then_inc(side_done, 1)
            dve.wait_ge(side_done, 3)
            nc.vector.scalar_tensor_tensor(out=far[:], in0=flat, scalar=float(HIGH), in1=far[:], op0=ALU.is_lt,
                                           op1=ALU.mult).then_inc(side_done, 1)
            dve.wait_ge(side_done, 4)
            nc.vector.tensor_reduce(far_any[:], far[:], AX, ALU.add).then_inc(step, 1)
            dve.wait_ge(flag_summed, 1)
            nc.vector.tensor_copy(k.far_count[:], flag_ps[:])




def near_attention(nc, k, src, ctx):
    def sb(name, shape, dt=F32):
        return ctx.enter_context(nc.sbuf_tensor(name, shape, dt))

    def ps(name, shape):
        return ctx.enter_context(nc.psum_tensor(name, shape, F32))

    def sem(name):
        return ctx.enter_context(nc.semaphore(name))

    wk, wv = sb("wk0", [P, C, D]), sb("wv0", [P, C, D])
    win = [sb(f"win{s}", [P, C, WN]) for s in range(2)]
    kt = [sb(f"kt{s}", [P, C, WN]) for s in range(2)]
    vals = [sb(f"vals{s}", [P, D]) for s in range(2)]
    qblk = [sb(f"qblk{s}", [P, C, 8, S]) for s in range(2)]
    tent = [sb(f"tent{s}", [P, PK, WN]) for s in range(2)]
    hit = sb("hit", [P, PK, WN])
    share = sb("share", [P, PK, WN])
    turned = sb("turned0", [P, 2, 512])
    score = sb("score", [P, PK])
    top = sb("top0", [P, PAIRS0])
    shifted = sb("shifted", [P, PK])
    weight = sb("weight", [P, PK])
    total = sb("total0", [P, PAIRS0])
    inv = sb("inv0", [P, PAIRS0])
    attn = sb("attn0", [P, PK])
    kept = sb("kept", [P, C, 2, S])
    kv_ps = ps("kv_ps", [P, 512])
    s_ps = ps("s_ps", [P, 2, 512])
    w_ps = ps("w_ps", [P, 2, 512])
    o_ps = ps("o_ps", [P, C, P])
    w_in = sem("wkv0_in")
    win_in = [sem(f"win_in{s}") for s in range(2)]
    kv_done, kv_kept, q_masked = sem("kv_done"), sem("kv_kept"), sem("q_masked")
    scored, dist_done, dist_abs, tent_done = sem("scored"), sem("dist_done"), sem("dist_abs"), sem("tent_done")
    hit_done, soft = sem("hit_done"), sem("soft_step")
    shift_done, exp_done = sem("shift_done"), sem("exp_done")
    share_done, turned_done, turned_kept = sem("share_done"), sem("turned_done"), sem("turned_kept")
    out_done, out_masked, out_kept = sem("out_done"), sem("out_masked"), sem("out_kept")
    SOFT = 5
    HALVES = NB // 2
    block = ctx.enter_context(nc.Block())

    def pairs_of_batches(eng, body):
        body(0, True, False)
        with eng.Fori(1, HALVES - 1) as i:
            body(i, False, False)
        body(HALVES - 1, False, True)

    @block.sync
    def _(sp):
        def load(b, s):
            ctx_b = src["ctx_t"][b]
            sp.dma_start(win[s][:, :, 0:LOW], ctx_b[:, :, 0:LOW]).then_inc(win_in[s], 16)
            sp.dma_start(win[s][:, :, LOW:WN], ctx_b[:, :, HIGH:M]).then_inc(win_in[s], 16)

        sp.dma_start(wk[:], src["wk0"]).then_inc(w_in, 16)
        sp.dma_start(wv[:], src["wv0"]).then_inc(w_in, 16)
        load(0, 0)
        load(1, 1)
        with sp.Fori(0, HALVES - 1) as i:
            for s in range(2):
                sp.wait_ge(kv_done, i * 2 + (s + 1))
                load(i * 2 + (s + 2), s)

    @block.tensor
    def _(pe):
        def keys_values(b, s, i):
            pe.wait_ge(win_in[s], i * 32 + 32)
            pe.wait_ge(kv_kept, b)
            for e in range(C):
                for c in range(C):
                    nc.tensor.matmul(kv_ps[:, e * WN:(e + 1) * WN], wk[:, c, e * P:(e + 1) * P], win[s][:, c, :],
                                     start=c == 0, stop=c == C - 1)
            for c in range(C):
                nc.tensor.matmul(kv_ps[:, C * WN:C * WN + D], win[s][:, c, :], wv[:, c, :], start=c == 0, stop=False)
            nc.tensor.matmul(kv_ps[:, C * WN:C * WN + D], k.ones[0:1, :], k.row("bv0"), start=False,
                             stop=True).then_inc(kv_done, 1)

        def scores(b, s):
            pe.wait_ge(kv_kept, b + 1)
            pe.wait_ge(q_masked, b + 1)
            pe.wait_ge(hit_done, b)
            for p in range(PAIRS0):
                c, j = divmod(p, 4)
                last = nc.tensor.matmul(s_ps[:, c, j * WN:(j + 1) * WN],
                                        qblk[s][:, c, 2 * j:2 * j + 2, :].rearrange("p h q -> p (h q)"),
                                        kt[s][:, c, :], start=True, stop=True)
            last.then_inc(scored, 1)

        def turn_shares(b, h, skip_wait):
            pe.wait_ge(share_done, b * 2 + (h + 1))
            if not skip_wait:
                pe.wait_ge(turned_kept, b * 2 + (h - 1))
            for j in range(4):
                for n in range(NK):
                    last = nc.tensor.matmul(w_ps[:, h, j * P:(j + 1) * P], share[:, (4 * h + j) * NK + n, :],
                                            k.ident, start=n == 0, stop=n == NK - 1)
            last.then_inc(turned_done, 1)

        def outputs(b, s):
            pe.wait_ge(out_masked, b)
            for p in range(PAIRS0):
                c, j = divmod(p, 4)
                if j == 0:
                    pe.wait_ge(turned_kept, b * 2 + (c + 1))
                last = nc.tensor.matmul(o_ps[32 * j:32 * j + 32, c, :], vals[s][:, 32 * p:32 * p + 32],
                                        turned[:, c, j * P:(j + 1) * P], start=True, stop=True)
            last.then_inc(out_done, 1)

        pe.wait_ge(w_in, 32)
        keys_values(0, 0, 0)
        scores(0, 0)

        def body(i, first, last):
            for s in range(2):
                b = i * 2 + s
                if not (last and s == 1):
                    keys_values(b + 1, 1 - s, i + s)
                    scores(b + 1, 1 - s)
                for h in range(2):
                    turn_shares(b, h, first and s == 0)
                outputs(b, s)

        pairs_of_batches(pe, body)

    @block.gpsimd
    def _(pool):
        def prepare(b, s, old):
            if old is not None:
                pool.wait_ge(scored, old)
            nc.gpsimd.tensor_tensor(
                qblk[s][:], k.q0[:, :, bass.ds(b * S, S)].unsqueeze(2).broadcast_to([P, C, 8, S]),
                small(k, "mask8").unsqueeze(1).unsqueeze(3).broadcast_to([P, C, 8, S]), ALU.mult).then_inc(q_masked, 1)
            if old is not None:
                pool.wait_ge(share_done, old * 2)
            nc.gpsimd.tensor_tensor(
                tent[s][:], small(k, "iota").unsqueeze(1).broadcast_to([P, PK, WN]),
                k.pos[:, bass.ds(b, 1), :].rearrange("p b n -> p (b n)").unsqueeze(2).broadcast_to([P, PK, WN]),
                ALU.subtract).then_inc(dist_done, 1)

        prepare(0, 0, None)

        def body(i, first, last):
            for s in range(2):
                b = i * 2 + s
                if not (last and s == 1):
                    prepare(b + 1, 1 - s, None if first and s == 0 else b)

        pairs_of_batches(pool, body)

    @block.scalar
    def _(act):
        def make_tent(b, s):
            act.wait_ge(dist_done, b + 1)
            nc.scalar.activation(tent[s][:], tent[s][:], ACT.Abs).then_inc(dist_abs, 1)
            act.wait_ge(dist_abs, b + 1)
            nc.scalar.activation(tent[s][:], tent[s][:], ACT.Relu, bias=1.0, scale=-1.0).then_inc(tent_done, 1)

        def keep_keys_values(b, s):
            act.wait_ge(kv_done, b + 1)
            for c in range(C):
                nc.scalar.activation(kt[s][:, c, :], kv_ps[:, c * WN:(c + 1) * WN], ACT.Identity,
                                     bias=small(k, "bk")[:, c:c + 1])
            nc.scalar.activation(vals[s][:], kv_ps[:, C * WN:C * WN + D], ACT.Copy).then_inc(kv_kept, 1)

        keep_keys_values(0, 0)
        make_tent(0, 0)

        def body(i, first, last):
            for s in range(2):
                b = i * 2 + s
                if not (last and s == 1):
                    keep_keys_values(b + 1, 1 - s)
                    make_tent(b + 1, 1 - s)
                act.wait_ge(shift_done, b + 1)
                nc.scalar.activation(weight[:], shifted[:], ACT.Exp).then_inc(exp_done, 1)
                for h in range(2):
                    act.wait_ge(turned_done, b * 2 + (h + 1))
                    nc.scalar.activation(turned[:, h, :], w_ps[:, h, :], ACT.Copy).then_inc(turned_kept, 1)

        pairs_of_batches(act, body)

    @block.vector
    def _(dve):
        def keep_outputs(b):
            dve.wait_ge(out_done, b + 1)
            nc.vector.tensor_tensor(
                kept[:], o_ps[:].rearrange("p c (r q) -> p c r q", r=2),
                small(k, "mask2").unsqueeze(1).unsqueeze(3).broadcast_to([P, C, 2, S]),
                ALU.mult).then_inc(out_masked, 1)
            dve.wait_ge(out_masked, b + 1)
            nc.vector.tensor_tensor(k.ctx_t[:, :, bass.ds(b * S, S)], kept[:, :, 0, :], kept[:, :, 1, :],
                                    ALU.add).then_inc(out_kept, 1)

        def by_pair(ap):
            return ap.unsqueeze(2).broadcast_to([P, PAIRS0, NK])

        def paired(t):
            return t[:].rearrange("p (a n) -> p a n", n=NK)

        def body(i, first, last):
            for s in range(2):
                b = i * 2 + s
                at = b * SOFT
                dve.wait_ge(tent_done, b + 1)
                dve.wait_ge(scored, b + 1)
                nc.vector.tensor_tensor(
                    hit[:].rearrange("p (a n) m -> p a n m", n=NK), tent[s][:].rearrange("p (a n) m -> p a n m", n=NK),
                    s_ps[:].rearrange("p c (j m) -> p (c j) m", m=WN).unsqueeze(2).broadcast_to([P, PAIRS0, NK, WN]),
                    ALU.mult).then_inc(hit_done, 1)
                dve.wait_ge(hit_done, b + 1)
                nc.vector.tensor_reduce(score[:], hit[:], AX, ALU.add).then_inc(soft, 1)
                if not (first and s == 0):
                    keep_outputs(b - 1)
                dve.wait_ge(soft, at + 1)
                nc.vector.tensor_reduce(top[:], paired(score), AX, ALU.max).then_inc(soft, 1)
                dve.wait_ge(soft, at + 2)
                nc.vector.tensor_tensor(paired(shifted), paired(score), by_pair(top[:]),
                                        ALU.subtract).then_inc(shift_done, 1)
                dve.wait_ge(exp_done, b + 1)
                nc.vector.tensor_reduce(total[:], paired(weight), AX, ALU.add).then_inc(soft, 1)
                dve.wait_ge(soft, at + 3)
                nc.vector.reciprocal(inv[:], total[:]).then_inc(soft, 1)
                dve.wait_ge(soft, at + 4)
                nc.vector.scalar_tensor_tensor(out=paired(attn), in0=paired(weight), scalar=0.5, in1=by_pair(inv[:]),
                                               op0=ALU.mult, op1=ALU.mult).then_inc(soft, 1)
                dve.wait_ge(soft, at + 5)
                for h in range(2):
                    n = PK // 2
                    if not (first and s == 0):
                        dve.wait_ge(turned_done, b * 2 + (h - 1))
                    nc.vector.tensor_tensor(share[:, h * n:(h + 1) * n, :], tent[s][:, h * n:(h + 1) * n, :],
                                            attn[:, h * n:(h + 1) * n].unsqueeze(2).broadcast_to([P, n, WN]),
                                            ALU.mult).then_inc(share_done, 1)

        pairs_of_batches(dve, body)
        keep_outputs(NB - 1)


def far_attention(nc, k, src):
    with ExitStack() as ctx:
        def sb(name, shape, dt=F32):
            return ctx.enter_context(nc.sbuf_tensor(f"far_{name}", shape, dt))

        def ps(name, shape):
            return ctx.enter_context(nc.psum_tensor(f"far_{name}", shape, F32))

        def sem(name):
            return ctx.enter_context(nc.semaphore(f"far_{name}"))

        wk, wv = sb("wk", [P, C, D]), sb("wv", [P, C, D])
        win, win2 = sb("win", [P, C, WN]), sb("win2", [P, C, WN])
        kt, vals = sb("kt", [P, C, WN]), sb("vals", [P, D])
        qblk = sb("qblk", [P, C, 8, S])
        tent, hit = sb("tent", [P, PK, WN]), sb("hit", [P, PK, WN])
        tent2, share = sb("tent2", [P, PK, WN]), sb("share", [P, PK, WN])
        turned = sb("turned", [P, 2, 512])
        part, score, shifted, weight, attn = (sb(n, [P, PK]) for n in ("part", "score", "shifted", "weight", "attn"))
        top, total, inv = (sb(n, [P, PAIRS0]) for n in ("top", "total", "inv"))
        kept, out_part, out_sum = sb("kept", [P, C, 2, S]), sb("out_part", [P, C, S]), sb("out_sum", [P, C, S])
        k_ps, v_ps, s_ps = ps("k_ps", [P, C, WN]), ps("v_ps", [P, D]), ps("s_ps", [P, 2, BANK])
        w_ps, o_ps = ps("w_ps", [P, 2, BANK]), ps("o_ps", [P, C, P])
        w_in, win_in, win2_in = sem("w_in"), sem("win_in"), sem("win2_in")
        k_done, k_kept, q_masked, scored = sem("k_done"), sem("k_kept"), sem("q_masked"), sem("scored")
        dist, dist_abs, tent_done, hit_done = sem("dist"), sem("dist_abs"), sem("tent_done"), sem("hit_done")
        part_done, score_done, soft, shift, exp_done = (
            sem(n) for n in ("part_done", "score_done", "soft", "shift", "exp_done"))
        attn_done, v_done, v_kept, dist2, dist2_abs, tent2_done = (
            sem(n) for n in ("attn_done", "v_done", "v_kept", "dist2", "dist2_abs", "tent2_done"))
        share_done, turned_done, turned_kept, out_done, masked, out_step, out_added, batch_out = (
            sem(n) for n in ("share_done", "turned_done", "turned_kept", "out_done", "masked", "out_step",
                             "out_added", "batch_out"))
        block = ctx.enter_context(nc.Block())

        def windows(eng, b, body):
            with eng.Fori(0, NWIN) as j:
                body(j, b * NWIN + j)

        @block.sync
        def _(sp):
            sp.dma_start(wk[:], src["wk0"]).then_inc(w_in, 16)
            sp.dma_start(wv[:], src["wv0"]).then_inc(w_in, 16)
            with sp.Fori(0, NB) as b:
                def for_keys(j, n):
                    sp.wait_ge(k_done, n + 1)
                    sp.dma_start(win[:], src["ctx_t"][b][:, :, bass.ds(j * WN, WN)]).then_inc(win_in, 16)

                def for_values(j, n):
                    sp.wait_ge(v_done, n + 1)
                    sp.dma_start(win2[:], src["ctx_t"][b][:, :, bass.ds(j * WN, WN)]).then_inc(win2_in, 16)

                windows(sp, b, for_keys)
                windows(sp, b, for_values)

        @block.tensor
        def _(pe):
            for first in (k_done, scored, v_done, turned_done, out_done):
                pe.sem_inc(first, 1)
            pe.wait_ge(w_in, 32)
            with pe.Fori(0, NB) as b:
                def scores(j, n):
                    pe.wait_ge(win_in, n * 16 + 16)
                    for e in range(C):
                        for c in range(C):
                            last = nc.tensor.matmul(k_ps[:, e, :], wk[:, c, e * P:(e + 1) * P], win[:, c, :],
                                                    start=c == 0, stop=c == C - 1)
                    last.then_inc(k_done, 1)
                    pe.wait_ge(k_kept, n + 1)
                    pe.wait_ge(q_masked, b + 1)
                    pe.wait_ge(hit_done, n + 1)
                    for p in range(PAIRS0):
                        c, i = divmod(p, 4)
                        last = nc.tensor.matmul(s_ps[:, c, i * WN:(i + 1) * WN],
                                                qblk[:, c, 2 * i:2 * i + 2, :].rearrange("p h q -> p (h q)"),
                                                kt[:, c, :], start=True, stop=True)
                    last.then_inc(scored, 1)

                def outputs(j, n):
                    pe.wait_ge(win2_in, n * 16 + 16)
                    for c in range(C):
                        nc.tensor.matmul(v_ps[:], win2[:, c, :], wv[:, c, :], start=c == 0, stop=False)
                    nc.tensor.matmul(v_ps[:], k.ones[0:1, :], k.row("bv0"), start=False, stop=True).then_inc(v_done, 1)
                    pe.wait_ge(share_done, n + 2)
                    for p in range(PAIRS0):
                        for i in range(NK):
                            last = nc.tensor.matmul(w_ps[:, p // 4, (p % 4) * P:(p % 4 + 1) * P],
                                                    share[:, p * NK + i, :], k.ident, start=i == 0, stop=i == NK - 1)
                    last.then_inc(turned_done, 1)
                    pe.wait_ge(v_kept, n + 1)
                    pe.wait_ge(turned_kept, n + 1)
                    pe.wait_ge(masked, n + 1)
                    for p in range(PAIRS0):
                        c, i = divmod(p, 4)
                        last = nc.tensor.matmul(o_ps[32 * i:32 * i + 32, c, :], vals[:, 32 * p:32 * p + 32],
                                                turned[:, c, i * P:(i + 1) * P], start=True, stop=True)
                    last.then_inc(out_done, 1)

                windows(pe, b, scores)
                windows(pe, b, outputs)

        @block.gpsimd
        def _(pool):
            with pool.Fori(0, NB) as b:
                def distances(out, j, done):
                    nc.gpsimd.tensor_tensor(
                        out[:], k.iota_all[:, bass.ds(j * WN, WN)].unsqueeze(1).broadcast_to([P, PK, WN]),
                        k.pos[:, bass.ds(b, 1), :].rearrange("p b n -> p (b n)").unsqueeze(2).broadcast_to([P, PK, WN]),
                        ALU.subtract).then_inc(done, 1)

                def for_scores(j, n):
                    pool.wait_ge(hit_done, n + 1)
                    distances(tent, j, dist)

                def for_outputs(j, n):
                    pool.wait_ge(share_done, n + 1)
                    distances(tent2, j, dist2)

                pool.wait_ge(scored, b * NWIN + 1)
                nc.gpsimd.tensor_tensor(
                    qblk[:], k.q0[:, :, bass.ds(b * S, S)].unsqueeze(2).broadcast_to([P, C, 8, S]),
                    small(k, "mask8").unsqueeze(1).unsqueeze(3).broadcast_to([P, C, 8, S]),
                    ALU.mult).then_inc(q_masked, 1)
                windows(pool, b, for_scores)
                windows(pool, b, for_outputs)

        @block.scalar
        def _(act):
            with act.Fori(0, NB) as b:
                def for_scores(j, n):
                    act.wait_ge(k_done, n + 2)
                    for c in range(C):
                        last = nc.scalar.activation(kt[:, c, :], k_ps[:, c, :], ACT.Identity,
                                                    bias=small(k, "bk")[:, c:c + 1])
                    last.then_inc(k_kept, 1)
                    act.wait_ge(dist, n + 1)
                    nc.scalar.activation(tent[:], tent[:], ACT.Abs).then_inc(dist_abs, 1)
                    act.wait_ge(dist_abs, n + 1)
                    nc.scalar.activation(tent[:], tent[:], ACT.Relu, bias=1.0, scale=-1.0).then_inc(tent_done, 1)

                def for_outputs(j, n):
                    act.wait_ge(v_done, n + 2)
                    act.wait_ge(out_done, n + 1)
                    nc.scalar.activation(vals[:], v_ps[:], ACT.Copy).then_inc(v_kept, 1)
                    act.wait_ge(dist2, n + 1)
                    nc.scalar.activation(tent2[:], tent2[:], ACT.Abs).then_inc(dist2_abs, 1)
                    act.wait_ge(dist2_abs, n + 1)
                    nc.scalar.activation(tent2[:], tent2[:], ACT.Relu, bias=1.0, scale=-1.0).then_inc(tent2_done, 1)
                    act.wait_ge(turned_done, n + 2)
                    nc.scalar.activation(turned[:], w_ps[:], ACT.Copy).then_inc(turned_kept, 1)

                windows(act, b, for_scores)
                act.wait_ge(shift, b + 1)
                nc.scalar.activation(weight[:], shifted[:], ACT.Exp).then_inc(exp_done, 1)
                windows(act, b, for_outputs)

        @block.vector
        def _(dve):
            def paired(t):
                return t[:].rearrange("p (a n) -> p a n", n=NK)

            def by_pair(t):
                return t[:].unsqueeze(2).broadcast_to([P, PAIRS0, NK])

            for first in (hit_done, part_done, share_done, masked):
                dve.sem_inc(first, 1)
            nc.vector.memset(score[:], 0.0).then_inc(score_done, 1)
            nc.vector.memset(out_sum[:], 0.0).then_inc(out_added, 1)
            with dve.Fori(0, NB) as b:
                def scores(j, n):
                    dve.wait_ge(tent_done, n + 1)
                    dve.wait_ge(scored, n + 2)
                    dve.wait_ge(part_done, n + 1)
                    nc.vector.tensor_tensor(
                        hit[:].rearrange("p (a n) m -> p a n m", n=NK), tent[:].rearrange("p (a n) m -> p a n m", n=NK),
                        s_ps[:].rearrange("p c (i m) -> p (c i) m", m=WN).unsqueeze(2).broadcast_to(
                            [P, PAIRS0, NK, WN]), ALU.mult).then_inc(hit_done, 1)
                    dve.wait_ge(hit_done, n + 2)
                    nc.vector.tensor_reduce(part[:], hit[:], AX, ALU.add).then_inc(part_done, 1)
                    dve.wait_ge(part_done, n + 2)
                    dve.wait_ge(score_done, n + (b + 1))
                    nc.vector.tensor_tensor(score[:], score[:], part[:], ALU.add).then_inc(score_done, 1)

                def outputs(j, n):
                    dve.wait_ge(soft, b * 5 + 4)
                    dve.wait_ge(tent2_done, n + 1)
                    dve.wait_ge(turned_done, n + 1)
                    nc.vector.tensor_tensor(share[:], tent2[:], attn[:].unsqueeze(2).broadcast_to([P, PK, WN]),
                                            ALU.mult).then_inc(share_done, 1)
                    dve.wait_ge(out_done, n + 2)
                    nc.vector.tensor_tensor(
                        kept[:], o_ps[:].rearrange("p c (r q) -> p c r q", r=2),
                        small(k, "mask2").unsqueeze(1).unsqueeze(3).broadcast_to([P, C, 2, S]),
                        ALU.mult).then_inc(masked, 1)
                    dve.wait_ge(masked, n + 2)
                    nc.vector.tensor_tensor(out_part[:], kept[:, :, 0, :], kept[:, :, 1, :],
                                            ALU.add).then_inc(out_step, 1)
                    dve.wait_ge(out_step, n + 1)
                    dve.wait_ge(out_added, n + (b + 1))
                    nc.vector.tensor_tensor(out_sum[:], out_sum[:], out_part[:], ALU.add).then_inc(out_added, 1)

                windows(dve, b, scores)
                at = b * 5
                dve.wait_ge(score_done, b * (NWIN + 1) + (NWIN + 1))
                nc.vector.tensor_reduce(top[:], paired(score), AX, ALU.max).then_inc(soft, 1)
                dve.wait_ge(soft, at + 1)
                nc.vector.tensor_tensor(paired(shifted), paired(score), by_pair(top), ALU.subtract).then_inc(shift, 1)
                dve.wait_ge(shift, b + 1)
                nc.vector.memset(score[:], 0.0).then_inc(score_done, 1)
                dve.wait_ge(exp_done, b + 1)
                nc.vector.tensor_reduce(total[:], paired(weight), AX, ALU.add).then_inc(soft, 1)
                dve.wait_ge(soft, at + 2)
                nc.vector.reciprocal(inv[:], total[:]).then_inc(soft, 1)
                dve.wait_ge(soft, at + 3)
                nc.vector.scalar_tensor_tensor(out=paired(attn), in0=paired(weight), scalar=0.5, in1=by_pair(inv),
                                               op0=ALU.mult, op1=ALU.mult).then_inc(soft, 1)
                windows(dve, b, outputs)
                dve.wait_ge(out_added, b * (NWIN + 1) + (NWIN + 1))
                nc.vector.tensor_copy(k.ctx_t[:, :, bass.ds(b * S, S)], out_sum[:]).then_inc(soft, 1)
                dve.wait_ge(soft, at + 5)
                nc.vector.memset(out_sum[:], 0.0).then_inc(out_added, 1)


def local_attention(nc, k, src):
    far = nc.values_load(k.far_count[0:1, 0:1], min_val=0, max_val=1 << 23)
    with nc.If(far < 1):
        with ExitStack() as ctx:
            near_attention(nc, k, src, ctx)
    with nc.Else():
        far_attention(nc, k, src)


def after_local(nc, k, src):
    with ExitStack() as ctx:
        wo = ctx.enter_context(nc.sbuf_tensor("wo0", [P, C, D], F32))
        y_ps = ctx.enter_context(nc.psum_tensor("y0_ps", [P, NT, BANK], F32))
        wo_in = ctx.enter_context(nc.semaphore("wo0_in"))
        y_done = ctx.enter_context(nc.semaphore("y0_done"))
        block = ctx.enter_context(nc.Block())

        @block.sync
        def _(sp):
            sp.dma_start(wo[:], src["wo0"]).then_inc(wo_in, 16)

        @block.tensor
        def _(pe):
            pe.wait_ge(wo_in, 16)
            for t in range(NT):
                for c in range(C):
                    nc.tensor.matmul(y_ps[:, t, 0:D], k.ctx_t[:, c, t * P:(t + 1) * P], wo[:, c, :],
                                     start=c == 0, stop=False)
                nc.tensor.matmul(y_ps[:, t, 0:D], k.ones[0:1, :], k.row("bo0"), start=False,
                                 stop=True).then_inc(y_done, 1)

        @block.vector
        def _(dve):
            for t in range(NT):
                dve.wait_ge(y_done, t + 1)
                nc.vector.tensor_tensor(k.x[:, t, :], k.x[:, t, :], y_ps[:, t, 0:D], ALU.add)


def store_stage(nc, k, out):
    with ExitStack() as ctx:
        stored = ctx.enter_context(nc.semaphore("stored"))
        block = ctx.enter_context(nc.Block())

        @block.sync
        def _(sp):
            sp.dma_start(out.rearrange("(t p) d -> p t d", p=P), k.x[:]).then_inc(stored, 16)
            sp.wait_ge(stored, 16)


def self_attention(nc, k, src):
    with ExitStack() as ctx:
        def sb(name, shape, dt=F32):
            return ctx.enter_context(nc.sbuf_tensor(name, shape, dt))

        def bank(name):
            return [ctx.enter_context(nc.psum_tensor(f"{name}{s}", [P, BANK], F32)) for s in range(2)]

        def sem(name):
            return ctx.enter_context(nc.semaphore(name))

        w = {n: sb(f"{n}a_w", [P, C, D]) for n in ("q", "k", "v", "o")}
        h = [sb(f"ha{s}", [P, C, P]) for s in range(2)]
        stats = [sb(f"stats_qk{s}", [P, 2, 6]) for s in range(2)]
        moments = [sb(f"moments_qk{s}", [P, 2, 2]) for s in range(2)]
        var_eps = [sb(f"var_eps_qk{s}", [P, 2]) for s in range(2)]
        rstd = [sb(f"rstd_qk{s}", [P, 2]) for s in range(2)]
        qkn = [sb(f"qkn{s}", [P, 2, D]) for s in range(2)]
        qkt = [sb(f"qkt{s}", [P, 2, C, P]) for s in range(2)]
        v = [sb(f"va{s}", [P, D]) for s in range(2)]
        attn = [sb(f"attn_a{s}", [P, P]) for s in range(2)]
        own = [sb(f"own{s}", [P, P]) for s in range(2)]
        ot = [sb(f"ot_a{s}", [P, C, P]) for s in range(2)]
        scaled = [sb(f"scaled{s}", [P, D]) for s in range(2)]
        spare = sb("spare", [P, 1])
        qk_ps, vy_ps, t_ps, s_ps = bank("qk_ps"), bank("vy_ps"), bank("t_ps"), bank("sa_ps")
        w_in = sem("wa_in")
        h_copied, qk_done, v_done = sem("h_copied"), sem("qk_done"), sem("va_done")
        stat, aggr, eps_added, rstd_done, normed = (sem(f"{n}_qk") for n in ("stat", "aggr", "eps", "rstd", "normed"))
        v_kept, qk_turned, qk_kept, scored = sem("va_kept"), sem("qk_turned"), sem("qk_kept"), sem("a_scored")
        gated, masked, o_done, o_kept = sem("a_gated"), sem("a_masked"), sem("a_o_done"), sem("a_o_kept")
        y_done, y_scaled, x_added = sem("a_y_done"), sem("a_y_scaled"), sem("a_x_added")
        block = ctx.enter_context(nc.Block())

        @block.sync
        def _(sp):
            for n, a in (("q", src["wqa"]), ("k", src["wka"]), ("v", src["wva"]), ("o", src["woa"])):
                sp.dma_start(w[n][:], a).then_inc(w_in, 16)

        @block.gpsimd
        def _(pool):
            with pool.Fori(0, NT // 2) as i:
                for s in range(2):
                    pool.wait_ge(x_added, i * 2 + 2)
                    nc.gpsimd.tensor_copy(h[s][:], k.h_t[:, :, bass.ds(i * 2 * P + s * P, P)]).then_inc(h_copied, 1)
                for s in range(2):
                    pool.wait_ge(eps_added, i * 2 + (s + 1))
                    nc.gpsimd.tensor_tensor(rstd[s][:], var_eps[s][:], k.minus_half[:, 0:1].broadcast_to([P, 2]),
                                            ALU.pow).then_inc(rstd_done, 1)

        @block.tensor
        def _(pe):
            pe.wait_ge(w_in, 64)
            with pe.Fori(0, NT // 2) as i:
                for s in range(2):
                    pe.wait_ge(h_copied, i * 2 + (s + 1))
                    for j, n in enumerate("qk"):
                        for c in range(C):
                            nc.tensor.matmul(qk_ps[s][:, j * D:(j + 1) * D], h[s][:, c, :], w[n][:, c, :],
                                             start=c == 0, stop=False)
                        last = nc.tensor.matmul(qk_ps[s][:, j * D:(j + 1) * D], k.ones[0:1, :], k.row(f"b{n}a"),
                                                start=False, stop=True)
                    last.then_inc(qk_done, 1)
                    for c in range(C):
                        nc.tensor.matmul(vy_ps[s][:, 0:D], h[s][:, c, :], w["v"][:, c, :], start=c == 0, stop=False)
                    nc.tensor.matmul(vy_ps[s][:, 0:D], k.ones[0:1, :], k.row("bva"), start=False,
                                     stop=True).then_inc(v_done, 1)
                for s in range(2):
                    pe.wait_ge(normed, i * 2 + (s + 1))
                    for j in range(2):
                        for c in range(C):
                            last = nc.tensor.transpose(t_ps[s][:, (j * C + c) * P:(j * C + c + 1) * P],
                                                       qkn[s][:, j, c * P:(c + 1) * P], k.ident)
                    last.then_inc(qk_turned, 1)
                for s in range(2):
                    pe.wait_ge(qk_kept, i * 2 + (s + 1))
                    for c in range(C):
                        last = nc.tensor.matmul(s_ps[s][:, 0:P], qkt[s][:, 1, c, :], qkt[s][:, 0, c, :],
                                                start=c == 0, stop=c == C - 1)
                    last.then_inc(scored, 1)
                for s in range(2):
                    pe.wait_ge(masked, i * 2 + (s + 1))
                    pe.wait_ge(v_kept, i * 2 + (s + 1))
                    for c in range(C):
                        last = nc.tensor.matmul(t_ps[s][:, c * P:(c + 1) * P], v[s][:, c * P:(c + 1) * P], own[s][:],
                                                start=True, stop=True)
                    last.then_inc(o_done, 1)
                for s in range(2):
                    pe.wait_ge(o_kept, i * 2 + (s + 1))
                    for c in range(C):
                        nc.tensor.matmul(vy_ps[s][:, 0:D], ot[s][:, c, :], w["o"][:, c, :], start=c == 0, stop=False)
                    nc.tensor.matmul(vy_ps[s][:, 0:D], k.ones[0:1, :], k.row("boa"), start=False,
                                     stop=True).then_inc(y_done, 1)

        @block.scalar
        def _(act):
            with act.Fori(0, NT // 2) as i:
                for s in range(2):
                    act.wait_ge(v_done, i * 2 + (s + 1))
                    nc.scalar.activation(v[s][:], vy_ps[s][:, 0:D], ACT.Copy).then_inc(v_kept, 1)
                for s in range(2):
                    act.wait_ge(qk_turned, i * 2 + (s + 1))
                    nc.scalar.activation(qkt[s][:].rearrange("p j c n -> p (j c n)"), t_ps[s][:],
                                         ACT.Copy).then_inc(qk_kept, 1)
                for s in range(2):
                    act.wait_ge(scored, i * 2 + (s + 1))
                    nc.scalar.activation(attn[s][:], s_ps[s][:, 0:P], ACT.Sigmoid, bias=k.log_s[:, 0:1],
                                         scale=1.0 / math.sqrt(D)).then_inc(gated, 1)
                for s in range(2):
                    act.wait_ge(o_done, i * 2 + (s + 1))
                    nc.scalar.activation(ot[s][:].rearrange("p c n -> p (c n)"), t_ps[s][:, 0:D],
                                         ACT.Copy).then_inc(o_kept, 1)

        @block.vector
        def _(dve):
            dve.sem_inc(x_added, 2)
            with dve.Fori(0, NT // 2) as i:
                for s in range(2):
                    dve.wait_ge(qk_done, i * 2 + (s + 1))
                    for j in range(2):
                        nc.vector.bn_stats(stats[s][:, j, :], qk_ps[s][:, j * D:(j + 1) * D]).then_inc(stat, 1)
                dve.wait_ge(stat, i * 4 + 4)
                nc.vector.memset(spare[:], 0.0)
                for s in range(2):
                    for j in range(2):
                        nc.vector.bn_aggr(moments[s][:, j, :], stats[s][:, j, :]).then_inc(aggr, 1)
                for s in range(2):
                    dve.wait_ge(aggr, i * 4 + (2 * s + 2))
                    nc.vector.tensor_scalar(var_eps[s][:], moments[s][:, :, 1], EPS, None,
                                            ALU.add).then_inc(eps_added, 1)
                for s in range(2):
                    dve.wait_ge(rstd_done, i * 2 + (s + 1))
                    for j in range(2):
                        last = nc.vector.tensor_scalar(qkn[s][:, j, :], qk_ps[s][:, j * D:(j + 1) * D],
                                                       moments[s][:, j, 0:1], rstd[s][:, j:j + 1],
                                                       ALU.subtract, ALU.mult)
                    last.then_inc(normed, 1)
                for s in range(2):
                    dve.wait_ge(gated, i * 2 + (s + 1))
                    nc.vector.tensor_tensor(own[s][:], attn[s][:], small(k, "same"), ALU.mult).then_inc(masked, 1)
                for s in range(2):
                    dve.wait_ge(y_done, i * 2 + (s + 1))
                    nc.vector.tensor_tensor(scaled[s][:], vy_ps[s][:, 0:D], small(k, "ls"),
                                            ALU.mult).then_inc(y_scaled, 1)
                for s in range(2):
                    dve.wait_ge(y_scaled, i * 2 + (s + 1))
                    xt = k.x[:, bass.ds(i * 2 + s, 1), :].rearrange("p a d -> p (a d)")
                    nc.vector.tensor_tensor(xt, xt, scaled[s][:], ALU.add).then_inc(x_added, 1)


def route(nc, k, layer):
    n, top_n = (E0, 2) if layer == 0 else (E1, TOP1)
    PAD, MARK = -1e30, 1e30
    with ExitStack() as ctx:
        def sb(name, shape, dt=F32):
            return ctx.enter_context(nc.sbuf_tensor(f"{name}_r{layer}", shape, dt))

        def sem(name):
            return ctx.enter_context(nc.semaphore(f"{name}_r{layer}"))

        square = sb("square", [P, C, T]) if layer == 0 else None
        w = sb("w", [P, C, n])
        mean_sq, rms = sb("mean_sq", [P, NT]), sb("rms", [P, NT])
        logit = sb("logit", [P, NT, n])
        top, total, inv = sb("top", [P, NT]), sb("total", [P, NT]), sb("inv", [P, NT])
        shifted, weight, prob = sb("shifted", [P, NT, n]), sb("weight", [P, NT, n]), sb("prob", [P, NT, n])
        ranked, marked = sb("ranked", [P, NT, n + 8]), sb("marked", [P, NT, n + 8])
        largest = sb("largest", [P, NT, 8])
        chosen, none, kept = sb("chosen", [P, NT, n]), sb("none", [P, NT]), sb("kept", [P, NT, n])
        l_ps = ctx.enter_context(nc.psum_tensor(f"l_ps_r{layer}", [P, NT, 64], F32))
        squared, w_scaled, logits_done = sem("squared"), sem("w_scaled"), sem("logits_done")
        rms_in, rms_done, step, shift_done, exp_done = (sem(x) for x in ("rms_in", "rms_done", "step", "shift", "exp"))
        padded, maxed, cut, marked_done = sem("padded"), sem("maxed"), sem("cut"), sem("marked")
        block = ctx.enter_context(nc.Block())

        @block.scalar
        def _(act):
            if layer == 0:
                nc.scalar.activation(square[:], k.h_t[:], ACT.Square).then_inc(squared, 1)
            act.wait_ge(shift_done, 1)
            nc.scalar.activation(weight[:], shifted[:], ACT.Exp).then_inc(exp_done, 1)

        @block.gpsimd
        def _(pool):
            if layer == 0:
                pool.wait_ge(rms_in, 1)
                nc.gpsimd.tensor_tensor(rms[:], mean_sq[:], k.minus_half[:, 0:1].broadcast_to([P, NT]),
                                        ALU.pow).then_inc(rms_done, 1)

        @block.tensor
        def _(pe):
            rw = w if layer == 0 else small(k, "rw1").rearrange("p (c e) -> p c e", c=C)
            if layer == 0:
                pe.wait_ge(w_scaled, 1)
                pe.wait_ge(squared, 1)
            for t in range(NT):
                for c in range(C):
                    last = nc.tensor.matmul(l_ps[:, t, 0:n], k.h_t[:, c, t * P:(t + 1) * P], rw[:, c, :],
                                            start=c == 0, stop=c == C - 1)
                if layer == 0:
                    for c in range(C):
                        last = nc.tensor.matmul(l_ps[:, t, n:n + 1], square[:, c, t * P:(t + 1) * P],
                                                k.ones[:, 0:1], start=c == 0, stop=c == C - 1)
            last.then_inc(logits_done, 1)

        @block.vector
        def _(dve):
            def over(ap):
                return ap.unsqueeze(2).broadcast_to([P, NT, n])

            nc.vector.memset(ranked[:, :, n:n + 8], PAD).then_inc(padded, 1)
            if layer == 0:
                nc.vector.tensor_tensor(w[:], small(k, "rw0").rearrange("p (c e) -> p c e", c=C),
                                        small(k, "rscale").unsqueeze(2).broadcast_to([P, C, n]),
                                        ALU.mult).then_inc(w_scaled, 1)
                dve.wait_ge(logits_done, 1)
                nc.vector.tensor_scalar(mean_sq[:], l_ps[:, :, n], 1.0 / D, 1e-6, ALU.mult,
                                        ALU.add).then_inc(rms_in, 1)
                dve.wait_ge(rms_done, 1)
                nc.vector.scalar_tensor_tensor(out=logit[:], in0=l_ps[:, :, 0:n], scalar=1.0 / math.sqrt(D),
                                               in1=over(rms[:]), op0=ALU.mult, op1=ALU.mult).then_inc(step, 1)
            else:
                dve.wait_ge(logits_done, 1)
                nc.vector.tensor_tensor(logit[:], l_ps[:, :, 0:n],
                                        small(k, "rb1").unsqueeze(1).broadcast_to([P, NT, n]),
                                        ALU.add).then_inc(step, 1)
            dve.wait_ge(step, 1)
            nc.vector.tensor_reduce(top[:], logit[:], AX, ALU.max).then_inc(step, 1)
            dve.wait_ge(step, 2)
            nc.vector.tensor_tensor(shifted[:], logit[:], over(top[:]), ALU.subtract).then_inc(shift_done, 1)
            dve.wait_ge(exp_done, 1)
            nc.vector.tensor_reduce(total[:], weight[:], AX, ALU.add).then_inc(step, 1)
            dve.wait_ge(step, 3)
            nc.vector.reciprocal(inv[:], total[:]).then_inc(step, 1)
            dve.wait_ge(step, 4)
            nc.vector.tensor_tensor(prob[:], weight[:], over(inv[:]), ALU.mult).then_inc(step, 1)
            dve.wait_ge(step, 5)
            nc.vector.tensor_copy(ranked[:, :, 0:n], logit[:] if layer == 0 else prob[:]).then_inc(step, 1)
            dve.wait_ge(step, 6)
            dve.wait_ge(padded, 1)
            for t in range(NT):
                nc.vector.max(largest[:, t, :], ranked[:, t, :]).then_inc(maxed, 1)
            dve.wait_ge(maxed, NT)
            nc.vector.memset(largest[:, :, top_n:8], PAD).then_inc(cut, 1)
            dve.wait_ge(cut, 1)
            for t in range(NT):
                nc.vector.match_replace(marked[:, t, :], largest[:, t, :], ranked[:, t, :],
                                        MARK).then_inc(marked_done, 1)
            dve.wait_ge(marked_done, NT)
            nc.vector.tensor_scalar(chosen[:], marked[:, :, 0:n], MARK, None, ALU.is_equal).then_inc(step, 1)
            dve.wait_ge(step, 7)
            nc.vector.tensor_tensor(kept[:], prob[:], chosen[:], ALU.mult).then_inc(step, 1)
            dve.wait_ge(step, 8)
            nc.vector.tensor_reduce(total[:], kept[:], AX, ALU.add).then_inc(step, 1)
            dve.wait_ge(step, 9)
            if layer == 0:
                nc.vector.tensor_scalar(none[:], total[:], 0.0, None, ALU.is_le).then_inc(step, 1)
                dve.wait_ge(step, 10)
                nc.vector.tensor_tensor(total[:], total[:], none[:], ALU.add).then_inc(step, 1)
            else:
                nc.vector.tensor_scalar(none[:], total[:], 1e-12, None, ALU.max).then_inc(step, 1)
                dve.wait_ge(step, 10)
                nc.vector.tensor_copy(total[:], none[:]).then_inc(step, 1)
            dve.wait_ge(step, 11)
            nc.vector.reciprocal(inv[:], total[:]).then_inc(step, 1)
            dve.wait_ge(step, 12)
            nc.vector.tensor_tensor(k.combine[:, :, 0:n], kept[:], over(inv[:]), ALU.mult).then_inc(step, 1)
            if layer == 0:
                dve.wait_ge(step, 13)
                nc.vector.tensor_tensor(k.combine[:, :, 0:n], k.combine[:, :, 0:n],
                                        small(k, "pes").unsqueeze(1).broadcast_to([P, NT, n]), ALU.mult)


def experts(nc, k, layer, up_w, down_w, func):
    GR, UNITS = 8, 4
    per_expert = layer == 1
    Y = 8 if per_expert else 4
    HALF = T // 2
    with ExitStack() as ctx:
        def sb(name, shape, dt=F32):
            return ctx.enter_context(nc.sbuf_tensor(f"{name}_e{layer}", shape, dt))

        def bank(name, n):
            return [ctx.enter_context(nc.psum_tensor(f"{name}{j}_e{layer}", [P, BANK], F32)) for j in range(n)]

        def sem(name):
            return ctx.enter_context(nc.semaphore(f"{name}_e{layer}"))

        up = [sb(f"up{s}", [P, C, 2, HID]) for s in range(2)]
        down = [sb(f"down{s}", [P, HC, D]) for s in range(2)]
        gate = [sb(f"gate{s}", [P, HALF]) for s in range(2)]
        hidden = [sb(f"hidden{s}", [P, HC, HALF]) for s in range(2)]
        g_ps, u_ps, y_ps = bank("g_ps", 2), bank("u_ps", 2), bank("y_ps", 4)
        up_in = [sem(f"up_in{s}") for s in range(2)]
        down_in = [sem(f"down_in{s}") for s in range(2)]
        up_done, gate_done, y_done = sem("up_done"), sem("gate_done"), sem("y_done")
        gated = sem("gated")
        x_added = sem("x_added")
        first_added = sem("first_added")
        block = ctx.enter_context(nc.Block())

        @block.sync
        def _(sp):
            def load(g, s):
                sp.dma_start(up[s][:], up_w[g].rearrange("p c (j h) -> p c j h", j=2)).then_inc(up_in[s], 16)
                sp.dma_start(down[s][:], down_w[g]).then_inc(down_in[s], 16)

            load(0, 0)
            load(1, 1)
            with sp.Fori(0, GR // 2 - 1) as i:
                for s in range(2):
                    sp.wait_ge(y_done, i * (UNITS * Y) + (2 * s + 2) * Y)
                    load(i * 2 + (s + 2), s)
            if per_expert:
                sp.wait_ge(y_done, GR // 2 * UNITS * Y - 2 * Y)
                load(GR, 0)

        @block.tensor
        def _(pe):
            def ups(s, half, unit, loads):
                pe.wait_ge(up_in[s], loads)
                for hc in range(HC):
                    b = hc % 2
                    pe.wait_ge(gated, unit * HC + (hc + 1))
                    for ps, j in ((g_ps[b], 0), (u_ps[b], 1)):
                        for c in range(C):
                            last = nc.tensor.matmul(ps[:], up[s][:, c, j, hc * P:(hc + 1) * P],
                                                    k.h_t[:, c, half * HALF:(half + 1) * HALF],
                                                    start=c == 0, stop=c == C - 1)
                    last.then_inc(up_done, 1)

            def downs(s, u, unit, loads, y0, by_expert):
                pe.wait_ge(down_in[s], loads)
                pe.wait_ge(gated, unit * HC + (HC + 2))
                hid = hidden[u % 2]
                m = 0
                for t in range(4):
                    rows = slice(t * P, (t + 1) * P)
                    for pair in range(2 if by_expert else 1):
                        y = y_ps[m % 4]
                        pe.wait_ge(x_added, y0 + (m + 1))
                        if by_expert:
                            for j in range(2):
                                last = nc.tensor.matmul(y[:, j * D:(j + 1) * D], hid[:, 2 * pair + j, rows],
                                                        down[s][:, 2 * pair + j, :], start=True, stop=True)
                        else:
                            for hc in range(HC):
                                last = nc.tensor.matmul(y[:, 0:D], hid[:, hc, rows], down[s][:, hc, :],
                                                        start=hc == 0, stop=hc == HC - 1)
                        last.then_inc(y_done, 1)
                        m += 1

            with pe.Fori(0, GR // 2) as i:
                def up_unit(u):
                    ups(u // 2, u % 2, i * UNITS + u, i * 16 + 16)

                def down_unit(u):
                    downs(u // 2, u, i * UNITS + u, i * 16 + 16, i * (UNITS * Y) + u * Y, per_expert)

                up_unit(0)
                for u in range(1, UNITS):
                    up_unit(u)
                    down_unit(u - 1)
                down_unit(UNITS - 1)
            if per_expert:
                done, loads = GR // 2 * UNITS, 16 * (GR // 2 + 1)
                ups(0, 0, done, loads)
                ups(0, 1, done + 1, loads)
                downs(0, 0, done, loads, done * Y, False)
                downs(0, 1, done + 1, loads, done * Y + 4, False)

        @block.scalar
        def _(act):
            def gates(unit):
                for hc in range(HC):
                    act.wait_ge(up_done, unit * HC + (hc + 1))
                    nc.scalar.activation(gate[hc % 2][:], g_ps[hc % 2][:], func).then_inc(gate_done, 1)

            with act.Fori(0, GR // 2) as i:
                for u in range(UNITS):
                    gates(i * UNITS + u)
            if per_expert:
                for u in range(2):
                    gates(GR // 2 * UNITS + u)

        @block.vector
        def _(dve):
            def gatings(u, unit):
                for hc in range(HC):
                    dve.wait_ge(gate_done, unit * HC + (hc + 1))
                    nc.vector.tensor_tensor(hidden[u % 2][:, hc, :], gate[hc % 2][:], u_ps[hc % 2][:],
                                            ALU.mult).then_inc(gated, 1)

            def adds(half, y0, g, by_expert):
                m = 0
                for t in range(4 * half, 4 * half + 4):
                    for pair in range(2 if by_expert else 1):
                        y = y_ps[m % 4]
                        dve.wait_ge(y_done, y0 + (m + 1))
                        dve.wait_ge(x_added, y0 + (m + 4))
                        if by_expert:
                            for j in range(2):
                                if j:
                                    dve.wait_ge(first_added, y0 + (m + 1))
                                nc.vector.scalar_tensor_tensor(
                                    out=k.x[:, t, :], in0=y[:, j * D:(j + 1) * D],
                                    scalar=k.combine[:, t, bass.ds(g * 4 + (2 * pair + j), 1)], in1=k.x[:, t, :],
                                    op0=ALU.mult, op1=ALU.add).then_inc(x_added if j else first_added, 1)
                        elif g is None:
                            nc.vector.tensor_tensor(k.x[:, t, :], k.x[:, t, :], y[:, 0:D],
                                                    ALU.add).then_inc(x_added, 1)
                        else:
                            nc.vector.scalar_tensor_tensor(
                                out=k.x[:, t, :], in0=y[:, 0:D], scalar=k.combine[:, t, bass.ds(g, 1)],
                                in1=k.x[:, t, :], op0=ALU.mult, op1=ALU.add).then_inc(x_added, 1)
                        m += 1

            dve.sem_inc(gated, 2)
            dve.sem_inc(x_added, 4)
            with dve.Fori(0, GR // 2) as i:
                def add_unit(u):
                    adds(u % 2, i * (UNITS * Y) + u * Y, i * 2 + u // 2, per_expert)

                gatings(0, i * UNITS)
                for u in range(1, UNITS):
                    gatings(u, i * UNITS + u)
                    add_unit(u - 1)
                add_unit(UNITS - 1)
            if per_expert:
                done = GR // 2 * UNITS
                gatings(0, done)
                gatings(1, done + 1)
                adds(0, done * Y, None, False)
                adds(1, done * Y + 4, None, False)


class Ring:

    def __init__(self, i, uses_per_tile, splits_per_tile, at, splits):
        assert uses_per_tile % 2 == 0
        self.i, self.each, self.split_each, self.at, self.splits = i, uses_per_tile // 2, splits_per_tile, at, splits

    def place(self, back=0):
        at = self.at - back
        return at % 2, self.i * self.each + (at // 2 + 1)

    def next(self, split=False):
        got = self.place()
        self.at += 1
        self.splits += 1 if split else 0
        return got

    def split_count(self):
        return self.i * self.split_each + self.splits


def cross_attention(nc, k, src):
    STEPS = 2 * PAIRS1
    USES = STEPS * 7 + 4
    SPLITS = STEPS * 5
    SCALE = HD1 ** -0.5
    TXT_EVEN = TXT + TXT % 2
    with ExitStack() as ctx:
        def sb(name, shape, dt=F32):
            return ctx.enter_context(nc.sbuf_tensor(name, shape, dt))

        def ps(name, shape):
            return ctx.enter_context(nc.psum_tensor(name, shape, F32))

        def sem(name):
            return ctx.enter_context(nc.semaphore(name))

        staged = sb("staged", [P, 4 * D])
        w_shared = sb("w_shared", [P, C * INNER])
        wq = w_shared[:].rearrange("p (c e) -> p c e", c=C)
        wo = w_shared[:].rearrange("p (h d) -> p h d", h=PAIRS1)
        wk, wv = sb("wk1", [P, 2, PAIRS1, D]), sb("wv1", [P, 2, C, INNER])
        ct = [sb(f"ct{b}", [P, 2, C, M], F32R) for b in range(2)]
        cn = [sb(f"cn{b}", [P, 2, NBLK, D], F32R) for b in range(2)]
        q = sb("q1", [P, PAIRS1, 2, P])
        a_hi, a_lo = sb("a_hi", [P, 2, C, P], F32R), sb("a_lo", [P, 2, C, P], F32R)
        prob = sb("prob1", [P, M])
        pt_hi, pt_lo = sb("pt_hi", [P, NBLK, P], F32R), sb("pt_lo", [P, NBLK, P], F32R)
        top = [sb(f"top1{s}", [P, 2]) for s in range(2)]
        bias = [sb(f"bias1{s}", [P, 2]) for s in range(2)]
        total = [sb(f"total1{s}", [P, 2]) for s in range(2)]
        inv = [sb(f"inv1{s}", [P, 2]) for s in range(2)]
        o, o_part = sb("o1", [P, 2, D]), sb("o1_part", [P, D])
        ot = sb("ot1", [P, 4, P])
        head_out = sb("head_out", [P, PAIRS1, P])
        s_ps = ps("s1_ps", [P, 4, BANK])
        t_ps = [ps(f"t1_ps{j}", [P, BANK]) for j in range(2)]
        txt_ps, img_ps = ps("txt_ps", [P, BANK]), ps("img_ps", [P, BANK])
        wq_in, wk_in, wv_in, wo_in = sem("wq1_in"), sem("wk1_in"), sem("wv1_in"), sem("wo1_in")
        queried, projected = sem("queried"), sem("projected")
        piece_in, hi_done, ct_split, cn_split = sem("piece_in"), sem("ctx_hi_done"), sem("ct_split"), sem("cn_split")
        scored, topped, bias_done, exp_done = sem("scored1"), sem("topped1"), sem("bias1_done"), sem("exp1_done")
        t_done = [sem(f"t1_done{j}") for j in range(2)]
        t_kept = [sem(f"t1_kept{j}") for j in range(2)]
        hi_kept = sem("hi_kept")
        summed, inv_done, part_kept, sums_kept = sem("summed1"), sem("inv1_done"), sem("part1_kept"), sem("sums1_kept")
        q_zeroed = sem("q_zeroed")
        split_begun = sem("split_begun")
        block = ctx.enter_context(nc.Block())

        def tiles(eng, body):
            body(0, Ring(0, USES, SPLITS, 3, 1), True, False)
            before = 3 + USES - 2 - 2 - 4 - 2 - USES
            with eng.Fori(1, NT - 1) as i:
                body(i, Ring(i, USES, SPLITS, before, -3), False, False)
            body(NT - 1, Ring(NT - 1, USES, SPLITS, before, -3), False, True)

        def ct_piece(j):
            half = (M + 1) // 2
            return j // 2, (j % 2) * half, half if j % 2 == 0 else M - half

        def cn_piece(j):
            return ((0, 4), (4, 3), (7, 3), (10, 3))[j - 4]

        @block.sync
        def _(sp):
            def load(i, b, pieces):
                for j in pieces:
                    if not isinstance(i, int) or i + b + j > 0:
                        wait_split(i, b, j)
                    if j < 4:
                        c, first, width = ct_piece(j)
                        sp.dma_start(staged[:, 0:width],
                                     src["ctx_t"][i * 2 + b][:, c, first:first + width]).then_inc(piece_in, 16)
                    else:
                        first, blocks = cn_piece(j)
                        sp.dma_start(staged[:, 0:blocks * D].rearrange("p (j d) -> p j d", d=D),
                                     src["ctx_n"][i * 2 + b][:, first:first + blocks, :]).then_inc(piece_in, 16)

            def wait_split(i, b, j):
                if j == 0:
                    sp.wait_ge(cn_split, i * 8 + 4 * b)
                elif j <= 4:
                    sp.wait_ge(ct_split, i * 8 + (4 * b + j))
                else:
                    sp.wait_ge(cn_split, i * 8 + (4 * b + j - 4))

            def load_wq():
                sp.dma_start(wq, src["wq1"]).then_inc(wq_in, 16)

            def load_wo(i):
                sp.wait_ge(queried, i + 2)
                sp.dma_start(wo, src["wo1"]).then_inc(wo_in, 16)

            load(0, 0, range(1))
            load_wq()
            sp.dma_start(wk[:], src["wk1"]).then_inc(wk_in, 16)
            load(0, 0, range(1, 8))
            sp.dma_start(wv[:], src["wv1"]).then_inc(wv_in, 16)
            load(0, 1, range(8))
            load(1, 0, range(8))
            load_wo(0)
            with sp.Fori(1, NT - 1) as i:
                load(i, 1, range(8))
                sp.wait_ge(projected, i + 0)
                load_wq()
                load(i + 1, 0, range(8))
                load_wo(i)
            load(NT - 1, 1, range(8))

        @block.gpsimd
        def _(pool):
            def split(i, b):
                for j in range(8):
                    n = i * 16 + (8 * b + j)
                    if j == 0 and not isinstance(i, int):
                        pool.wait_ge(scored, i * STEPS + (b - 1) * PAIRS1)
                    if j == 4 and not isinstance(i, int):
                        pool.wait_ge(summed, i * STEPS + (b - 1) * PAIRS1)
                    if j < 4:
                        c, first, width = ct_piece(j)
                        piece = staged[:, 0:width]
                        hi, lo = (ct[b][:, part, c, first:first + width] for part in range(2))
                    else:
                        first, blocks = cn_piece(j)
                        piece = staged[:, 0:blocks * D]
                        hi, lo = (cn[b][:, part, first:first + blocks, :].rearrange("p j d -> p (j d)")
                                  for part in range(2))
                    pool.wait_ge(piece_in, n * 16 + 16)
                    pool.sem_inc(split_begun, 1)
                    nc.gpsimd.tensor_scalar(hi, piece, 1.0, None, ALU.mult).then_inc(hi_done, 1)
                    pool.wait_ge(hi_done, n + 1)
                    nc.gpsimd.tensor_tensor(lo, piece, hi.bitcast(F32), ALU.subtract).then_inc(
                        ct_split if j < 4 else cn_split, 1)

            for b in range(2):
                split(0, b)
            with pool.Fori(1, NT) as i:
                for b in range(2):
                    split(i, b)


        @block.tensor
        def _(pe):
            def use(ring, split=False):
                bank, count = ring.next(split)
                if not isinstance(count, int) or count > 1:
                    pe.wait_ge(t_kept[bank], count - 1)
                return bank

            def kept(place):
                pe.wait_ge(t_kept[place[0]], place[1])

            def kept_before(ring, place):
                if place[0] != ring.place()[0]:
                    kept(place)

            def queries(ring, t):
                for half in range(2):
                    bank = use(ring)
                    for j in range(4):
                        p = 4 * half + j
                        for c in range(C):
                            last = nc.tensor.matmul(t_ps[bank][:, j * P:(j + 1) * P], wq[:, c, p * P:(p + 1) * P],
                                                    k.h_t[:, c, bass.ds(t * P, P)], start=c == 0, stop=c == C - 1)
                    last.then_inc(t_done[bank], 1)
                return ring.place(2), ring.place(1)

            def key_side(ring, n):
                b, p = divmod(n % STEPS, PAIRS1)
                bank = use(ring, True)
                for kind in range(2):
                    for c in range(C):
                        j = kind * C + c
                        last = nc.tensor.matmul(t_ps[bank][:, j * P:(j + 1) * P], wk[:, kind, p, c * P:(c + 1) * P],
                                                q[:, p, :, b * S:(b + 1) * S], start=True, stop=True)
                last.then_inc(t_done[bank], 1)

            def scores(n, part):
                b = n // PAIRS1
                """Part 0 is the text, parts 1 to 3 the image."""
                first, width = (0, TXT_EVEN) if part == 0 else (TXT + (part - 1) * SBLK, SBLK)
                kind = min(part, 1)
                for c in range(C):
                    out = s_ps[:, part, 0:width]
                    hi, lo = a_hi[:, kind, c, :], a_lo[:, kind, c, :]
                    nc.tensor.matmul(out, hi, ct[b][:, 0, c, first:first + width], start=c == 0, stop=False)
                    nc.tensor.matmul(out, hi, ct[b][:, 1, c, first:first + width], start=False, stop=False)
                    last = nc.tensor.matmul(out, lo, ct[b][:, 0, c, first:first + width], start=False, stop=c == C - 1)
                return last

            def turn(ring, g):
                bank = use(ring, True)
                for j in range(1 if g == 0 else 4):
                    blk = 0 if g == 0 else 4 * (g - 1) + j
                    first, width = (0, TXT) if g == 0 else (TXT + blk * IBLK, IBLK)
                    last = nc.tensor.transpose(t_ps[bank][0:width, j * P:(j + 1) * P],
                                               prob[:, first:first + width], k.ident)
                last.then_inc(t_done[bank], 1)

            def sums(n):
                hi, lo, rows = pt_hi[0:TXT, 0, :], pt_lo[0:TXT, 0, :], cn[n // PAIRS1]
                nc.tensor.matmul(txt_ps[:, 0:D], hi, rows[0:TXT, 0, 0, :], start=True, stop=False)
                nc.tensor.matmul(txt_ps[:, 0:D], hi, rows[0:TXT, 1, 0, :], start=False, stop=False)
                nc.tensor.matmul(txt_ps[:, 0:D], lo, rows[0:TXT, 0, 0, :], start=False, stop=True)
                for j in range(1, NBLK):
                    nc.tensor.matmul(img_ps[:], pt_hi[0:IBLK, j, :], rows[0:IBLK, :, j, :], start=j == 1, stop=False)
                    last = nc.tensor.matmul(img_ps[:, D:2 * D], pt_lo[0:IBLK, j, :], rows[0:IBLK, 0, j, :],
                                            start=False, stop=j == NBLK - 1)
                last.then_inc(summed, 1)

            def turn_sums(ring):
                bank = use(ring)
                for j in range(4):
                    last = nc.tensor.transpose(t_ps[bank][:, j * P:(j + 1) * P],
                                               o[:, j // 2, (j % 2) * P:(j % 2 + 1) * P], k.ident)
                last.then_inc(t_done[bank], 1)

            def value_side(ring, n):
                bank = use(ring)
                for r in range(2):
                    h = 2 * (n % PAIRS1) + r
                    for j in range(4):
                        last = nc.tensor.matmul(t_ps[bank][r * S:(r + 1) * S, 0:S],
                                                wv[:, j // 2, j % 2, h * HD1:(h + 1) * HD1],
                                                ot[:, j, r * S:(r + 1) * S], start=j == 0, stop=j == 3)
                last.then_inc(t_done[bank], 1)

            def project(ring):
                kept(ring.place(1))
                for half in range(2):
                    bank = use(ring)
                    cols = slice(half * P, (half + 1) * P)
                    for p in range(PAIRS1):
                        nc.tensor.matmul(t_ps[bank][:, 0:P], head_out[:, p, :], wo[:, p, cols], start=p == 0, stop=False)
                    nc.tensor.matmul(t_ps[bank][:, 0:P], k.ones[0:1, :], k.bo1[:, cols], start=False,
                                     stop=True).then_inc(t_done[bank], 1)

            pe.wait_ge(wq_in, 16)
            start = Ring(0, USES, SPLITS, 0, 0)
            for place in queries(start, 0):
                kept(place)
            pe.wait_ge(wk_in, 16)
            key_side(start, 0)

            def body(i, ring, first, last_tile):
                base = i * STEPS
                a_place = ring.place(1 if first else 2)
                for n in range(STEPS + 2 if last_tile else STEPS):
                    before, two_before = not first or n >= 1, not first or n >= 2
                    if n < STEPS and n % PAIRS1 == 0:
                        pe.wait_ge(ct_split, i * 8 + (n // PAIRS1 * 4 + 4))
                    if n <= STEPS and before:
                        pe.wait_ge(exp_done, base + n)
                    if n < STEPS:
                        kept_before(ring, a_place)
                    for g in range(4):
                        if n <= STEPS and before:
                            turn(ring, g)
                        if n < STEPS:
                            last = scores(n, g)
                    if n < STEPS:
                        last.then_inc(scored, 1)
                    turned = [ring.place(2), ring.place(1)]
                    if two_before:
                        pe.wait_ge(sums_kept, base + (n - 1))
                        turn_sums(ring)
                        ot_place = ring.place(1)
                    if n == STEPS - 1 and not last_tile:
                        if not first:
                            pe.wait_ge(wq_in, i * 16 + 16)
                        q_places = queries(ring, i + 1)
                    if n < STEPS - 1:
                        a_place = ring.place()
                        key_side(ring, n + 1)
                    if n <= STEPS and before:
                        if n % PAIRS1 == 1:
                            pe.wait_ge(cn_split, i * 8 + (n // PAIRS1 * 4 + 4))
                        for place in turned:
                            kept(place)
                        sums(n - 1 if n else STEPS - 1)
                    if n == STEPS - 1 and not last_tile:
                        for place in q_places:
                            kept(place)
                        a_place = ring.place()
                        key_side(ring, n + 1)
                    if two_before:
                        if first and n == 2:
                            pe.wait_ge(wv_in, 16)
                        kept_before(ring, ot_place)
                        value_side(ring, n - 2)
                    if n == 1 and not first:
                        pe.wait_ge(wo_in, i * 16)
                        project(ring)
                    if n == STEPS + 1:
                        project(ring)

            tiles(pe, body)

        def keep(eng, copy, ring, out, rows=P, cols=BANK):
            bank, count = ring.next()
            eng.wait_ge(t_done[bank], count)
            copy(out, t_ps[bank][0:rows, 0:cols]).then_inc(t_kept[bank], 1)

        def keep_hi(act, ring, out, rows=P, cols=BANK):
            bank, count = ring.next(True)
            act.wait_ge(t_done[bank], count)
            nc.scalar.activation(out, t_ps[bank][0:rows, 0:cols], ACT.Copy).then_inc(hi_kept, 1)

        def keep_lo(dve, ring, out, hi, rows=P, cols=BANK):
            bank, count = ring.next(True)
            dve.wait_ge(hi_kept, ring.split_count())
            nc.vector.tensor_tensor(out, t_ps[bank][0:rows, 0:cols], hi.bitcast(F32),
                                    ALU.subtract).then_inc(t_kept[bank], 1)

        def turned_part(pt, g):
            if g == 0:
                return pt[0:TXT, 0, :]
            return pt[0:IBLK, 4 * g - 3:4 * g + 1, :].rearrange("p j n -> p (j n)")

        def turned_size(g):
            return (TXT, P) if g == 0 else (IBLK, BANK)

        def flat(a):
            return a[:].rearrange("p k c n -> p (k c n)")

        def keep_queries(eng, copy, mine, ring):
            for half in range(2):
                bank, count = ring.next()
                if half == mine:
                    eng.wait_ge(t_done[bank], count)
                    for r in range(2):
                        rows = slice(r * HD1, (r + 1) * HD1)
                        last = copy(q[rows, 4 * half:4 * half + 4, r, :],
                                    t_ps[bank][rows, :].rearrange("p (j n) -> p j n", j=4))
                    last.then_inc(t_kept[bank], 1)

        @block.scalar
        def _(act):
            def copy(out, in_):
                return nc.scalar.activation(out, in_, ACT.Copy)

            act.wait_ge(q_zeroed, 1)
            start = Ring(0, USES, SPLITS, 0, 0)
            keep_queries(act, copy, 0, start)
            keep_hi(act, start, flat(a_hi))

            def body(i, ring, first, last_tile):
                for n in range(STEPS + 2 if last_tile else STEPS):
                    s = n % 2
                    before, two_before = not first or n >= 1, not first or n >= 2
                    if n <= STEPS and before:
                        for g in range(4):
                            keep_hi(act, ring, turned_part(pt_hi, g), *turned_size(g))
                    if two_before:
                        keep(act, copy, ring, ot[:].rearrange("p j n -> p (j n)"))
                    if n < STEPS - 1:
                        keep_hi(act, ring, flat(a_hi))
                    if n < STEPS:
                        act.wait_ge(bias_done, i * STEPS + (n + 1))
                        nc.scalar.activation(prob[:, TXT:M].rearrange("p (j m) -> p j m", j=SB),
                                             s_ps[:, 1:4, 0:SBLK], ACT.Exp, bias=bias[s][:, 1:2], scale=SCALE,
                                             accum_out=total[s][:, 1:2])
                        nc.scalar.activation(prob[:, 0:TXT], s_ps[:, 0, 0:TXT], ACT.Exp, bias=bias[s][:, 0:1],
                                             scale=SCALE, accum_out=total[s][:, 0:1]).then_inc(exp_done, 1)
                    if n == STEPS - 1 and not last_tile:
                        keep_queries(act, copy, 0, ring)
                        keep_hi(act, ring, flat(a_hi))
                    if two_before:
                        b, p = divmod((n - 2) % STEPS, PAIRS1)
                        keep(act, copy, ring, head_out[:, p, b * S:(b + 1) * S], P, S)
                    if n == 1 and not first or n == STEPS + 1:
                        ring.next()
                        ring.next()

            tiles(act, body)

        @block.vector
        def _(dve):
            def copy(out, in_):
                return nc.vector.tensor_copy(out, in_)

            nc.vector.memset(q[:], 0.0).then_inc(q_zeroed, 1)
            dve.wait_ge(q_zeroed, 1)
            start = Ring(0, USES, SPLITS, 0, 0)
            keep_queries(dve, copy, 1, start)
            dve.sem_inc(queried, 1)
            keep_lo(dve, start, flat(a_lo), flat(a_hi))

            def body(i, ring, first, last_tile):
                base = i * STEPS
                for n in range(STEPS + 2 if last_tile else STEPS):
                    s = n % 2
                    before, two_before = not first or n >= 1, not first or n >= 2
                    if n <= STEPS and before:
                        for g in range(4):
                            keep_lo(dve, ring, turned_part(pt_lo, g), turned_part(pt_hi, g), *turned_size(g))
                    if n < STEPS:
                        dve.wait_ge(scored, base + (n + 1))
                        nc.vector.tensor_reduce(top[s][:, 0:1], s_ps[:, 0, 0:TXT], AX, ALU.max)
                        nc.vector.tensor_reduce(top[s][:, 1:2], s_ps[:, 1:4, 0:SBLK], mybir.AxisListType.XY,
                                                ALU.max).then_inc(topped, 1)
                        dve.wait_ge(topped, base + (n + 1))
                        nc.vector.tensor_scalar(bias[s][:], top[s][:], -SCALE, None, ALU.mult).then_inc(bias_done, 1)
                    if two_before:
                        ring.next()
                    if n == STEPS - 1 and not last_tile:
                        keep_queries(dve, copy, 1, ring)
                        dve.sem_inc(queried, 1)
                    if n < STEPS - 1 or n == STEPS - 1 and not last_tile:
                        keep_lo(dve, ring, flat(a_lo), flat(a_hi))
                    if n <= STEPS and before:
                        dve.wait_ge(exp_done, base + n)
                        nc.vector.reciprocal(inv[1 - s][:], total[1 - s][:]).then_inc(inv_done, 1)
                        dve.wait_ge(summed, base + n)
                        dve.wait_ge(inv_done, base + n)
                        nc.vector.tensor_scalar(o_part[:], img_ps[:, D:2 * D], inv[1 - s][:, 1:2], None,
                                                ALU.mult).then_inc(part_kept, 1)
                        nc.vector.tensor_scalar(o[:, 0, :], txt_ps[:, 0:D], inv[1 - s][:, 0:1], None, ALU.mult)
                        dve.wait_ge(part_kept, base + n)
                        nc.vector.scalar_tensor_tensor(out=o[:, 1, :], in0=img_ps[:, 0:D], scalar=inv[1 - s][:, 1:2],
                                                       in1=o_part[:], op0=ALU.mult, op1=ALU.add).then_inc(sums_kept, 1)
                    if two_before:
                        ring.next()
                    if n == 1 and not first or n == STEPS + 1:
                        t = i if n == STEPS + 1 else i - 1
                        for half in range(2):
                            bank, count = ring.next()
                            dve.wait_ge(t_done[bank], count)
                            xt = k.x[:, bass.ds(t, 1), half * P:(half + 1) * P].rearrange("p a d -> p (a d)")
                            nc.vector.tensor_tensor(xt, xt, t_ps[bank][:, 0:P], ALU.add).then_inc(t_kept[bank], 1)
                        dve.sem_inc(projected, 1)

            tiles(dve, body)


def scan_layer(nc, k, src):
    HALF = T // 2
    HB = NB // 2
    with ExitStack() as outer:
        def keep(name, shape, dt=F32):
            return outer.enter_context(nc.sbuf_tensor(name, shape, dt))

        gate = keep("gate_z", [P, C, T])
        xc = keep("xc", [P, C, T])
        u = keep("u", [P, C, T])
        dt = keep("dt", [P, T])
        a_neg = keep("a_neg", [P, C * NS])
        par = keep("par", [NPAR, T])
        diag = keep("diag_d", [P, C, P])
        w_out = keep("w_out", [P, C, D])
        gated = keep("gated_y", [P, C, T])
        w_out_in = outer.enter_context(nc.semaphore("w_out_in"))

        with ExitStack() as ctx:
            w_in_proj = ctx.enter_context(nc.sbuf_tensor("w_in_proj", [P, C, 2 * D], F32))
            xpad = ctx.enter_context(nc.sbuf_tensor("xpad", [P, C, NB, S + KC - 1], F32))
            acc = [ctx.enter_context(nc.sbuf_tensor(f"conv_acc{c}", [P, NB, S], F32)) for c in range(C)]
            ps = ctx.enter_context(nc.psum_tensor("xz_ps", [P, 2 * C, 2, BANK], F32))
            proj_in = ctx.enter_context(nc.semaphore("proj_in"))
            projected = ctx.enter_context(nc.semaphore("projected"))
            x_kept = ctx.enter_context(nc.semaphore("x_kept"))
            pad_zeroed = ctx.enter_context(nc.semaphore("pad_zeroed"))
            tap_done = ctx.enter_context(nc.semaphore("tap_done"))
            block = ctx.enter_context(nc.Block())

            @block.sync
            def _(sp):
                sp.dma_start(w_in_proj[:], src["win"]).then_inc(proj_in, 16)
                sp.dma_start(w_out[:], src["wout"]).then_inc(w_out_in, 16)

            @block.tensor
            def _(pe):
                pe.wait_ge(proj_in, 16)
                for e in range(2 * C):
                    for g in range(2):
                        for c in range(C):
                            last = nc.tensor.matmul(ps[:, e, g, :], w_in_proj[:, c, e * P:(e + 1) * P],
                                                    k.h_t[:, c, g * HALF:(g + 1) * HALF],
                                                    start=c == 0, stop=c == C - 1)
                        last.then_inc(projected, 1)

            @block.scalar
            def _(act):
                for e in range(C):
                    for g in range(2):
                        act.wait_ge(projected, 2 * e + g + 1)
                        nc.scalar.activation(xpad[:, e, g * HB:(g + 1) * HB, KC - 1:],
                                             ps[:, e, g, :].rearrange("p (b l) -> p b l", l=S),
                                             ACT.Copy).then_inc(x_kept, 1)
                for e in range(C):
                    for g in range(2):
                        act.wait_ge(projected, 2 * (C + e) + g + 1)
                        nc.scalar.activation(gate[:, e, g * HALF:(g + 1) * HALF], ps[:, C + e, g, :], ACT.Silu)
                for c in range(C):
                    act.wait_ge(tap_done, KC * C - C + c + 1)
                    nc.scalar.activation(xc[:, c, :], acc[c][:].rearrange("p b l -> p (b l)"), ACT.Silu,
                                         bias=small(k, "convb")[:, c:c + 1])

            @block.vector
            def _(dve):
                nc.vector.memset(xpad[:, :, :, 0:KC - 1], 0.0).then_inc(pad_zeroed, 1)
                dve.wait_ge(pad_zeroed, 1)
                w = small(k, "convw")
                for tap in range(KC):
                    for c in range(C):
                        seen = xpad[:, c, :, tap:tap + S]
                        if tap == 0:
                            dve.wait_ge(x_kept, 2 * c + 2)
                            nc.vector.tensor_scalar(acc[c][:], seen, w[:, c * KC:c * KC + 1], None,
                                                    ALU.mult).then_inc(tap_done, 1)
                        else:
                            dve.wait_ge(tap_done, C * (tap - 1) + c + 1)
                            nc.vector.scalar_tensor_tensor(
                                out=acc[c][:], in0=seen, scalar=w[:, c * KC + tap:c * KC + tap + 1], in1=acc[c][:],
                                op0=ALU.mult, op1=ALU.add).then_inc(tap_done, 1)

        with ExitStack() as ctx:
            w_par = ctx.enter_context(nc.sbuf_tensor("w_par", [P, C, NPAR], F32))
            pick_dt = ctx.enter_context(nc.sbuf_tensor("pick_dt", [NPAR, P], F32))
            mag = ctx.enter_context(nc.sbuf_tensor("mag", [NPAR, T], F32))
            pos = ctx.enter_context(nc.sbuf_tensor("pos_part", [NPAR, T], F32))
            exp_a = ctx.enter_context(nc.sbuf_tensor("exp_a", [P, C * NS], F32))
            p_ps = ctx.enter_context(nc.psum_tensor("par_ps", [P, 2, BANK], F32))
            d_ps = ctx.enter_context(nc.psum_tensor("dt_ps", [P, 2, BANK], F32))
            par_in, par_done, par_kept = (ctx.enter_context(nc.semaphore(n)) for n in ("par_in", "par_done", "par_kept"))
            soft, soft_kept = (ctx.enter_context(nc.semaphore(n)) for n in ("softplus_step", "softplus_kept"))
            pos_done, pick_set, dt_done, dt_kept = (
                ctx.enter_context(nc.semaphore(n)) for n in ("pos_done", "pick_set", "dt_done", "dt_kept"))
            exp_done = ctx.enter_context(nc.semaphore("exp_a_done"))
            block = ctx.enter_context(nc.Block())
            row = slice(NPAR - 1, NPAR)

            @block.sync
            def _(sp):
                sp.dma_start(w_par[:], src["wpar"]).then_inc(par_in, 16)

            @block.tensor
            def _(pe):
                pe.wait_ge(par_in, 16)
                for g in range(2):
                    for c in range(C):
                        last = nc.tensor.matmul(p_ps[0:NPAR, g, :], w_par[:, c, :], xc[:, c, g * HALF:(g + 1) * HALF],
                                                start=c == 0, stop=c == C - 1)
                last.then_inc(par_done, 1)
                pe.wait_ge(soft_kept, 1)
                pe.wait_ge(pick_set, 2)
                for g in range(2):
                    last = nc.tensor.matmul(d_ps[:, g, :], pick_dt[:], par[:, g * HALF:(g + 1) * HALF],
                                            start=True, stop=True)
                last.then_inc(dt_done, 1)

            @block.scalar
            def _(act):
                nc.scalar.activation(exp_a[:], small(k, "alog"), ACT.Exp).then_inc(exp_done, 1)
                act.wait_ge(par_done, 1)
                nc.scalar.activation(par[:], p_ps[0:NPAR].rearrange("p g n -> p (g n)"), ACT.Copy).then_inc(par_kept, 1)
                act.wait_ge(par_kept, 1)
                nc.scalar.activation(mag[row], par[row], ACT.Abs).then_inc(soft, 1)
                act.wait_ge(soft, 1)
                nc.scalar.activation(mag[row], mag[row], ACT.Exp, scale=-1.0).then_inc(soft, 1)
                act.wait_ge(soft, 2)
                nc.scalar.activation(mag[row], mag[row], ACT.Ln, bias=1.0).then_inc(soft, 1)
                act.wait_ge(dt_done, 1)
                nc.scalar.activation(dt[:], d_ps[:].rearrange("p g n -> p (g n)"), ACT.Copy).then_inc(dt_kept, 1)

            @block.vector
            def _(dve):
                nc.vector.memset(pick_dt[:], 0.0).then_inc(pick_set, 1)
                dve.wait_ge(pick_set, 1)
                nc.vector.memset(pick_dt[row], 1.0).then_inc(pick_set, 1)
                dve.wait_ge(exp_done, 1)
                nc.vector.tensor_scalar(a_neg[:], exp_a[:], -1.0, None, ALU.mult)
                for c in range(C):
                    nc.vector.tensor_scalar(diag[:, c, :], k.ident, small(k, "dpar")[:, c:c + 1], None, ALU.mult)
                dve.wait_ge(par_kept, 1)
                nc.vector.tensor_scalar(pos[row], par[row], 0.0, None, ALU.max).then_inc(pos_done, 1)
                dve.wait_ge(pos_done, 1)
                dve.wait_ge(soft, 3)
                nc.vector.tensor_tensor(par[row], pos[row], mag[row], ALU.add).then_inc(soft_kept, 1)
                dve.wait_ge(dt_kept, 1)
                for c in range(C):
                    nc.vector.tensor_tensor(u[:, c, :], xc[:, c, :], dt[:], ALU.mult)

        with ExitStack() as ctx:
            def sb(name, shape):
                return ctx.enter_context(nc.sbuf_tensor(name, shape, F32))

            def sem(name):
                return ctx.enter_context(nc.semaphore(name))

            ones = sb("ones33", [NPAR, P])
            row_b, row_c = sb("row_b", [NPAR, T]), sb("row_c", [NPAR, T])
            decay = [sb(f"decay{c}", [P, NB, S]) for c in range(C)]
            drive = [sb(f"drive{c}", [P, T]) for c in range(C)]
            state = [sb(f"state{c}", [P, T]) for c in range(C)]
            read = [sb(f"read{c}", [P, T]) for c in range(C)]
            c_row = sb("c_row", [P, T])
            b_ps = ctx.enter_context(nc.psum_tensor("b_ps", [P, 2, BANK], F32))
            c_ps = ctx.enter_context(nc.psum_tensor("c_ps", [P, 2, BANK], F32))
            y_ps = ctx.enter_context(nc.psum_tensor("scan_y_ps", [P, C, 2, BANK], F32))
            set_up, rows_masked, b_done, c_done = sem("scan_set_up"), sem("rows_masked"), sem("b_done"), sem("c_done")
            c_kept, decayed, driven, scanned = sem("c_kept"), sem("decayed"), sem("driven"), sem("scanned")
            read_done, y_added = sem("read_done"), sem("scan_y_added")
            block = ctx.enter_context(nc.Block())


            @block.scalar
            def _(act):
                def rows(n):
                    nc.scalar.activation(row_b[:], par[:], ACT.Identity, scale=small(k, "ident")[0:NPAR, bass.ds(n, 1)])
                    nc.scalar.activation(row_c[:], par[:], ACT.Identity,
                                         scale=small(k, "ident")[0:NPAR, bass.ds(n + NS, 1)]).then_inc(rows_masked, 1)

                def decays(n):
                    for c in range(C):
                        nc.scalar.activation(decay[c][:, :, 1:], dt[:].rearrange("p (b l) -> p b l", l=S)[:, :, 1:],
                                             ACT.Exp, scale=a_neg[:, bass.ds(n + c * NS, 1)]).then_inc(decayed, 1)

                rows(0)
                act.wait_ge(set_up, 1)
                decays(0)
                act.wait_ge(c_done, 1)
                nc.scalar.activation(c_row[:], c_ps[:].rearrange("p g n -> p (g n)"), ACT.Copy).then_inc(c_kept, 1)
                with act.Fori(0, NS - 1) as n:
                    act.wait_ge(c_done, n + 1)
                    rows(n + 1)
                    for c in range(C):
                        act.wait_ge(scanned, n * 2 + (c + 3))
                        nc.scalar.activation(decay[c][:, :, 1:], dt[:].rearrange("p (b l) -> p b l", l=S)[:, :, 1:],
                                             ACT.Exp, scale=a_neg[:, bass.ds(n + (c * NS + 1), 1)]).then_inc(decayed, 1)
                    act.wait_ge(c_done, n + 2)
                    act.wait_ge(read_done, n * 2 + 4)
                    nc.scalar.activation(c_row[:], c_ps[:].rearrange("p g n -> p (g n)"), ACT.Copy).then_inc(c_kept, 1)

            @block.tensor
            def _(pe):
                def spread(out, row_):
                    for g in range(2):
                        last = nc.tensor.matmul(out[:, g, :], ones[:], row_[:, g * HALF:(g + 1) * HALF],
                                                start=True, stop=True)
                    return last

                def add(c, final):
                    for g in range(2):
                        last = nc.tensor.matmul(y_ps[:, c, g, :], k.ident, read[c][:, g * HALF:(g + 1) * HALF],
                                                start=False, stop=final, skip_group_check=True)
                    last.then_inc(y_added, 1)

                pe.sem_inc(y_added, 2)
                for c in range(C):
                    for g in range(2):
                        nc.tensor.matmul(y_ps[:, c, g, :], diag[:, c, :], xc[:, c, g * HALF:(g + 1) * HALF],
                                         start=True, stop=False, skip_group_check=True)
                pe.wait_ge(set_up, 1)
                pe.wait_ge(rows_masked, 1)
                spread(b_ps, row_b).then_inc(b_done, 1)
                spread(c_ps, row_c).then_inc(c_done, 1)
                with pe.Fori(0, NS - 1) as n:
                    pe.wait_ge(rows_masked, n + 2)
                    pe.wait_ge(driven, n * 2 + 2)
                    spread(b_ps, row_b).then_inc(b_done, 1)
                    pe.wait_ge(c_kept, n + 1)
                    spread(c_ps, row_c).then_inc(c_done, 1)
                    for c in range(C):
                        pe.wait_ge(read_done, n * 2 + (c + 3))
                        add(c, False)
                for c in range(C):
                    pe.wait_ge(read_done, (NS - 1) * 2 + c + 3)
                    add(c, True)

            @block.gpsimd
            def _(pool):
                pool.sem_inc(read_done, 2)
                with pool.Fori(0, NS) as n:
                    pool.wait_ge(c_kept, n + 1)
                    for c in range(C):
                        pool.wait_ge(scanned, n * 2 + (c + 3))
                        pool.wait_ge(y_added, n * 2 + 2)
                        nc.gpsimd.tensor_tensor(read[c][:], state[c][:], c_row[:], ALU.mult).then_inc(read_done, 1)

            @block.vector
            def _(dve):
                dve.sem_inc(scanned, 2)
                nc.vector.memset(ones[:], 1.0)
                for c in range(C):
                    last = nc.vector.memset(decay[c][:], 0.0)
                last.then_inc(set_up, 1)
                with dve.Fori(0, NS) as n:
                    dve.wait_ge(scanned, n * 2 + 2)
                    dve.wait_ge(b_done, n + 1)
                    for c in range(C):
                        nc.vector.tensor_tensor(drive[c][:], u[:, c, :], b_ps[:].rearrange("p g n -> p (g n)"),
                                                ALU.mult).then_inc(driven, 1)
                    for c in range(C):
                        dve.wait_ge(driven, n * 2 + (c + 1))
                        dve.wait_ge(decayed, n * 2 + (c + 1))
                        dve.wait_ge(read_done, n * 2 + 2)
                        nc.vector.tensor_tensor_scan(state[c][:], decay[c][:].rearrange("p b l -> p (b l)"),
                                                     drive[c][:], 0.0, ALU.mult, ALU.add).then_inc(scanned, 1)
                for c in range(C):
                    dve.wait_ge(y_added, (NS - 1) * 2 + c + 3)
                    nc.vector.tensor_tensor(gated[:, c, :], y_ps[:, c].rearrange("p g n -> p (g n)"), gate[:, c, :],
                                            ALU.mult)

        with ExitStack() as ctx:
            o_ps = ctx.enter_context(nc.psum_tensor("scan_o_ps", [P, NT, BANK], F32))
            o_done = ctx.enter_context(nc.semaphore("scan_o_done"))
            block = ctx.enter_context(nc.Block())

            @block.tensor
            def _(pe):
                pe.wait_ge(w_out_in, 16)
                for t in range(NT):
                    for c in range(C):
                        last = nc.tensor.matmul(o_ps[:, t, 0:D], gated[:, c, t * P:(t + 1) * P], w_out[:, c, :],
                                                start=c == 0, stop=c == C - 1)
                    last.then_inc(o_done, 1)

            @block.vector
            def _(dve):
                for t in range(NT):
                    dve.wait_ge(o_done, t + 1)
                    nc.vector.tensor_tensor(k.x[:, t, :], k.x[:, t, :], o_ps[:, t, 0:D], ALU.add)


def perceiver_program(nc, src, out):
    with ExitStack() as ctx:
        k = Chip()

        def sb(name, shape, dt=F32, scope=ctx):
            return scope.enter_context(nc.sbuf_tensor(name, shape, dt))

        k.x = sb("x_sb", [P, NT, D])
        k.h_t = sb("h_t", [P, C, T])
        k.small = sb("small", [P, SMALL_N])
        k.ident = small(k, "ident")
        k.ones = sb("ones", [P, P])
        k.minus_half = sb("minus_half", [P, 1])
        k.log_s = sb("log_s", [P, 1])
        k.length = sb("length", [P, NB])
        k.far_count = sb("far_count", [1, 1], I32)
        k.combine = sb("combine", [P, NT, E1])
        k.bo1 = sb("bo1", [1, D])
        with ExitStack() as attentions:
            rows = k.rows = sb("rows", [1, len(ROWS), D], scope=attentions)
            k.early = sb("early", [P, EARLY_N], scope=attentions)
            k.row = lambda name: rows[:, ROWS[name], :]
            with ExitStack() as local:
                k.iota_all = sb("iota_all", [P, NWIN * WN], scope=local)
                k.q0 = sb("q0", [P, C, T], scope=local)
                k.pos = sb("pos", [P, NB + 1, PK], scope=local)
                k.ctx_t = sb("ctx_out_t", [P, C, T], scope=local)
                load_stage(nc, k, src)
                norm_stage(nc, k, "a")
                positions_stage(nc, k, src)
                local_attention(nc, k, src)
                after_local(nc, k, src)
            norm_stage(nc, k, "b")
            self_attention(nc, k, src)
        norm_stage(nc, k, "c")
        route(nc, k, 0)
        experts(nc, k, 0, src["up0"], src["down0"], ACT.Gelu_apprx_tanh)
        norm_stage(nc, k, "d", clear=True)
        cross_attention(nc, k, src)
        norm_stage(nc, k, "e")
        scan_layer(nc, k, src)
        norm_stage(nc, k, "f")
        route(nc, k, 1)
        experts(nc, k, 1, src["up1"], src["down1"], ACT.Silu)
        store_stage(nc, k, out)


def _small_arrays(np, a):
    part = np.arange(P)
    near = np.concatenate([np.arange(LOW), np.arange(HIGH, M)])
    loc = (part % S)[:, None]
    ref = np.tile(np.arange(NK) + (-NK // 2), PAIRS0)

    def rep(v):
        return np.broadcast_to(np.asarray(v).reshape(1, -1), (P, np.asarray(v).size))

    def cols(v):
        v = np.asarray(v).reshape(C, P, -1)
        return v.transpose(1, 0, 2).reshape(P, -1)

    boff = np.asarray(a["L0_xattn_boff"]).reshape(PAIRS0, 2, NK).transpose(1, 0, 2).reshape(2, PK)
    parts = dict(
        ident=np.eye(P), mask8=(part[:, None] // HD0 == np.arange(8)[None]) * 0.125,
        mask2=((part[:, None] % 32) // HD0 == np.arange(2)[None]), ref=rep(ref), loc=loc,
        boff=np.repeat(boff, S, axis=0), bq=cols(a["L0_xattn_bq"]), bk=cols(a["L0_xattn_bk"]),
        rscale=cols(a["L0_ffn_router_scale"]), pes=rep(a["L0_ffn_per_expert_scale"]),
        rw0=cols(a["L0_ffn_router_w"]), convw=cols(a["L1_attn_conv_w"]), convb=cols(a["L1_attn_conv_b"]),
        alog=cols(a["L1_attn_A_log"]), dpar=cols(a["L1_attn_D_param"]),
        rw1=cols(np.asarray(a["L1_ffn_router_w"]).T), rb1=rep(a["L1_ffn_router_bias"]),
    )
    early = dict(same=(part[:, None] // S == part[None] // S), iota=rep(near), ls=rep(a["L0_attn_layerscale"]))
    packed = []
    for arrays, places in ((parts, SMALL), (early, EARLY)):
        assert list(arrays) == list(places) and all(v.shape == (P, places[n][1]) for n, v in arrays.items())
        packed.append(np.concatenate([np.asarray(v, dtype=np.float32) for v in arrays.values()], axis=1))
    return packed


def _laid_out(np, a):
    def chunks(w):
        w = np.asarray(w)
        return w.reshape(w.shape[0] // P, P, -1).transpose(1, 0, 2)

    ctx = np.asarray(a["ctx_1024"])
    ctx_t = np.zeros((NB, P, C, MPAD), ctx.dtype)
    ctx_t[..., :M] = ctx.transpose(0, 2, 1).reshape(NB, C, P, M).transpose(0, 2, 1, 3)
    ctx_n = np.zeros((NB, NBLK, P, D), ctx.dtype)
    ctx_n[:, 0, :TXT] = ctx[:, :TXT]
    ctx_n[:, 1:, :IBLK] = ctx[:, TXT:].reshape(NB, IB, IBLK, D)
    woff = np.asarray(a["L0_xattn_Woff"]).reshape(PAIRS0, 2, NK, D).transpose(1, 0, 2, 3).reshape(2 * PK, D)
    up0 = np.asarray(a["L0_ffn_gating_w"]).reshape(E0, 2 * HID, C, P)
    up1 = np.stack([np.asarray(a["L1_ffn_gate_w"]).reshape(GROUPS, HID, D),
                    np.asarray(a["L1_ffn_up_w"]).reshape(GROUPS, HID, D)], axis=1)
    shared = np.stack([np.asarray(a["L1_ffn_sgate_w"]), np.asarray(a["L1_ffn_sup_w"])])[None]
    up1 = np.concatenate([up1, shared], axis=0).reshape(GROUPS + 1, 2 * HID, C, P)
    down1 = np.asarray(a["L1_ffn_down_w"]).reshape(GROUPS, HC, D, P).transpose(0, 3, 1, 2)
    sdown = np.asarray(a["L1_ffn_sdown_w"]).T.reshape(1, HC, P, D).transpose(0, 2, 1, 3)
    rows = np.arange(NWIN * WN)
    packed = _small_arrays(np, a)
    laid = dict(
        iota_all=np.broadcast_to(np.where(rows < M, rows, 1 << 20).astype(np.float32), (P, NWIN * WN)),
        x=np.asarray(a["x"]).reshape(T, D), mask=a["mask_BxS2_if0"], small=packed[0], early=packed[1],
        rows=np.stack([np.asarray(a[n]) for n in ("L0_xattn_bv", "L0_xattn_bo", "L0_attn_bq", "L0_attn_bk",
                                                  "L0_attn_bv", "L0_attn_bo")])[None],
        bo1=np.asarray(a["L1_xattn_bo"])[None],
        ctx_t=ctx_t, ctx_n=ctx_n.transpose(0, 2, 1, 3),
        wq0=chunks(np.asarray(a["L0_xattn_Wq"]).T), wk0=chunks(np.asarray(a["L0_xattn_Wk"]).T),
        wv0=chunks(np.asarray(a["L0_xattn_Wv"]).T), wo0=chunks(np.asarray(a["L0_xattn_Wo"]).T),
        woff0=chunks(woff.T).reshape(P, C, 2, PK),
        wqa=chunks(np.asarray(a["L0_attn_Wq"]).T), wka=chunks(np.asarray(a["L0_attn_Wk"]).T),
        wva=chunks(np.asarray(a["L0_attn_Wv"]).T), woa=chunks(np.asarray(a["L0_attn_Wo"]).T),
        up0=up0.transpose(0, 3, 2, 1), down0=np.asarray(a["L0_ffn_linear_w"]).reshape(E0, HC, P, D).transpose(0, 2, 1, 3),
        wq1=chunks(a["L1_xattn_Wq"]),
        wk1=np.stack([chunks(np.asarray(a[n]).T) for n in ("L1_xattn_Wk", "L1_xattn_Wk_ip")], axis=1),
        wv1=np.stack([chunks(a[n]) for n in ("L1_xattn_Wv", "L1_xattn_Wv_ip")], axis=1),
        wo1=chunks(a["L1_xattn_Wo"]),
        win=chunks(np.asarray(a["L1_attn_in_proj_w"]).T), wpar=chunks(np.asarray(a["L1_attn_x_proj_w"]).T),
        wout=chunks(np.asarray(a["L1_attn_out_proj_w"]).T),
        up1=up1.transpose(0, 3, 2, 1), down1=np.concatenate([down1, sdown], axis=0),
    )
    return {n: np.ascontiguousarray(v) for n, v in laid.items()}


def kernel(**inputs):
    import numpy as np
    import concourse.bacc as bacc
    from concourse.bass_utils import run_bass_kernel_spmd

    nc = bacc.Bacc("TRN2", target_bir_lowering=False, num_devices=1)
    laid = _laid_out(np, inputs)
    arrays = {f"in_{n}": v for n, v in laid.items()}
    aps = {n: nc.dram_tensor(f"in_{n}", v.shape, mybir.dt.from_np(v.dtype), kind="ExternalInput").ap()
           for n, v in laid.items()}
    out = nc.dram_tensor("out_x", (T, D), F32, kind="ExternalOutput").ap()
    perceiver_program(nc, aps, out)
    r = run_bass_kernel_spmd(nc, [arrays], core_ids=[0])
    return r.results[0]["out_x"].reshape(NB, S, D)
```

```python
import math
from contextlib import ExitStack

import concourse.bass as bass
from concourse import mybir

ALU = mybir.AluOpType
ACT = mybir.ActivationFunctionType
F32 = mybir.dt.float32
F32R = mybir.dt.float32r
I32 = mybir.dt.int32
AX = mybir.AxisListType.X
BANK = 512

P = 128
D = 256
C = D // P
NB, S = 16, 64
T = NB * S
NT = T // P
M = 1601
EPS = 1e-5

H0, HD0, NK = 16, 16, 5
PAIRS0 = H0 // 2
PK = PAIRS0 * NK
LOW, HIGH = 96, 1569
WN = LOW + M - HIGH
NWIN = 13
MPAD = NWIN * WN
assert WN == P

E0, HID = 8, 512
HC = HID // P

H1, HD1, TXT = 16, 64, 77
PAIRS1 = H1 // 2
INNER = H1 * HD1
IMG = M - TXT
IB, IBLK = 12, 127
SB, SBLK = 3, 508
assert IB * IBLK == IMG and SB * SBLK == IMG
NBLK = IB + 1

NS, KC = 16, 4
NPAR = 2 * NS + 1

E1, TOP1 = 32, 4
GROUPS = E1 // HC

SMALL = {}
_at = 0
for _name, _n in (
    ("ident", P), ("mask8", 8), ("mask2", 2), ("ref", PK), ("loc", 1),
    ("boff", PK), ("bq", C), ("bk", C), ("rscale", C), ("pes", E0), ("rw0", C * E0),
    ("convw", C * KC), ("convb", C), ("alog", C * NS), ("dpar", C), ("rw1", C * E1), ("rb1", E1),
):
    SMALL[_name] = (_at, _n)
    _at += _n
SMALL_N = _at
EARLY = {"same": (0, P), "iota": (P, WN), "ls": (P + WN, D)}
EARLY_N = P + WN + D
ROWS = {n: i for i, n in enumerate(("bv0", "bo0", "bqa", "bka", "bva", "boa"))}


class Chip:
    pass


def broadcast(ap, dim, n):
    return ap.unsqueeze(dim).broadcast(dim, n)


def small(k, name):
    a, n = SMALL[name] if name in SMALL else EARLY[name]
    return (k.small if name in SMALL else k.early)[:, a:a + n]


def clear_semaphores(nc, eng):
    ended = sorted(nc.released_uncleared_semaphores)
    first = 0
    for j in range(1, len(ended) + 1):
        if j == len(ended) or ended[j] != ended[j - 1] + 1:
            eng.sem_clear(range(ended[first], ended[j - 1] + 1))
            first = j


def norm_stage(nc, k, tag, clear=False, load=None):
    with ExitStack() as ctx:
        stats = ctx.enter_context(nc.sbuf_tensor(f"stats_{tag}", [P, NT, 6], F32))
        moments = ctx.enter_context(nc.sbuf_tensor(f"moments_{tag}", [P, NT, 2], F32))
        var_eps = ctx.enter_context(nc.sbuf_tensor(f"var_eps_{tag}", [P, NT], F32))
        rstd = ctx.enter_context(nc.sbuf_tensor(f"rstd_{tag}", [P, NT], F32))
        xn = ctx.enter_context(nc.sbuf_tensor(f"xn_{tag}", [P, NT, D], F32))
        turned = ctx.enter_context(nc.psum_tensor(f"turned_{tag}", [P, NT, BANK], F32))
        stats_done = ctx.enter_context(nc.semaphore(f"stats_done_{tag}"))
        moments_done = ctx.enter_context(nc.semaphore(f"moments_done_{tag}"))
        eps_added = ctx.enter_context(nc.semaphore(f"eps_added_{tag}"))
        rstd_done = ctx.enter_context(nc.semaphore(f"rstd_done_{tag}"))
        normed = ctx.enter_context(nc.semaphore(f"normed_{tag}"))
        tile_turned = ctx.enter_context(nc.semaphore(f"tile_turned_{tag}"))
        block = ctx.enter_context(nc.Block())

        if clear:
            @block.sync
            def _(sp):
                clear_semaphores(nc, sp)

        if load is not None:
            @block.sync
            def _(sp):
                load(sp)

        @block.vector
        def _(dve):
            for t in range(NT):
                nc.vector.bn_stats(stats[:, t, :], k.x[:, t, :]).then_inc(stats_done, 1)
            for t in range(NT):
                dve.wait_ge(stats_done, t + 1)
                nc.vector.bn_aggr(moments[:, t, :], stats[:, t, :]).then_inc(moments_done, 1)
            dve.wait_ge(moments_done, NT)
            nc.vector.tensor_scalar(var_eps[:], moments[:, :, 1], EPS, None, ALU.add).then_inc(eps_added, 1)
            dve.wait_ge(rstd_done, 1)
            for t in range(NT):
                nc.vector.tensor_scalar(xn[:, t, :], k.x[:, t, :], moments[:, t, 0:1], rstd[:, t:t + 1],
                                        ALU.subtract, ALU.mult).then_inc(normed, 1)

        @block.gpsimd
        def _(pool):
            pool.wait_ge(eps_added, 1)
            nc.gpsimd.tensor_tensor(rstd[:], var_eps[:], k.minus_half[:, 0:1].broadcast_to([P, NT]),
                                    ALU.pow).then_inc(rstd_done, 1)

        @block.tensor
        def _(pe):
            for t in range(NT):
                pe.wait_ge(normed, t + 1)
                for c in range(C):
                    last = nc.tensor.transpose(turned[:, t, c * P:(c + 1) * P], xn[:, t, c * P:(c + 1) * P], k.ident)
                last.then_inc(tile_turned, 1)

        @block.scalar
        def _(act):
            for t in range(NT):
                act.wait_ge(tile_turned, t + 1)
                nc.scalar.activation(k.h_t[:, :, t * P:(t + 1) * P],
                                     turned[:, t, 0:D].rearrange("p (c n) -> p c n", c=C), ACT.Copy)


def load_stage(nc, k, src):
    with ExitStack() as ctx:
        mask_i = ctx.enter_context(nc.sbuf_tensor("mask_i", [NB, M], I32))
        unmasked = ctx.enter_context(nc.sbuf_tensor("unmasked", [NB, M], F32))
        count = ctx.enter_context(nc.sbuf_tensor("count", [NB, 1], F32))
        last_pos = ctx.enter_context(nc.sbuf_tensor("last_pos", [NB, 1], F32))
        diag = ctx.enter_context(nc.sbuf_tensor("diag", [NB, NB], F32))
        spread = ctx.enter_context(nc.psum_tensor("spread", [P, NB], F32))
        mask_in = ctx.enter_context(nc.semaphore("mask_in"))
        small_in = ctx.enter_context(nc.semaphore("small_in"))
        rest_in = ctx.enter_context(nc.semaphore("rest_in"))
        consts_set = ctx.enter_context(nc.semaphore("consts_set"))
        len_step = ctx.enter_context(nc.semaphore("len_step"))
        len_spread = ctx.enter_context(nc.semaphore("len_spread"))
        block = ctx.enter_context(nc.Block())

        @block.sync
        def _(sp):
            sp.dma_start(mask_i[:], src["mask"]).then_inc(mask_in, 16)
            sp.dma_start(k.x[:], src["x"].rearrange("(t p) d -> p t d", p=P)).then_inc(rest_in, 16)
            sp.dma_start(k.small[:], src["small"]).then_inc(small_in, 16)
            sp.dma_start(k.rows[:], src["rows"]).then_inc(rest_in, 16)
            sp.dma_start(k.early[:], src["early"]).then_inc(rest_in, 16)
            sp.dma_start(k.bo1[:], src["bo1"]).then_inc(rest_in, 16)
            sp.wait_ge(rest_in, 64)

        @block.vector
        def _(dve):
            nc.vector.memset(k.minus_half[:], -0.5)
            nc.vector.memset(k.ones[:], 1.0).then_inc(consts_set, 1)
            nc.vector.memset(k.log_s[:], -math.log(S))
            dve.wait_ge(mask_in, 16)
            nc.vector.tensor_scalar(unmasked[:], mask_i[:], -1.0, 1.0, ALU.mult, ALU.add).then_inc(len_step, 1)
            dve.wait_ge(len_step, 1)
            nc.vector.tensor_reduce(count[:], unmasked[:], AX, ALU.add).then_inc(len_step, 1)
            dve.wait_ge(len_step, 2)
            nc.vector.tensor_scalar(last_pos[:], count[:], -1.0, None, ALU.add).then_inc(len_step, 1)
            dve.wait_ge(len_step, 3)
            dve.wait_ge(small_in, 16)
            nc.vector.tensor_scalar(diag[:], k.ident[0:NB, 0:NB], last_pos[:, 0:1], None,
                                    ALU.mult).then_inc(len_step, 1)
            dve.wait_ge(len_spread, 1)
            nc.vector.tensor_copy(k.length[:], spread[:])

        @block.tensor
        def _(pe):
            pe.wait_ge(len_step, 4)
            pe.wait_ge(consts_set, 1)
            nc.tensor.matmul(spread[:], k.ones[0:NB, :], diag[:], start=True, stop=True).then_inc(len_spread, 1)


def positions_stage(nc, k, src):

    with ExitStack() as ctx:
        def sb(name, shape, dt=F32):
            return ctx.enter_context(nc.sbuf_tensor(name, shape, dt))

        def sem(name):
            return ctx.enter_context(nc.semaphore(name))

        wq, woff, wq_in, woff_in = k.wq0, k.woff0, k.wq0_in, k.woff0_in
        v = sb("where", [P, NB, PK])
        turns = sb("turns", [P, NB, PK])
        side = sb("side", [P, NB, PK])
        per_len = sb("per_len", [P, NB])
        far = sb("far", [P, NB * PK])
        far_any = sb("far_any", [P, 1])
        q_ps = ctx.enter_context(nc.psum_tensor("q_ps", [P, C, 2, 512], F32))
        off_ps = ctx.enter_context(nc.psum_tensor("off_ps", [P, 2, 512], F32))
        flag_ps = ctx.enter_context(nc.psum_tensor("flag_ps", [1, 1], F32))
        q_done = sem("q0_done")
        q_kept = sem("q0_kept")
        off_done = sem("off_done")
        step = sem("where_step")
        side_done = sem("row_step")
        flag_summed = sem("flag_summed")
        block = ctx.enter_context(nc.Block())

        @block.sync
        def _(sp):
            sp.wait_ge(k.iota_in, 16)

        @block.tensor
        def _(pe):
            pe.wait_ge(wq_in, 16)
            for e in range(C):
                for g in range(2):
                    for c in range(C):
                        last = nc.tensor.matmul(q_ps[:, e, g, :], wq[:, c, e * P:(e + 1) * P],
                                                k.h_t[:, c, g * 512:(g + 1) * 512], start=c == 0, stop=c == C - 1)
                    last.then_inc(q_done, 1)
            pe.wait_ge(woff_in, 16)
            pe.wait_ge(q_kept, 4)
            for b in range(NB):
                for r in range(2):
                    for c in range(C):
                        last = nc.tensor.matmul(
                            off_ps[r * S:(r + 1) * S, b // 8, (b % 8) * PK:(b % 8 + 1) * PK],
                            k.q0[:, c, b * S:(b + 1) * S], woff[:, c, r, :], start=c == 0, stop=c == C - 1)
            last.then_inc(off_done, 1)
            pe.wait_ge(step, 13)
            nc.tensor.matmul(flag_ps[:], far_any[:], k.ones[:, 0:1], start=True, stop=True).then_inc(flag_summed, 1)

        @block.scalar
        def _(act):
            for e in range(C):
                for g in range(2):
                    act.wait_ge(q_done, 2 * e + g + 1)
                    nc.scalar.activation(k.q0[:, e, g * 512:(g + 1) * 512], q_ps[:, e, g, :], ACT.Identity,
                                         bias=small(k, "bq")[:, e:e + 1]).then_inc(q_kept, 1)

        @block.vector
        def _(dve):
            def rep(ap):
                return ap.unsqueeze(1).broadcast_to([P, NB, PK])

            def by_batch(ap):
                return ap.unsqueeze(2).broadcast_to([P, NB, PK])

            length = by_batch(k.length[:])
            nc.vector.memset(k.pos[:, NB:NB + 1, :], 0.0)
            nc.vector.reciprocal(per_len[:], k.length[:])
            dve.wait_ge(off_done, 1)
            nc.vector.tensor_tensor(v[:].rearrange("p (a b) n -> p a b n", a=2),
                                    off_ps[:, :, 0:8 * PK].rearrange("p a (b n) -> p a b n", n=PK),
                                    rep(small(k, "boff")).rearrange("p (a b) n -> p a b n", a=2),
                                    ALU.add).then_inc(step, 1)
            dve.wait_ge(step, 1)
            nc.vector.tensor_tensor(v[:], v[:], rep(small(k, "ref")), ALU.add).then_inc(step, 1)
            dve.wait_ge(step, 2)
            nc.vector.tensor_scalar(v[:], v[:], small(k, "loc"), None, ALU.add).then_inc(step, 1)
            dve.wait_ge(step, 3)
            nc.vector.tensor_tensor(turns[:], v[:], by_batch(per_len[:]), ALU.mult).then_inc(step, 1)
            dve.wait_ge(step, 4)
            big = 1.5 * 2.0 ** 23
            nc.vector.tensor_scalar(turns[:], turns[:], big, big, ALU.add, ALU.subtract).then_inc(step, 1)
            dve.wait_ge(step, 5)
            nc.vector.tensor_tensor(turns[:], turns[:], length, ALU.mult).then_inc(step, 1)
            dve.wait_ge(step, 6)
            nc.vector.tensor_tensor(v[:], v[:], turns[:], ALU.subtract).then_inc(step, 1)
            dve.wait_ge(step, 7)
            nc.vector.tensor_tensor(side[:], v[:], length, ALU.mult).then_inc(step, 1)
            dve.wait_ge(step, 8)
            nc.vector.scalar_tensor_tensor(out=side[:], in0=side[:], scalar=0.0, in1=length, op0=ALU.is_lt,
                                           op1=ALU.mult).then_inc(step, 1)
            dve.wait_ge(step, 9)
            nc.vector.tensor_tensor(v[:], v[:], side[:], ALU.add).then_inc(step, 1)
            dve.wait_ge(step, 10)
            nc.vector.tensor_scalar(v[:], v[:], 1.0 / (M - 1), 2.0, ALU.mult, ALU.mult).then_inc(step, 1)
            dve.wait_ge(step, 11)
            nc.vector.tensor_scalar(v[:], v[:], 1.0, 1.0, ALU.subtract, ALU.add).then_inc(step, 1)
            dve.wait_ge(step, 12)
            nc.vector.tensor_scalar(v[:], v[:], float(M), -1.0, ALU.mult, ALU.add).then_inc(side_done, 1)
            dve.wait_ge(side_done, 1)
            nc.vector.tensor_scalar(k.pos[:, 0:NB, :], v[:], 0.5, None, ALU.mult).then_inc(side_done, 1)
            dve.wait_ge(side_done, 2)
            flat = k.pos[:, 0:NB, :].rearrange("p b n -> p (b n)")
            nc.vector.tensor_scalar(far[:], flat, float(LOW - 1), None, ALU.is_gt).then_inc(side_done, 1)
            dve.wait_ge(side_done, 3)
            nc.vector.scalar_tensor_tensor(out=far[:], in0=flat, scalar=float(HIGH), in1=far[:], op0=ALU.is_lt,
                                           op1=ALU.mult).then_inc(side_done, 1)
            dve.wait_ge(side_done, 4)
            nc.vector.tensor_reduce(far_any[:], far[:], AX, ALU.add).then_inc(step, 1)
            dve.wait_ge(flag_summed, 1)
            nc.vector.tensor_copy(k.far_count[:], flag_ps[:])




def near_attention(nc, k, src, ctx):
    def sb(name, shape, dt=F32):
        return ctx.enter_context(nc.sbuf_tensor(name, shape, dt))

    def ps(name, shape):
        return ctx.enter_context(nc.psum_tensor(name, shape, F32))

    def sem(name):
        return ctx.enter_context(nc.semaphore(name))

    wk, wv, w_in = k.wk0, k.wv0, k.wkv0_in
    win = [sb(f"win{s}", [P, C, WN]) for s in range(2)]
    kt = [sb(f"kt{s}", [P, C, WN]) for s in range(2)]
    vals = [sb(f"vals{s}", [P, D]) for s in range(2)]
    qblk = [sb(f"qblk{s}", [P, C, 8, S]) for s in range(2)]
    tent = [sb(f"tent{s}", [P, PK, WN]) for s in range(2)]
    hit = sb("hit", [P, PK, WN])
    share = sb("share", [P, PK, WN])
    turned = sb("turned0", [P, 2, 512])
    score = sb("score", [P, PK])
    top = sb("top0", [P, PAIRS0])
    shifted = sb("shifted", [P, PK])
    weight = sb("weight", [P, PK])
    total = sb("total0", [P, PAIRS0])
    inv = sb("inv0", [P, PAIRS0])
    attn = sb("attn0", [P, PK])
    kept = sb("kept", [P, C, 2, S])
    kv_ps = ps("kv_ps", [P, 512])
    s_ps = ps("s_ps", [P, 2, 512])
    w_ps = ps("w_ps", [P, 2, 512])
    o_ps = ps("o_ps", [P, C, P])
    win_in = [sem(f"win_in{s}") for s in range(2)]
    kv_done, kv_kept, q_masked = sem("kv_done"), sem("kv_kept"), sem("q_masked")
    scored, dist_done, dist_abs, tent_done = sem("scored"), sem("dist_done"), sem("dist_abs"), sem("tent_done")
    hit_done, soft = sem("hit_done"), sem("soft_step")
    shift_done, exp_done = sem("shift_done"), sem("exp_done")
    share_done, turned_done, turned_kept = sem("share_done"), sem("turned_done"), sem("turned_kept")
    out_done, out_masked, out_kept = sem("out_done"), sem("out_masked"), sem("out_kept")
    SOFT = 4
    HALVES = NB // 2
    HK = PK // 2

    def half_tents(s, h):
        return tent[s][:, h * HK:(h + 1) * HK, :]

    block = ctx.enter_context(nc.Block())

    def pairs_of_batches(eng, body):
        body(0, True, False)
        with eng.Fori(1, HALVES - 1) as i:
            body(i, False, False)
        body(HALVES - 1, False, True)

    @block.sync
    def _(sp):
        def load(b, s):
            ctx_b = src["ctx_t"][b]
            sp.dma_start(win[s][:, :, 0:LOW], ctx_b[:, :, 0:LOW]).then_inc(win_in[s], 16)
            sp.dma_start(win[s][:, :, LOW:WN], ctx_b[:, :, HIGH:M]).then_inc(win_in[s], 16)

        load(0, 0)
        load(1, 1)
        with sp.Fori(0, HALVES - 1) as i:
            for s in range(2):
                sp.wait_ge(kv_done, i * 2 + (s + 1))
                load(i * 2 + (s + 2), s)

    @block.tensor
    def _(pe):
        def keys_values(b, s, i):
            pe.wait_ge(win_in[s], i * 32 + 32)
            pe.wait_ge(kv_kept, b)
            for e in range(C):
                for c in range(C):
                    nc.tensor.matmul(kv_ps[:, e * WN:(e + 1) * WN], wk[:, c, e * P:(e + 1) * P], win[s][:, c, :],
                                     start=c == 0, stop=c == C - 1)
            for c in range(C):
                nc.tensor.matmul(kv_ps[:, C * WN:C * WN + D], win[s][:, c, :], wv[:, c, :], start=c == 0, stop=False)
            nc.tensor.matmul(kv_ps[:, C * WN:C * WN + D], k.ones[0:1, :], k.row("bv0"), start=False,
                             stop=True).then_inc(kv_done, 1)

        def scores(b, s):
            pe.wait_ge(kv_kept, b + 1)
            pe.wait_ge(q_masked, b + 1)
            pe.wait_ge(hit_done, b)
            for p in range(PAIRS0):
                c, j = divmod(p, 4)
                last = nc.tensor.matmul(s_ps[:, c, j * WN:(j + 1) * WN],
                                        qblk[s][:, c, 2 * j:2 * j + 2, :].rearrange("p h q -> p (h q)"),
                                        kt[s][:, c, :], start=True, stop=True)
            last.then_inc(scored, 1)

        def turn_shares(b, h, skip_wait):
            pe.wait_ge(share_done, b * 2 + (h + 1))
            if not skip_wait:
                pe.wait_ge(turned_kept, b * 2 + (h - 1))
            for j in range(4):
                for n in range(NK):
                    last = nc.tensor.matmul(w_ps[:, h, j * P:(j + 1) * P], share[:, (4 * h + j) * NK + n, :],
                                            k.ident, start=n == 0, stop=n == NK - 1)
            last.then_inc(turned_done, 1)

        def outputs(b, s):
            pe.wait_ge(out_masked, b)
            for p in range(PAIRS0):
                c, j = divmod(p, 4)
                if j == 0:
                    pe.wait_ge(turned_kept, b * 2 + (c + 1))
                last = nc.tensor.matmul(o_ps[32 * j:32 * j + 32, c, :], vals[s][:, 32 * p:32 * p + 32],
                                        turned[:, c, j * P:(j + 1) * P], start=True, stop=True)
            last.then_inc(out_done, 1)

        pe.wait_ge(w_in, 32)
        keys_values(0, 0, 0)
        scores(0, 0)

        def body(i, first, last):
            for s in range(2):
                b = i * 2 + s
                if not (last and s == 1):
                    keys_values(b + 1, 1 - s, i + s)
                    scores(b + 1, 1 - s)
                for h in range(2):
                    turn_shares(b, h, first and s == 0)
                outputs(b, s)

        pairs_of_batches(pe, body)

    @block.gpsimd
    def _(pool):
        def prepare(b, s, old):
            if old is not None:
                pool.wait_ge(scored, old)
            nc.gpsimd.tensor_tensor(
                qblk[s][:], k.q0[:, :, bass.ds(b * S, S)].unsqueeze(2).broadcast_to([P, C, 8, S]),
                small(k, "mask8").unsqueeze(1).unsqueeze(3).broadcast_to([P, C, 8, S]), ALU.mult).then_inc(q_masked, 1)
            for h in range(2):
                if old is not None:
                    pool.wait_ge(share_done, old * 2 + (h - 1))
                nc.gpsimd.tensor_tensor(
                    half_tents(s, h), small(k, "iota").unsqueeze(1).broadcast_to([P, HK, WN]),
                    k.pos[:, bass.ds(b, 1), h * HK:(h + 1) * HK].rearrange("p b n -> p (b n)")
                    .unsqueeze(2).broadcast_to([P, HK, WN]), ALU.subtract).then_inc(dist_done, 1)

        prepare(0, 0, None)

        def body(i, first, last):
            for s in range(2):
                b = i * 2 + s
                if not (last and s == 1):
                    prepare(b + 1, 1 - s, None if first and s == 0 else b)

        pairs_of_batches(pool, body)

    @block.scalar
    def _(act):
        def distances(b, s, h):
            act.wait_ge(dist_done, b * 2 + (h + 1))
            nc.scalar.activation(half_tents(s, h), half_tents(s, h), ACT.Abs).then_inc(dist_abs, 1)

        def tents(b, s, h):
            act.wait_ge(dist_abs, b * 2 + (h + 1))
            nc.scalar.activation(half_tents(s, h), half_tents(s, h), ACT.Relu, bias=1.0, scale=-1.0).then_inc(tent_done, 1)

        def keep_turned(b, h):
            act.wait_ge(turned_done, b * 2 + (h + 1))
            nc.scalar.activation(turned[:, h, :], w_ps[:, h, :], ACT.Copy).then_inc(turned_kept, 1)

        def keep_keys_values(b, s):
            act.wait_ge(kv_done, b + 1)
            for c in range(C):
                nc.scalar.activation(kt[s][:, c, :], kv_ps[:, c * WN:(c + 1) * WN], ACT.Identity,
                                     bias=small(k, "bk")[:, c:c + 1])
            nc.scalar.activation(vals[s][:], kv_ps[:, C * WN:C * WN + D], ACT.Copy).then_inc(kv_kept, 1)

        keep_keys_values(0, 0)
        for h in range(2):
            distances(0, 0, h)
            tents(0, 0, h)

        def body(i, first, last):
            for s in range(2):
                b = i * 2 + s
                after, before = not (last and s == 1), not (first and s == 0)
                if after:
                    distances(b + 1, 1 - s, 0)
                    tents(b + 1, 1 - s, 0)
                if before:
                    keep_turned(b - 1, 0)
                if after:
                    distances(b + 1, 1 - s, 1)
                if before:
                    keep_turned(b - 1, 1)
                act.wait_ge(shift_done, b + 1)
                nc.scalar.activation(weight[:], shifted[:], ACT.Exp).then_inc(exp_done, 1)
                if after:
                    tents(b + 1, 1 - s, 1)
                    keep_keys_values(b + 1, 1 - s)

        pairs_of_batches(act, body)
        for h in range(2):
            keep_turned(NB - 1, h)

    @block.vector
    def _(dve):
        def keep_outputs(b):
            dve.wait_ge(out_done, b + 1)
            if not isinstance(b, int) or b > 0:
                dve.wait_ge(out_kept, b + 0)
            nc.vector.tensor_tensor(
                kept[:], o_ps[:].rearrange("p c (r q) -> p c r q", r=2),
                small(k, "mask2").unsqueeze(1).unsqueeze(3).broadcast_to([P, C, 2, S]),
                ALU.mult).then_inc(out_masked, 1)
            dve.wait_ge(out_masked, b + 1)
            nc.vector.tensor_tensor(k.ctx_t[:, :, bass.ds(b * S, S)], kept[:, :, 0, :], kept[:, :, 1, :],
                                    ALU.add).then_inc(out_kept, 1)

        def by_pair(ap):
            return ap.unsqueeze(2).broadcast_to([P, PAIRS0, NK])

        def paired(t):
            return t[:].rearrange("p (a n) -> p a n", n=NK)

        def body(i, first, last):
            for s in range(2):
                b = i * 2 + s
                at = b * SOFT
                dve.wait_ge(tent_done, b * 2 + 2)
                dve.wait_ge(scored, b + 1)
                for n in range(PK):
                    c, j = divmod(n // NK, 4)
                    last_hit = nc.vector.scalar_tensor_tensor(
                        out=hit[:, n, :], in0=tent[s][:, n, :], scalar=1.0, in1=s_ps[:, c, j * WN:(j + 1) * WN],
                        op0=ALU.mult, op1=ALU.mult, accum_out=score[:, n:n + 1])
                last_hit.then_inc(hit_done, 1)
                dve.wait_ge(hit_done, b + 1)
                nc.vector.tensor_reduce(top[:], paired(score), AX, ALU.max).then_inc(soft, 1)
                dve.wait_ge(soft, at + 1)
                nc.vector.tensor_tensor(paired(shifted), paired(score), by_pair(top[:]),
                                        ALU.subtract).then_inc(shift_done, 1)
                dve.wait_ge(exp_done, b + 1)
                nc.vector.tensor_reduce(total[:], paired(weight), AX, ALU.add).then_inc(soft, 1)
                dve.wait_ge(soft, at + 2)
                nc.vector.reciprocal(inv[:], total[:]).then_inc(soft, 1)
                dve.wait_ge(soft, at + 3)
                nc.vector.scalar_tensor_tensor(out=paired(attn), in0=paired(weight), scalar=0.5, in1=by_pair(inv[:]),
                                               op0=ALU.mult, op1=ALU.mult).then_inc(soft, 1)
                dve.wait_ge(soft, at + 4)
                for h in range(2):
                    n = PK // 2
                    if not (first and s == 0):
                        dve.wait_ge(turned_done, b * 2 + (h - 1))
                    nc.vector.tensor_tensor(share[:, h * n:(h + 1) * n, :], tent[s][:, h * n:(h + 1) * n, :],
                                            attn[:, h * n:(h + 1) * n].unsqueeze(2).broadcast_to([P, n, WN]),
                                            ALU.mult).then_inc(share_done, 1)
                if not (first and s == 0):
                    keep_outputs(b - 1)

        pairs_of_batches(dve, body)
        keep_outputs(NB - 1)


def far_attention(nc, k, src):
    with ExitStack() as ctx:
        def sb(name, shape, dt=F32):
            return ctx.enter_context(nc.sbuf_tensor(f"far_{name}", shape, dt))

        def ps(name, shape):
            return ctx.enter_context(nc.psum_tensor(f"far_{name}", shape, F32))

        def sem(name):
            return ctx.enter_context(nc.semaphore(f"far_{name}"))

        wk, wv, w_in = k.wk0, k.wv0, k.wkv0_in
        win, win2 = sb("win", [P, C, WN]), sb("win2", [P, C, WN])
        kt, vals = sb("kt", [P, C, WN]), sb("vals", [P, D])
        qblk = sb("qblk", [P, C, 8, S])
        tent, hit = sb("tent", [P, PK, WN]), sb("hit", [P, PK, WN])
        tent2, share = sb("tent2", [P, PK, WN]), sb("share", [P, PK, WN])
        turned = sb("turned", [P, 2, 512])
        part, score, shifted, weight, attn = (sb(n, [P, PK]) for n in ("part", "score", "shifted", "weight", "attn"))
        top, total, inv = (sb(n, [P, PAIRS0]) for n in ("top", "total", "inv"))
        kept, out_part, out_sum = sb("kept", [P, C, 2, S]), sb("out_part", [P, C, S]), sb("out_sum", [P, C, S])
        k_ps, v_ps, s_ps = ps("k_ps", [P, C, WN]), ps("v_ps", [P, D]), ps("s_ps", [P, 2, BANK])
        w_ps, o_ps = ps("w_ps", [P, 2, BANK]), ps("o_ps", [P, C, P])
        win_in, win2_in = sem("win_in"), sem("win2_in")
        k_done, k_kept, q_masked, scored = sem("k_done"), sem("k_kept"), sem("q_masked"), sem("scored")
        dist, dist_abs, tent_done, hit_done = sem("dist"), sem("dist_abs"), sem("tent_done"), sem("hit_done")
        part_done, score_done, soft, shift, exp_done = (
            sem(n) for n in ("part_done", "score_done", "soft", "shift", "exp_done"))
        attn_done, v_done, v_kept, dist2, dist2_abs, tent2_done = (
            sem(n) for n in ("attn_done", "v_done", "v_kept", "dist2", "dist2_abs", "tent2_done"))
        share_done, turned_done, turned_kept, out_done, masked, out_step, out_added, batch_out = (
            sem(n) for n in ("share_done", "turned_done", "turned_kept", "out_done", "masked", "out_step",
                             "out_added", "batch_out"))
        block = ctx.enter_context(nc.Block())

        def windows(eng, b, body):
            with eng.Fori(0, NWIN) as j:
                body(j, b * NWIN + j)

        @block.sync
        def _(sp):
            with sp.Fori(0, NB) as b:
                def for_keys(j, n):
                    sp.wait_ge(k_done, n + 1)
                    sp.dma_start(win[:], src["ctx_t"][b][:, :, bass.ds(j * WN, WN)]).then_inc(win_in, 16)

                def for_values(j, n):
                    sp.wait_ge(v_done, n + 1)
                    sp.dma_start(win2[:], src["ctx_t"][b][:, :, bass.ds(j * WN, WN)]).then_inc(win2_in, 16)

                windows(sp, b, for_keys)
                windows(sp, b, for_values)

        @block.tensor
        def _(pe):
            for first in (k_done, scored, v_done, turned_done, out_done):
                pe.sem_inc(first, 1)
            pe.wait_ge(w_in, 32)
            with pe.Fori(0, NB) as b:
                def scores(j, n):
                    pe.wait_ge(win_in, n * 16 + 16)
                    for e in range(C):
                        for c in range(C):
                            last = nc.tensor.matmul(k_ps[:, e, :], wk[:, c, e * P:(e + 1) * P], win[:, c, :],
                                                    start=c == 0, stop=c == C - 1)
                    last.then_inc(k_done, 1)
                    pe.wait_ge(k_kept, n + 1)
                    pe.wait_ge(q_masked, b + 1)
                    pe.wait_ge(hit_done, n + 1)
                    for p in range(PAIRS0):
                        c, i = divmod(p, 4)
                        last = nc.tensor.matmul(s_ps[:, c, i * WN:(i + 1) * WN],
                                                qblk[:, c, 2 * i:2 * i + 2, :].rearrange("p h q -> p (h q)"),
                                                kt[:, c, :], start=True, stop=True)
                    last.then_inc(scored, 1)

                def outputs(j, n):
                    pe.wait_ge(win2_in, n * 16 + 16)
                    for c in range(C):
                        nc.tensor.matmul(v_ps[:], win2[:, c, :], wv[:, c, :], start=c == 0, stop=False)
                    nc.tensor.matmul(v_ps[:], k.ones[0:1, :], k.row("bv0"), start=False, stop=True).then_inc(v_done, 1)
                    pe.wait_ge(share_done, n + 2)
                    for p in range(PAIRS0):
                        for i in range(NK):
                            last = nc.tensor.matmul(w_ps[:, p // 4, (p % 4) * P:(p % 4 + 1) * P],
                                                    share[:, p * NK + i, :], k.ident, start=i == 0, stop=i == NK - 1)
                    last.then_inc(turned_done, 1)
                    pe.wait_ge(v_kept, n + 1)
                    pe.wait_ge(turned_kept, n + 1)
                    pe.wait_ge(masked, n + 1)
                    for p in range(PAIRS0):
                        c, i = divmod(p, 4)
                        last = nc.tensor.matmul(o_ps[32 * i:32 * i + 32, c, :], vals[:, 32 * p:32 * p + 32],
                                                turned[:, c, i * P:(i + 1) * P], start=True, stop=True)
                    last.then_inc(out_done, 1)

                windows(pe, b, scores)
                windows(pe, b, outputs)

        @block.gpsimd
        def _(pool):
            with pool.Fori(0, NB) as b:
                def distances(out, j, done):
                    nc.gpsimd.tensor_tensor(
                        out[:], k.iota_all[:, bass.ds(j * WN, WN)].unsqueeze(1).broadcast_to([P, PK, WN]),
                        k.pos[:, bass.ds(b, 1), :].rearrange("p b n -> p (b n)").unsqueeze(2).broadcast_to([P, PK, WN]),
                        ALU.subtract).then_inc(done, 1)

                def for_scores(j, n):
                    pool.wait_ge(hit_done, n + 1)
                    distances(tent, j, dist)

                def for_outputs(j, n):
                    pool.wait_ge(share_done, n + 1)
                    distances(tent2, j, dist2)

                pool.wait_ge(scored, b * NWIN + 1)
                nc.gpsimd.tensor_tensor(
                    qblk[:], k.q0[:, :, bass.ds(b * S, S)].unsqueeze(2).broadcast_to([P, C, 8, S]),
                    small(k, "mask8").unsqueeze(1).unsqueeze(3).broadcast_to([P, C, 8, S]),
                    ALU.mult).then_inc(q_masked, 1)
                windows(pool, b, for_scores)
                windows(pool, b, for_outputs)

        @block.scalar
        def _(act):
            with act.Fori(0, NB) as b:
                def for_scores(j, n):
                    act.wait_ge(k_done, n + 2)
                    for c in range(C):
                        last = nc.scalar.activation(kt[:, c, :], k_ps[:, c, :], ACT.Identity,
                                                    bias=small(k, "bk")[:, c:c + 1])
                    last.then_inc(k_kept, 1)
                    act.wait_ge(dist, n + 1)
                    nc.scalar.activation(tent[:], tent[:], ACT.Abs).then_inc(dist_abs, 1)
                    act.wait_ge(dist_abs, n + 1)
                    nc.scalar.activation(tent[:], tent[:], ACT.Relu, bias=1.0, scale=-1.0).then_inc(tent_done, 1)

                def for_outputs(j, n):
                    act.wait_ge(v_done, n + 2)
                    act.wait_ge(out_done, n + 1)
                    nc.scalar.activation(vals[:], v_ps[:], ACT.Copy).then_inc(v_kept, 1)
                    act.wait_ge(dist2, n + 1)
                    nc.scalar.activation(tent2[:], tent2[:], ACT.Abs).then_inc(dist2_abs, 1)
                    act.wait_ge(dist2_abs, n + 1)
                    nc.scalar.activation(tent2[:], tent2[:], ACT.Relu, bias=1.0, scale=-1.0).then_inc(tent2_done, 1)
                    act.wait_ge(turned_done, n + 2)
                    nc.scalar.activation(turned[:], w_ps[:], ACT.Copy).then_inc(turned_kept, 1)

                windows(act, b, for_scores)
                act.wait_ge(shift, b + 1)
                nc.scalar.activation(weight[:], shifted[:], ACT.Exp).then_inc(exp_done, 1)
                windows(act, b, for_outputs)

        @block.vector
        def _(dve):
            def paired(t):
                return t[:].rearrange("p (a n) -> p a n", n=NK)

            def by_pair(t):
                return t[:].unsqueeze(2).broadcast_to([P, PAIRS0, NK])

            for first in (hit_done, part_done, share_done, masked):
                dve.sem_inc(first, 1)
            nc.vector.memset(score[:], 0.0).then_inc(score_done, 1)
            nc.vector.memset(out_sum[:], 0.0).then_inc(out_added, 1)
            with dve.Fori(0, NB) as b:
                def scores(j, n):
                    dve.wait_ge(tent_done, n + 1)
                    dve.wait_ge(scored, n + 2)
                    dve.wait_ge(part_done, n + 1)
                    nc.vector.tensor_tensor(
                        hit[:].rearrange("p (a n) m -> p a n m", n=NK), tent[:].rearrange("p (a n) m -> p a n m", n=NK),
                        s_ps[:].rearrange("p c (i m) -> p (c i) m", m=WN).unsqueeze(2).broadcast_to(
                            [P, PAIRS0, NK, WN]), ALU.mult).then_inc(hit_done, 1)
                    dve.wait_ge(hit_done, n + 2)
                    nc.vector.tensor_reduce(part[:], hit[:], AX, ALU.add).then_inc(part_done, 1)
                    dve.wait_ge(part_done, n + 2)
                    dve.wait_ge(score_done, n + (b + 1))
                    nc.vector.tensor_tensor(score[:], score[:], part[:], ALU.add).then_inc(score_done, 1)

                def outputs(j, n):
                    dve.wait_ge(soft, b * 5 + 4)
                    dve.wait_ge(tent2_done, n + 1)
                    dve.wait_ge(turned_done, n + 1)
                    nc.vector.tensor_tensor(share[:], tent2[:], attn[:].unsqueeze(2).broadcast_to([P, PK, WN]),
                                            ALU.mult).then_inc(share_done, 1)
                    dve.wait_ge(out_done, n + 2)
                    nc.vector.tensor_tensor(
                        kept[:], o_ps[:].rearrange("p c (r q) -> p c r q", r=2),
                        small(k, "mask2").unsqueeze(1).unsqueeze(3).broadcast_to([P, C, 2, S]),
                        ALU.mult).then_inc(masked, 1)
                    dve.wait_ge(masked, n + 2)
                    nc.vector.tensor_tensor(out_part[:], kept[:, :, 0, :], kept[:, :, 1, :],
                                            ALU.add).then_inc(out_step, 1)
                    dve.wait_ge(out_step, n + 1)
                    dve.wait_ge(out_added, n + (b + 1))
                    nc.vector.tensor_tensor(out_sum[:], out_sum[:], out_part[:], ALU.add).then_inc(out_added, 1)

                windows(dve, b, scores)
                at = b * 5
                dve.wait_ge(score_done, b * (NWIN + 1) + (NWIN + 1))
                nc.vector.tensor_reduce(top[:], paired(score), AX, ALU.max).then_inc(soft, 1)
                dve.wait_ge(soft, at + 1)
                nc.vector.tensor_tensor(paired(shifted), paired(score), by_pair(top), ALU.subtract).then_inc(shift, 1)
                dve.wait_ge(shift, b + 1)
                nc.vector.memset(score[:], 0.0).then_inc(score_done, 1)
                dve.wait_ge(exp_done, b + 1)
                nc.vector.tensor_reduce(total[:], paired(weight), AX, ALU.add).then_inc(soft, 1)
                dve.wait_ge(soft, at + 2)
                nc.vector.reciprocal(inv[:], total[:]).then_inc(soft, 1)
                dve.wait_ge(soft, at + 3)
                nc.vector.scalar_tensor_tensor(out=paired(attn), in0=paired(weight), scalar=0.5, in1=by_pair(inv),
                                               op0=ALU.mult, op1=ALU.mult).then_inc(soft, 1)
                windows(dve, b, outputs)
                dve.wait_ge(out_added, b * (NWIN + 1) + (NWIN + 1))
                nc.vector.tensor_copy(k.ctx_t[:, :, bass.ds(b * S, S)], out_sum[:]).then_inc(soft, 1)
                dve.wait_ge(soft, at + 5)
                nc.vector.memset(out_sum[:], 0.0).then_inc(out_added, 1)


def local_attention(nc, k, src):
    far = nc.values_load(k.far_count[0:1, 0:1], min_val=0, max_val=1 << 23)
    with nc.If(far < 1):
        with ExitStack() as ctx:
            near_attention(nc, k, src, ctx)
    with nc.Else():
        far_attention(nc, k, src)


def after_local(nc, k, src):
    with ExitStack() as ctx:
        wo = ctx.enter_context(nc.sbuf_tensor("wo0", [P, C, D], F32))
        y_ps = ctx.enter_context(nc.psum_tensor("y0_ps", [P, NT, BANK], F32))
        wo_in = ctx.enter_context(nc.semaphore("wo0_in"))
        y_done = ctx.enter_context(nc.semaphore("y0_done"))
        block = ctx.enter_context(nc.Block())

        @block.sync
        def _(sp):
            sp.dma_start(wo[:], src["wo0"]).then_inc(wo_in, 16)

        @block.tensor
        def _(pe):
            pe.wait_ge(wo_in, 16)
            for t in range(NT):
                for c in range(C):
                    nc.tensor.matmul(y_ps[:, t, 0:D], k.ctx_t[:, c, t * P:(t + 1) * P], wo[:, c, :],
                                     start=c == 0, stop=False)
                nc.tensor.matmul(y_ps[:, t, 0:D], k.ones[0:1, :], k.row("bo0"), start=False,
                                 stop=True).then_inc(y_done, 1)

        @block.vector
        def _(dve):
            for t in range(NT):
                dve.wait_ge(y_done, t + 1)
                nc.vector.tensor_tensor(k.x[:, t, :], k.x[:, t, :], y_ps[:, t, 0:D], ALU.add)


def store_stage(nc, k, out):
    with ExitStack() as ctx:
        stored = ctx.enter_context(nc.semaphore("stored"))
        block = ctx.enter_context(nc.Block())

        @block.sync
        def _(sp):
            sp.dma_start(out.rearrange("(t p) d -> p t d", p=P), k.x[:]).then_inc(stored, 16)
            sp.wait_ge(stored, 16)


def self_attention(nc, k, src):
    with ExitStack() as ctx:
        def sb(name, shape, dt=F32):
            return ctx.enter_context(nc.sbuf_tensor(name, shape, dt))

        def bank(name):
            return [ctx.enter_context(nc.psum_tensor(f"{name}{s}", [P, BANK], F32)) for s in range(2)]

        def sem(name):
            return ctx.enter_context(nc.semaphore(name))

        w = {n: sb(f"{n}a_w", [P, C, D]) for n in ("q", "k", "v", "o")}
        h = [sb(f"ha{s}", [P, C, P]) for s in range(2)]
        stats = [sb(f"stats_qk{s}", [P, 2, 6]) for s in range(2)]
        moments = [sb(f"moments_qk{s}", [P, 2, 2]) for s in range(2)]
        var_eps = [sb(f"var_eps_qk{s}", [P, 2]) for s in range(2)]
        rstd = [sb(f"rstd_qk{s}", [P, 2]) for s in range(2)]
        qkn = [sb(f"qkn{s}", [P, 2, D]) for s in range(2)]
        qkt = [sb(f"qkt{s}", [P, 2, C, P]) for s in range(2)]
        v = [sb(f"va{s}", [P, D]) for s in range(2)]
        attn = [sb(f"attn_a{s}", [P, P]) for s in range(2)]
        own = [sb(f"own{s}", [P, P]) for s in range(2)]
        ot = [sb(f"ot_a{s}", [P, C, P]) for s in range(2)]
        scaled = [sb(f"scaled{s}", [P, D]) for s in range(2)]
        spare = sb("spare", [P, 1])
        qk_ps, vy_ps, t_ps, s_ps = bank("qk_ps"), bank("vy_ps"), bank("t_ps"), bank("sa_ps")
        w_in = sem("wa_in")
        h_copied, qk_done, v_done = sem("h_copied"), sem("qk_done"), sem("va_done")
        stat, aggr, eps_added, rstd_done, normed = (sem(f"{n}_qk") for n in ("stat", "aggr", "eps", "rstd", "normed"))
        v_kept, qk_turned, qk_kept, scored = sem("va_kept"), sem("qk_turned"), sem("qk_kept"), sem("a_scored")
        gated, masked, o_done, o_kept = sem("a_gated"), sem("a_masked"), sem("a_o_done"), sem("a_o_kept")
        y_done, y_scaled, x_added = sem("a_y_done"), sem("a_y_scaled"), sem("a_x_added")
        block = ctx.enter_context(nc.Block())

        @block.sync
        def _(sp):
            for n, a in (("q", src["wqa"]), ("k", src["wka"]), ("v", src["wva"]), ("o", src["woa"])):
                sp.dma_start(w[n][:], a).then_inc(w_in, 16)

        @block.gpsimd
        def _(pool):
            with pool.Fori(0, NT // 2) as i:
                for s in range(2):
                    pool.wait_ge(x_added, i * 2 + 2)
                    nc.gpsimd.tensor_copy(h[s][:], k.h_t[:, :, bass.ds(i * 2 * P + s * P, P)]).then_inc(h_copied, 1)
                for s in range(2):
                    pool.wait_ge(eps_added, i * 2 + (s + 1))
                    nc.gpsimd.tensor_tensor(rstd[s][:], var_eps[s][:], k.minus_half[:, 0:1].broadcast_to([P, 2]),
                                            ALU.pow).then_inc(rstd_done, 1)

        @block.tensor
        def _(pe):
            pe.wait_ge(w_in, 64)
            with pe.Fori(0, NT // 2) as i:
                for s in range(2):
                    pe.wait_ge(h_copied, i * 2 + (s + 1))
                    for j, n in enumerate("qk"):
                        for c in range(C):
                            nc.tensor.matmul(qk_ps[s][:, j * D:(j + 1) * D], h[s][:, c, :], w[n][:, c, :],
                                             start=c == 0, stop=False)
                        last = nc.tensor.matmul(qk_ps[s][:, j * D:(j + 1) * D], k.ones[0:1, :], k.row(f"b{n}a"),
                                                start=False, stop=True)
                    last.then_inc(qk_done, 1)
                    for c in range(C):
                        nc.tensor.matmul(vy_ps[s][:, 0:D], h[s][:, c, :], w["v"][:, c, :], start=c == 0, stop=False)
                    nc.tensor.matmul(vy_ps[s][:, 0:D], k.ones[0:1, :], k.row("bva"), start=False,
                                     stop=True).then_inc(v_done, 1)
                for s in range(2):
                    pe.wait_ge(normed, i * 2 + (s + 1))
                    for j in range(2):
                        for c in range(C):
                            last = nc.tensor.transpose(t_ps[s][:, (j * C + c) * P:(j * C + c + 1) * P],
                                                       qkn[s][:, j, c * P:(c + 1) * P], k.ident)
                    last.then_inc(qk_turned, 1)
                for s in range(2):
                    pe.wait_ge(qk_kept, i * 2 + (s + 1))
                    for c in range(C):
                        last = nc.tensor.matmul(s_ps[s][:, 0:P], qkt[s][:, 1, c, :], qkt[s][:, 0, c, :],
                                                start=c == 0, stop=c == C - 1)
                    last.then_inc(scored, 1)
                for s in range(2):
                    pe.wait_ge(masked, i * 2 + (s + 1))
                    pe.wait_ge(v_kept, i * 2 + (s + 1))
                    for c in range(C):
                        last = nc.tensor.matmul(t_ps[s][:, c * P:(c + 1) * P], v[s][:, c * P:(c + 1) * P], own[s][:],
                                                start=True, stop=True)
                    last.then_inc(o_done, 1)
                for s in range(2):
                    pe.wait_ge(o_kept, i * 2 + (s + 1))
                    for c in range(C):
                        nc.tensor.matmul(vy_ps[s][:, 0:D], ot[s][:, c, :], w["o"][:, c, :], start=c == 0, stop=False)
                    nc.tensor.matmul(vy_ps[s][:, 0:D], k.ones[0:1, :], k.row("boa"), start=False,
                                     stop=True).then_inc(y_done, 1)

        @block.scalar
        def _(act):
            with act.Fori(0, NT // 2) as i:
                for s in range(2):
                    act.wait_ge(v_done, i * 2 + (s + 1))
                    nc.scalar.activation(v[s][:], vy_ps[s][:, 0:D], ACT.Copy).then_inc(v_kept, 1)
                for s in range(2):
                    act.wait_ge(qk_turned, i * 2 + (s + 1))
                    nc.scalar.activation(qkt[s][:].rearrange("p j c n -> p (j c n)"), t_ps[s][:],
                                         ACT.Copy).then_inc(qk_kept, 1)
                for s in range(2):
                    act.wait_ge(scored, i * 2 + (s + 1))
                    nc.scalar.activation(attn[s][:], s_ps[s][:, 0:P], ACT.Sigmoid, bias=k.log_s[:, 0:1],
                                         scale=1.0 / math.sqrt(D)).then_inc(gated, 1)
                for s in range(2):
                    act.wait_ge(o_done, i * 2 + (s + 1))
                    nc.scalar.activation(ot[s][:].rearrange("p c n -> p (c n)"), t_ps[s][:, 0:D],
                                         ACT.Copy).then_inc(o_kept, 1)

        @block.vector
        def _(dve):
            dve.sem_inc(x_added, 2)
            with dve.Fori(0, NT // 2) as i:
                for s in range(2):
                    dve.wait_ge(qk_done, i * 2 + (s + 1))
                    for j in range(2):
                        nc.vector.bn_stats(stats[s][:, j, :], qk_ps[s][:, j * D:(j + 1) * D]).then_inc(stat, 1)
                dve.wait_ge(stat, i * 4 + 4)
                nc.vector.memset(spare[:], 0.0)
                for s in range(2):
                    for j in range(2):
                        nc.vector.bn_aggr(moments[s][:, j, :], stats[s][:, j, :]).then_inc(aggr, 1)
                for s in range(2):
                    dve.wait_ge(aggr, i * 4 + (2 * s + 2))
                    nc.vector.tensor_scalar(var_eps[s][:], moments[s][:, :, 1], EPS, None,
                                            ALU.add).then_inc(eps_added, 1)
                for s in range(2):
                    dve.wait_ge(rstd_done, i * 2 + (s + 1))
                    for j in range(2):
                        last = nc.vector.tensor_scalar(qkn[s][:, j, :], qk_ps[s][:, j * D:(j + 1) * D],
                                                       moments[s][:, j, 0:1], rstd[s][:, j:j + 1],
                                                       ALU.subtract, ALU.mult)
                    last.then_inc(normed, 1)
                for s in range(2):
                    dve.wait_ge(gated, i * 2 + (s + 1))
                    nc.vector.tensor_tensor(own[s][:], attn[s][:], small(k, "same"), ALU.mult).then_inc(masked, 1)
                for s in range(2):
                    dve.wait_ge(y_done, i * 2 + (s + 1))
                    nc.vector.tensor_tensor(scaled[s][:], vy_ps[s][:, 0:D], small(k, "ls"),
                                            ALU.mult).then_inc(y_scaled, 1)
                for s in range(2):
                    dve.wait_ge(y_scaled, i * 2 + (s + 1))
                    xt = k.x[:, bass.ds(i * 2 + s, 1), :].rearrange("p a d -> p (a d)")
                    nc.vector.tensor_tensor(xt, xt, scaled[s][:], ALU.add).then_inc(x_added, 1)


def route(nc, k, layer, experts_w):
    n, top_n = (E0, 2) if layer == 0 else (E1, TOP1)
    PAD, MARK = -1e30, 1e30
    with ExitStack() as ctx:
        def sb(name, shape, dt=F32):
            return ctx.enter_context(nc.sbuf_tensor(f"{name}_r{layer}", shape, dt))

        def sem(name):
            return ctx.enter_context(nc.semaphore(f"{name}_r{layer}"))

        square = sb("square", [P, C, T]) if layer == 0 else None
        w = sb("w", [P, C, n])
        mean_sq, rms = sb("mean_sq", [P, NT]), sb("rms", [P, NT])
        logit = sb("logit", [P, NT, n])
        top, total, inv = sb("top", [P, NT]), sb("total", [P, NT]), sb("inv", [P, NT])
        shifted, weight, prob = sb("shifted", [P, NT, n]), sb("weight", [P, NT, n]), sb("prob", [P, NT, n])
        ranked, marked = sb("ranked", [P, NT, n + 8]), sb("marked", [P, NT, n + 8])
        largest = sb("largest", [P, NT, 8])
        chosen, none, kept = sb("chosen", [P, NT, n]), sb("none", [P, NT]), sb("kept", [P, NT, n])
        l_ps = ctx.enter_context(nc.psum_tensor(f"l_ps_r{layer}", [P, NT, 64], F32))
        squared, w_scaled, logits_done = sem("squared"), sem("w_scaled"), sem("logits_done")
        rms_in, rms_done, step, shift_done, exp_done = (sem(x) for x in ("rms_in", "rms_done", "step", "shift", "exp"))
        padded, maxed, cut, marked_done = sem("padded"), sem("maxed"), sem("cut"), sem("marked")
        block = ctx.enter_context(nc.Block())

        @block.scalar
        def _(act):
            if layer == 0:
                nc.scalar.activation(square[:], k.h_t[:], ACT.Square).then_inc(squared, 1)
            experts_w.first_hi(act, k.h_t)
            act.wait_ge(shift_done, 1)
            nc.scalar.activation(weight[:], shifted[:], ACT.Exp).then_inc(exp_done, 1)

        @block.gpsimd
        def _(pool):
            experts_w.first_lo(pool)
            if layer == 0:
                pool.wait_ge(rms_in, 1)
                nc.gpsimd.tensor_tensor(rms[:], mean_sq[:], k.minus_half[:, 0:1].broadcast_to([P, NT]),
                                        ALU.pow).then_inc(rms_done, 1)

        @block.tensor
        def _(pe):
            rw = w if layer == 0 else small(k, "rw1").rearrange("p (c e) -> p c e", c=C)
            if layer == 0:
                pe.wait_ge(w_scaled, 1)
                pe.wait_ge(squared, 1)
            for t in range(NT):
                for c in range(C):
                    last = nc.tensor.matmul(l_ps[:, t, 0:n], k.h_t[:, c, t * P:(t + 1) * P], rw[:, c, :],
                                            start=c == 0, stop=c == C - 1)
                if layer == 0:
                    for c in range(C):
                        last = nc.tensor.matmul(l_ps[:, t, n:n + 1], square[:, c, t * P:(t + 1) * P],
                                                k.ones[:, 0:1], start=c == 0, stop=c == C - 1)
            last.then_inc(logits_done, 1)

        @block.vector
        def _(dve):
            def over(ap):
                return ap.unsqueeze(2).broadcast_to([P, NT, n])

            nc.vector.memset(ranked[:, :, n:n + 8], PAD).then_inc(padded, 1)
            if layer == 0:
                nc.vector.tensor_tensor(w[:], small(k, "rw0").rearrange("p (c e) -> p c e", c=C),
                                        small(k, "rscale").unsqueeze(2).broadcast_to([P, C, n]),
                                        ALU.mult).then_inc(w_scaled, 1)
            experts_w.tokens_lo(dve, k.h_t)
            if layer == 0:
                dve.wait_ge(logits_done, 1)
                nc.vector.tensor_scalar(mean_sq[:], l_ps[:, :, n], 1.0 / D, 1e-6, ALU.mult,
                                        ALU.add).then_inc(rms_in, 1)
                dve.wait_ge(rms_done, 1)
                nc.vector.scalar_tensor_tensor(out=logit[:], in0=l_ps[:, :, 0:n], scalar=1.0 / math.sqrt(D),
                                               in1=over(rms[:]), op0=ALU.mult, op1=ALU.mult).then_inc(step, 1)
            else:
                dve.wait_ge(logits_done, 1)
                nc.vector.tensor_tensor(logit[:], l_ps[:, :, 0:n],
                                        small(k, "rb1").unsqueeze(1).broadcast_to([P, NT, n]),
                                        ALU.add).then_inc(step, 1)
            dve.wait_ge(step, 1)
            nc.vector.tensor_reduce(top[:], logit[:], AX, ALU.max).then_inc(step, 1)
            dve.wait_ge(step, 2)
            nc.vector.tensor_tensor(shifted[:], logit[:], over(top[:]), ALU.subtract).then_inc(shift_done, 1)
            dve.wait_ge(exp_done, 1)
            nc.vector.tensor_reduce(total[:], weight[:], AX, ALU.add).then_inc(step, 1)
            dve.wait_ge(step, 3)
            nc.vector.reciprocal(inv[:], total[:]).then_inc(step, 1)
            dve.wait_ge(step, 4)
            nc.vector.tensor_tensor(prob[:], weight[:], over(inv[:]), ALU.mult).then_inc(step, 1)
            dve.wait_ge(step, 5)
            nc.vector.tensor_copy(ranked[:, :, 0:n], logit[:] if layer == 0 else prob[:]).then_inc(step, 1)
            dve.wait_ge(step, 6)
            dve.wait_ge(padded, 1)
            for t in range(NT):
                nc.vector.max(largest[:, t, :], ranked[:, t, :]).then_inc(maxed, 1)
            dve.wait_ge(maxed, NT)
            nc.vector.memset(largest[:, :, top_n:8], PAD).then_inc(cut, 1)
            dve.wait_ge(cut, 1)
            for t in range(NT):
                nc.vector.match_replace(marked[:, t, :], largest[:, t, :], ranked[:, t, :],
                                        MARK).then_inc(marked_done, 1)
            dve.wait_ge(marked_done, NT)
            nc.vector.tensor_scalar(chosen[:], marked[:, :, 0:n], MARK, None, ALU.is_equal).then_inc(step, 1)
            dve.wait_ge(step, 7)
            nc.vector.tensor_tensor(kept[:], prob[:], chosen[:], ALU.mult).then_inc(step, 1)
            dve.wait_ge(step, 8)
            nc.vector.tensor_reduce(total[:], kept[:], AX, ALU.add).then_inc(step, 1)
            dve.wait_ge(step, 9)
            if layer == 0:
                nc.vector.tensor_scalar(none[:], total[:], 0.0, None, ALU.is_le).then_inc(step, 1)
                dve.wait_ge(step, 10)
                nc.vector.tensor_tensor(total[:], total[:], none[:], ALU.add).then_inc(step, 1)
            else:
                nc.vector.tensor_scalar(none[:], total[:], 1e-12, None, ALU.max).then_inc(step, 1)
                dve.wait_ge(step, 10)
                nc.vector.tensor_copy(total[:], none[:]).then_inc(step, 1)
            dve.wait_ge(step, 11)
            nc.vector.reciprocal(inv[:], total[:]).then_inc(step, 1)
            dve.wait_ge(step, 12)
            nc.vector.tensor_tensor(k.combine[:, :, 0:n], kept[:], over(inv[:]), ALU.mult).then_inc(step, 1)
            if layer == 0:
                dve.wait_ge(step, 13)
                nc.vector.tensor_tensor(k.combine[:, :, 0:n], k.combine[:, :, 0:n],
                                        small(k, "pes").unsqueeze(1).broadcast_to([P, NT, n]), ALU.mult)


class ExpertWeights:

    def __init__(self, nc, scope, layer, up_w, down_w):
        def sb(name, shape, dt=F32):
            return scope.enter_context(nc.sbuf_tensor(f"{name}_w{layer}", shape, dt))

        def sem(name):
            return scope.enter_context(nc.semaphore(f"{name}_w{layer}"))

        self.nc, self.up_w, self.down_w = nc, up_w, down_w
        self.up_raw, self.down_raw = sb("up_raw", [P, C, 2, HID]), sb("down_raw", [P, HC, D])
        self.up = [[sb(f"up{s}_{part}", [P, C, 2, HID], F32R) for part in ("hi", "lo")] for s in range(2)]
        self.down = [[sb(f"down{s}_{part}", [P, HC, D], F32R) for part in ("hi", "lo")] for s in range(2)]
        self.up_in, self.down_in, self.begun = sem("up_in"), sem("down_in"), sem("split_begun")
        self.hi_done, self.up_split, self.down_split = sem("w_hi"), sem("up_split"), sem("down_split")
        self.h_t = [sb(f"h_{part}", [P, C, T], F32R) for part in ("hi", "lo")]
        self.h_hi_done, self.h_split = sem("h_hi"), sem("h_split")

    def load(self, sp, g):
        sp.dma_start(self.up_raw[:], self.up_w[g].rearrange("p c (j h) -> p c j h", j=2)).then_inc(self.up_in, 16)
        if not isinstance(g, int) or g > 0:
            sp.wait_ge(self.down_split, g * 1)
        sp.dma_start(self.down_raw[:], self.down_w[g]).then_inc(self.down_in, 16)

    def first_hi(self, act, h_t):
        act.wait_ge(self.up_in, 16)
        for c in range(C):
            self.nc.scalar.activation(self.up[0][0][:, c], self.up_raw[:, c], ACT.Copy).then_inc(self.hi_done, 1)
        act.wait_ge(self.down_in, 16)
        self.nc.scalar.activation(self.down[0][0][:], self.down_raw[:], ACT.Copy).then_inc(self.hi_done, 1)
        for c in range(C):
            self.nc.scalar.activation(self.h_t[0][:, c], h_t[:, c], ACT.Copy).then_inc(self.h_hi_done, 1)

    def first_lo(self, pool):
        gpsimd = self.nc.gpsimd
        for c in range(C):
            pool.wait_ge(self.hi_done, c + 1)
            gpsimd.tensor_tensor(self.up[0][1][:, c], self.up_raw[:, c], self.up[0][0][:, c].bitcast(F32),
                                 ALU.subtract).then_inc(self.up_split, 1)
        pool.wait_ge(self.hi_done, 3)
        gpsimd.tensor_tensor(self.down[0][1][:], self.down_raw[:], self.down[0][0][:].bitcast(F32),
                             ALU.subtract).then_inc(self.down_split, 1)

    def tokens_lo(self, dve, h_t):
        for c in range(C):
            dve.wait_ge(self.h_hi_done, c + 1)
            self.nc.vector.tensor_tensor(self.h_t[1][:, c], h_t[:, c], self.h_t[0][:, c].bitcast(F32),
                                         ALU.subtract).then_inc(self.h_split, 1)

    def split(self, pool, g, s, unused):
        gpsimd = self.nc.gpsimd
        pool.wait_ge(self.up_in, g * 16 + 16)
        if unused is not None:
            pool.wait_ge(*unused)
        pool.sem_inc(self.begun, 1)
        up_hi, up_lo = self.up[s]
        for c in range(C):
            gpsimd.tensor_scalar(up_hi[:, c], self.up_raw[:, c], 1.0, None, ALU.mult).then_inc(self.hi_done, 1)
        for c in range(C):
            pool.wait_ge(self.hi_done, g * 3 + (c + 1))
            gpsimd.tensor_tensor(up_lo[:, c], self.up_raw[:, c], up_hi[:, c].bitcast(F32),
                                 ALU.subtract).then_inc(self.up_split, 1)
        down_hi, down_lo = self.down[s]
        pool.wait_ge(self.down_in, g * 16 + 16)
        pool.sem_inc(self.begun, 1)
        gpsimd.tensor_scalar(down_hi[:], self.down_raw[:], 1.0, None, ALU.mult).then_inc(self.hi_done, 1)
        pool.wait_ge(self.hi_done, g * 3 + 3)
        gpsimd.tensor_tensor(down_lo[:], self.down_raw[:], down_hi[:].bitcast(F32),
                             ALU.subtract).then_inc(self.down_split, 1)


def experts(nc, k, layer, w, func, then=None):
    GR, UNITS = 8, 4
    per_expert = layer == 1
    GROUPS_ALL = GR + per_expert
    Y = 8 if per_expert else 4
    HALF = T // 2
    with ExitStack() as ctx:
        def sb(name, shape, dt=F32):
            return ctx.enter_context(nc.sbuf_tensor(f"{name}_e{layer}", shape, dt))

        def parts(name, shape):
            return [sb(f"{name}_hi", shape, F32R), sb(f"{name}_lo", shape, F32R)]

        def bank(name, n):
            return [ctx.enter_context(nc.psum_tensor(f"{name}{j}_e{layer}", [P, BANK], F32)) for j in range(n)]

        def sem(name):
            return ctx.enter_context(nc.semaphore(f"{name}_e{layer}"))

        gate = [sb(f"gate{s}", [P, HALF]) for s in range(2)]
        product = [sb(f"product{s}", [P, HALF]) for s in range(2)]
        hidden = [parts(f"hidden{s}", [P, HC, HALF]) for s in range(2)]
        g_ps, u_ps, y_ps = bank("g_ps", 2), bank("u_ps", 2), bank("y_ps", 4)
        up_done, gate_done, y_done = sem("up_done"), sem("gate_done"), sem("y_done")
        gated = sem("gated")
        hidden_hi = sem("hidden_hi")
        hidden_split = sem("hidden_split")
        x_added = sem("x_added")
        first_added = sem("first_added")
        block = ctx.enter_context(nc.Block())

        def products(out, a, b, start, stop):
            nc.tensor.matmul(out, a[0], b[0], start=start, stop=False)
            nc.tensor.matmul(out, a[0], b[1], start=False, stop=False)
            return nc.tensor.matmul(out, a[1], b[0], start=False, stop=stop)

        @block.sync
        def _(sp):
            with sp.Fori(1, GROUPS_ALL) as g:
                sp.wait_ge(w.up_split, g * C)
                w.load(sp, g)
            if then is not None:
                then.load_first(sp)

        @block.gpsimd
        def _(pool):
            w.split(pool, 1, 1, None)
            with pool.Fori(0, GR // 2 - 1) as i:
                for s in range(2):
                    w.split(pool, i * 2 + (s + 2), s, (y_done, i * (UNITS * Y) + (2 * s + 2) * Y))
            if per_expert:
                w.split(pool, GR, 0, (y_done, GR // 2 * UNITS * Y - 2 * Y))
            if then is not None:
                then.split_first(pool)

        @block.tensor
        def _(pe):
            def ups(s, half, unit, g):
                pe.wait_ge(w.up_split, g * C + C)
                for hc in range(HC):
                    b = hc % 2
                    pe.wait_ge(gated, unit * HC + (hc + 1))
                    for ps, j in ((g_ps[b], 0), (u_ps[b], 1)):
                        for c in range(C):
                            last = products(ps[:], [part[:, c, j, hc * P:(hc + 1) * P] for part in w.up[s]],
                                            [part[:, c, half * HALF:(half + 1) * HALF] for part in w.h_t],
                                            c == 0, c == C - 1)
                    last.then_inc(up_done, 1)

            def downs(s, u, unit, g, y0, by_expert):
                pe.wait_ge(w.down_split, g + 1)
                pe.wait_ge(hidden_split, unit * HC + (HC + 2))
                hid = hidden[u % 2]
                m = 0
                for t in range(4):
                    rows = slice(t * P, (t + 1) * P)
                    for pair in range(2 if by_expert else 1):
                        y = y_ps[m % 4]
                        pe.wait_ge(x_added, y0 + (m + 1))
                        for j in range(2 if by_expert else HC):
                            hc = 2 * pair + j if by_expert else j
                            last = products(y[:, j * D:(j + 1) * D] if by_expert else y[:, 0:D],
                                            [h[:, hc, rows] for h in hid], [part[:, hc, :] for part in w.down[s]],
                                            by_expert or hc == 0, by_expert or hc == HC - 1)
                        last.then_inc(y_done, 1)
                        m += 1

            pe.wait_ge(w.h_split, C)
            with pe.Fori(0, GR // 2) as i:
                def up_unit(u):
                    ups(u // 2, u % 2, i * UNITS + u, i * 2 + u // 2)

                def down_unit(u):
                    downs(u // 2, u, i * UNITS + u, i * 2 + u // 2, i * (UNITS * Y) + u * Y, per_expert)

                up_unit(0)
                for u in range(1, UNITS):
                    up_unit(u)
                    down_unit(u - 1)
                down_unit(UNITS - 1)
            if per_expert:
                done = GR // 2 * UNITS
                ups(0, 0, done, GR)
                ups(0, 1, done + 1, GR)
                downs(0, 0, done, GR, done * Y, False)
                downs(0, 1, done + 1, GR, done * Y + 4, False)

        @block.scalar
        def _(act):
            def gates(u, unit):
                def hi(hc):
                    act.wait_ge(gated, unit * HC + (hc + 3))
                    nc.scalar.activation(hidden[u % 2][0][:, hc, :], product[hc % 2][:], ACT.Copy).then_inc(hidden_hi, 1)

                for hc in range(HC):
                    act.wait_ge(up_done, unit * HC + (hc + 1))
                    nc.scalar.activation(gate[hc % 2][:], g_ps[hc % 2][:], func).then_inc(gate_done, 1)
                    if hc:
                        hi(hc - 1)
                hi(HC - 1)

            with act.Fori(0, GR // 2) as i:
                for u in range(UNITS):
                    gates(u, i * UNITS + u)
            if per_expert:
                for u in range(2):
                    gates(u, GR // 2 * UNITS + u)

        @block.vector
        def _(dve):
            def gatings(u, unit):
                def lo(hc):
                    dve.wait_ge(hidden_hi, unit * HC + (hc + 1))
                    nc.vector.tensor_tensor(hidden[u % 2][1][:, hc, :], product[hc % 2][:],
                                            hidden[u % 2][0][:, hc, :].bitcast(F32),
                                            ALU.subtract).then_inc(hidden_split, 1)

                for hc in range(HC):
                    dve.wait_ge(gate_done, unit * HC + (hc + 1))
                    dve.wait_ge(hidden_split, unit * HC + (hc + 1))
                    nc.vector.tensor_tensor(product[hc % 2][:], gate[hc % 2][:], u_ps[hc % 2][:],
                                            ALU.mult).then_inc(gated, 1)
                    if hc:
                        lo(hc - 1)
                lo(HC - 1)

            def adds(half, y0, g, by_expert):
                m = 0
                for t in range(4 * half, 4 * half + 4):
                    for pair in range(2 if by_expert else 1):
                        y = y_ps[m % 4]
                        dve.wait_ge(y_done, y0 + (m + 1))
                        dve.wait_ge(x_added, y0 + (m + 4))
                        if by_expert:
                            for j in range(2):
                                if j:
                                    dve.wait_ge(first_added, y0 + (m + 1))
                                nc.vector.scalar_tensor_tensor(
                                    out=k.x[:, t, :], in0=y[:, j * D:(j + 1) * D],
                                    scalar=k.combine[:, t, bass.ds(g * 4 + (2 * pair + j), 1)], in1=k.x[:, t, :],
                                    op0=ALU.mult, op1=ALU.add).then_inc(x_added if j else first_added, 1)
                        elif g is None:
                            nc.vector.tensor_tensor(k.x[:, t, :], k.x[:, t, :], y[:, 0:D],
                                                    ALU.add).then_inc(x_added, 1)
                        else:
                            nc.vector.scalar_tensor_tensor(
                                out=k.x[:, t, :], in0=y[:, 0:D], scalar=k.combine[:, t, bass.ds(g, 1)],
                                in1=k.x[:, t, :], op0=ALU.mult, op1=ALU.add).then_inc(x_added, 1)
                        m += 1

            dve.sem_inc(gated, 2)
            dve.sem_inc(hidden_split, 2)
            dve.sem_inc(x_added, 4)
            with dve.Fori(0, GR // 2) as i:
                def add_unit(u):
                    adds(u % 2, i * (UNITS * Y) + u * Y, i * 2 + u // 2, per_expert)

                gatings(0, i * UNITS)
                for u in range(1, UNITS):
                    gatings(u, i * UNITS + u)
                    add_unit(u - 1)
                add_unit(UNITS - 1)
            if per_expert:
                done = GR // 2 * UNITS
                gatings(0, done)
                gatings(1, done + 1)
                adds(0, done * Y, None, False)
                adds(1, done * Y + 4, None, False)


class Ring:

    def __init__(self, i, uses_per_tile, splits_per_tile, at, splits):
        assert uses_per_tile % 2 == 0
        self.i, self.each, self.split_each, self.at, self.splits = i, uses_per_tile // 2, splits_per_tile, at, splits

    def place(self, back=0):
        at = self.at - back
        return at % 2, self.i * self.each + (at // 2 + 1)

    def next(self, split=False):
        got = self.place()
        self.at += 1
        self.splits += 1 if split else 0
        return got

    def split_count(self):
        return self.i * self.split_each + self.splits



def ct_piece(j):
    half = (M + 1) // 2
    return j // 2, (j % 2) * half, half if j % 2 == 0 else M - half


def cn_piece(j):
    return ((0, 4), (4, 3), (7, 3), (10, 3))[j - 4]


def load_ct(sp, first, ctx_b, j):
    c, start, width = ct_piece(j)
    sp.dma_start(first.staged[:, 0:width], ctx_b[:, c, start:start + width]).then_inc(first.piece_in, 16)


def split_piece(nc, pool, first, piece, hi, lo, n, done):
    pool.wait_ge(first.piece_in, n * 16 + 16)
    pool.sem_inc(first.split_begun, 1)
    nc.gpsimd.tensor_scalar(hi, piece, 1.0, None, ALU.mult).then_inc(first.hi_done, 1)
    pool.wait_ge(first.hi_done, n + 1)
    nc.gpsimd.tensor_tensor(lo, piece, hi.bitcast(F32), ALU.subtract).then_inc(done, 1)


def split_ct(nc, pool, first, ct, n, j):
    c, start, width = ct_piece(j)
    hi, lo = (ct[:, part, c, start:start + width] for part in range(2))
    split_piece(nc, pool, first, first.staged[:, 0:width], hi, lo, n + j, first.ct_split)


class CrossFirst:

    def __init__(self, nc, scope, src):
        def sb(name, shape, dt=F32):
            return scope.enter_context(nc.sbuf_tensor(name, shape, dt))

        self.nc, self.src = nc, src
        self.w_shared = sb("w_shared", [P, C * INNER])
        self.wq = self.w_shared[:].rearrange("p (c e) -> p c e", c=C)
        self.wk = sb("wk1", [P, 2, PAIRS1, D])
        self.staged = sb("staged", [P, 4 * D])
        self.ct = sb("ct0", [P, 2, C, M], F32R)
        self.wq_in, self.wk_in, self.piece_in, self.hi_done, self.ct_split, self.split_begun = (
            scope.enter_context(nc.semaphore(n))
            for n in ("wq1_in", "wk1_in", "piece_in", "ctx_hi_done", "ct_split", "ctx_split_begun"))

    def load_first(self, sp):
        for j in range(4):
            if j:
                sp.wait_ge(self.ct_split, j)
            load_ct(sp, self, self.src["ctx_t"][0], j)
        sp.dma_start(self.wq, self.src["wq1"]).then_inc(self.wq_in, 16)
        sp.dma_start(self.wk[:], self.src["wk1"]).then_inc(self.wk_in, 16)

    def split_first(self, pool):
        for j in range(4):
            split_ct(self.nc, pool, self, self.ct, 0, j)


def cross_attention(nc, k, src, first):
    STEPS = 2 * PAIRS1
    USES = STEPS * 7 + 4
    SPLITS = STEPS * 5
    SCALE = HD1 ** -0.5
    TXT_EVEN = TXT + TXT % 2
    with ExitStack() as ctx:
        def sb(name, shape, dt=F32):
            return ctx.enter_context(nc.sbuf_tensor(name, shape, dt))

        def ps(name, shape):
            return ctx.enter_context(nc.psum_tensor(name, shape, F32))

        def sem(name):
            return ctx.enter_context(nc.semaphore(name))

        staged, wk, wq = first.staged, first.wk, first.wq
        wo = first.w_shared[:].rearrange("p (h d) -> p h d", h=PAIRS1)
        wv = sb("wv1", [P, 2, C, INNER])
        ct = [first.ct, sb("ct1", [P, 2, C, M], F32R)]
        cn = [sb(f"cn{b}", [P, 2, NBLK, D], F32R) for b in range(2)]
        q = sb("q1", [P, PAIRS1, 2, P])
        a_hi, a_lo = sb("a_hi", [P, 2, C, P], F32R), sb("a_lo", [P, 2, C, P], F32R)
        prob = sb("prob1", [P, M])
        pt_hi, pt_lo = sb("pt_hi", [P, NBLK, P], F32R), sb("pt_lo", [P, NBLK, P], F32R)
        top = [sb(f"top1{s}", [P, 2]) for s in range(2)]
        bias = [sb(f"bias1{s}", [P, 2]) for s in range(2)]
        total = [sb(f"total1{s}", [P, 2]) for s in range(2)]
        inv = [sb(f"inv1{s}", [P, 2]) for s in range(2)]
        o, o_part = sb("o1", [P, 2, D]), sb("o1_part", [P, D])
        ot = sb("ot1", [P, 4, P])
        head_out = sb("head_out", [P, PAIRS1, P])
        s_ps = ps("s1_ps", [P, 4, BANK])
        t_ps = [ps(f"t1_ps{j}", [P, BANK]) for j in range(2)]
        txt_ps, img_ps = ps("txt_ps", [P, BANK]), ps("img_ps", [P, BANK])
        wq_in, wk_in, wv_in, wo_in = first.wq_in, first.wk_in, sem("wv1_in"), sem("wo1_in")
        queried, projected = sem("queried"), sem("projected")
        piece_in, hi_done, ct_split, cn_split = first.piece_in, first.hi_done, first.ct_split, sem("cn_split")
        scored, topped, bias_done, exp_done = sem("scored1"), sem("topped1"), sem("bias1_done"), sem("exp1_done")
        t_done = [sem(f"t1_done{j}") for j in range(2)]
        t_kept = [sem(f"t1_kept{j}") for j in range(2)]
        hi_kept = sem("hi_kept")
        summed, inv_done, part_kept, sums_kept = sem("summed1"), sem("inv1_done"), sem("part1_kept"), sem("sums1_kept")
        q_zeroed = sem("q_zeroed")
        split_begun = first.split_begun
        block = ctx.enter_context(nc.Block())

        def tiles(eng, body):
            body(0, Ring(0, USES, SPLITS, 3, 1), True, False)
            before = 3 - (4 + 2 + 2 + 2)
            with eng.Fori(1, NT - 1) as i:
                body(i, Ring(i, USES, SPLITS, before, -3), False, False)
            body(NT - 1, Ring(NT - 1, USES, SPLITS, before, -3), False, True)

        @block.sync
        def _(sp):
            def load(i, b, pieces):
                for j in pieces:
                    wait_split(i, b, j)
                    if j < 4:
                        load_ct(sp, first, src["ctx_t"][i * 2 + b], j)
                    else:
                        start, blocks = cn_piece(j)
                        sp.dma_start(staged[:, 0:blocks * D].rearrange("p (j d) -> p j d", d=D),
                                     src["ctx_n"][i * 2 + b][:, start:start + blocks, :]).then_inc(piece_in, 16)

            def wait_split(i, b, j):
                if j == 0:
                    sp.wait_ge(cn_split, i * 8 + 4 * b)
                elif j <= 4:
                    sp.wait_ge(ct_split, i * 8 + (4 * b + j))
                else:
                    sp.wait_ge(cn_split, i * 8 + (4 * b + j - 4))

            def load_wq():
                sp.dma_start(wq, src["wq1"]).then_inc(wq_in, 16)

            def load_wo(i):
                sp.wait_ge(queried, i + 2)
                sp.dma_start(wo, src["wo1"]).then_inc(wo_in, 16)

            load(0, 0, range(4, 8))
            sp.dma_start(wv[:], src["wv1"]).then_inc(wv_in, 16)
            load(0, 1, range(8))
            load(1, 0, range(8))
            load_wo(0)
            with sp.Fori(1, NT - 1) as i:
                load(i, 1, range(8))
                sp.wait_ge(projected, i + 0)
                load_wq()
                load(i + 1, 0, range(8))
                load_wo(i)
            load(NT - 1, 1, range(8))

        @block.gpsimd
        def _(pool):
            def split(i, b, pieces=range(8)):
                for j in pieces:
                    if j == 0 and not isinstance(i, int):
                        pool.wait_ge(scored, i * STEPS + (b - 1) * PAIRS1)
                    if j == 4 and not isinstance(i, int):
                        pool.wait_ge(summed, i * STEPS + (b - 1) * PAIRS1)
                    if j < 4:
                        split_ct(nc, pool, first, ct[b], i * 16 + 8 * b, j)
                    else:
                        start, blocks = cn_piece(j)
                        hi, lo = (cn[b][:, part, start:start + blocks, :].rearrange("p j d -> p (j d)")
                                  for part in range(2))
                        split_piece(nc, pool, first, staged[:, 0:blocks * D], hi, lo, i * 16 + (8 * b + j), cn_split)

            split(0, 0, range(4, 8))
            split(0, 1)
            with pool.Fori(1, NT) as i:
                for b in range(2):
                    split(i, b)


        @block.tensor
        def _(pe):
            def use(ring, split=False):
                bank, count = ring.next(split)
                if not isinstance(count, int) or count > 1:
                    pe.wait_ge(t_kept[bank], count - 1)
                return bank

            def kept(place):
                pe.wait_ge(t_kept[place[0]], place[1])

            def kept_before(ring, place):
                if place[0] != ring.place()[0]:
                    kept(place)

            def queries(ring, t):
                for half in range(2):
                    bank = use(ring)
                    for j in range(4):
                        p = 4 * half + j
                        for c in range(C):
                            last = nc.tensor.matmul(t_ps[bank][:, j * P:(j + 1) * P], wq[:, c, p * P:(p + 1) * P],
                                                    k.h_t[:, c, bass.ds(t * P, P)], start=c == 0, stop=c == C - 1)
                    last.then_inc(t_done[bank], 1)
                return ring.place(2), ring.place(1)

            def key_side(ring, n):
                b, p = divmod(n % STEPS, PAIRS1)
                bank = use(ring, True)
                for kind in range(2):
                    for c in range(C):
                        j = kind * C + c
                        last = nc.tensor.matmul(t_ps[bank][:, j * P:(j + 1) * P], wk[:, kind, p, c * P:(c + 1) * P],
                                                q[:, p, :, b * S:(b + 1) * S], start=True, stop=True)
                last.then_inc(t_done[bank], 1)

            def scores(n, part):
                b = n // PAIRS1
                """Part 0 is the text, parts 1 to 3 the image."""
                first, width = (0, TXT_EVEN) if part == 0 else (TXT + (part - 1) * SBLK, SBLK)
                kind = min(part, 1)
                for c in range(C):
                    out = s_ps[:, part, 0:width]
                    hi, lo = a_hi[:, kind, c, :], a_lo[:, kind, c, :]
                    nc.tensor.matmul(out, hi, ct[b][:, 0, c, first:first + width], start=c == 0, stop=False)
                    nc.tensor.matmul(out, hi, ct[b][:, 1, c, first:first + width], start=False, stop=False)
                    last = nc.tensor.matmul(out, lo, ct[b][:, 0, c, first:first + width], start=False, stop=c == C - 1)
                return last

            def turn(ring, g):
                bank = use(ring, True)
                for j in range(1 if g == 0 else 4):
                    blk = 0 if g == 0 else 4 * (g - 1) + j
                    first, width = (0, TXT) if g == 0 else (TXT + blk * IBLK, IBLK)
                    last = nc.tensor.transpose(t_ps[bank][0:width, j * P:(j + 1) * P],
                                               prob[:, first:first + width], k.ident)
                last.then_inc(t_done[bank], 1)

            def sums(n):
                hi, lo, rows = pt_hi[0:TXT, 0, :], pt_lo[0:TXT, 0, :], cn[n // PAIRS1]
                nc.tensor.matmul(txt_ps[:, 0:D], hi, rows[0:TXT, 0, 0, :], start=True, stop=False)
                nc.tensor.matmul(txt_ps[:, 0:D], hi, rows[0:TXT, 1, 0, :], start=False, stop=False)
                nc.tensor.matmul(txt_ps[:, 0:D], lo, rows[0:TXT, 0, 0, :], start=False, stop=True)
                for j in range(1, NBLK):
                    nc.tensor.matmul(img_ps[:], pt_hi[0:IBLK, j, :], rows[0:IBLK, :, j, :], start=j == 1, stop=False)
                    last = nc.tensor.matmul(img_ps[:, D:2 * D], pt_lo[0:IBLK, j, :], rows[0:IBLK, 0, j, :],
                                            start=False, stop=j == NBLK - 1)
                last.then_inc(summed, 1)

            def turn_sums(ring):
                bank = use(ring)
                for j in range(4):
                    last = nc.tensor.transpose(t_ps[bank][:, j * P:(j + 1) * P],
                                               o[:, j // 2, (j % 2) * P:(j % 2 + 1) * P], k.ident)
                last.then_inc(t_done[bank], 1)

            def value_side(ring, n):
                bank = use(ring)
                for r in range(2):
                    h = 2 * (n % PAIRS1) + r
                    for j in range(4):
                        last = nc.tensor.matmul(t_ps[bank][r * S:(r + 1) * S, 0:S],
                                                wv[:, j // 2, j % 2, h * HD1:(h + 1) * HD1],
                                                ot[:, j, r * S:(r + 1) * S], start=j == 0, stop=j == 3)
                last.then_inc(t_done[bank], 1)

            def project(ring):
                kept(ring.place(1))
                for half in range(2):
                    bank = use(ring)
                    cols = slice(half * P, (half + 1) * P)
                    for p in range(PAIRS1):
                        nc.tensor.matmul(t_ps[bank][:, 0:P], head_out[:, p, :], wo[:, p, cols], start=p == 0, stop=False)
                    nc.tensor.matmul(t_ps[bank][:, 0:P], k.ones[0:1, :], k.bo1[:, cols], start=False,
                                     stop=True).then_inc(t_done[bank], 1)

            pe.wait_ge(wq_in, 16)
            start = Ring(0, USES, SPLITS, 0, 0)
            for place in queries(start, 0):
                kept(place)
            pe.wait_ge(wk_in, 16)
            key_side(start, 0)

            def body(i, ring, first_tile, last_tile):
                base = i * STEPS
                a_place = ring.place(1 if first_tile else 2)
                for n in range(STEPS + 2 if last_tile else STEPS):
                    before, two_before = not first_tile or n >= 1, not first_tile or n >= 2
                    if n < STEPS and n % PAIRS1 == 0:
                        pe.wait_ge(ct_split, i * 8 + (n // PAIRS1 * 4 + 4))
                    if n <= STEPS and before:
                        pe.wait_ge(exp_done, base + n)
                    if n < STEPS:
                        kept_before(ring, a_place)
                    for g in range(4):
                        if n <= STEPS and before:
                            turn(ring, g)
                        if n < STEPS:
                            last = scores(n, g)
                    if n < STEPS:
                        last.then_inc(scored, 1)
                    turned = [ring.place(2), ring.place(1)]
                    if two_before:
                        pe.wait_ge(sums_kept, base + (n - 1))
                        turn_sums(ring)
                        ot_place = ring.place(1)
                    if n == STEPS - 1 and not last_tile:
                        if not first_tile:
                            pe.wait_ge(wq_in, i * 16 + 16)
                        q_places = queries(ring, i + 1)
                    if n < STEPS - 1:
                        a_place = ring.place()
                        key_side(ring, n + 1)
                    if n <= STEPS and before:
                        if n % PAIRS1 == 1:
                            pe.wait_ge(cn_split, i * 8 + (n // PAIRS1 * 4 + 4))
                        for place in turned:
                            kept(place)
                        sums(n - 1 if n else STEPS - 1)
                    if n == STEPS - 1 and not last_tile:
                        for place in q_places:
                            kept(place)
                        a_place = ring.place()
                        key_side(ring, n + 1)
                    if two_before:
                        if first_tile and n == 2:
                            pe.wait_ge(wv_in, 16)
                        kept_before(ring, ot_place)
                        value_side(ring, n - 2)
                    if n == 1 and not first_tile:
                        pe.wait_ge(wo_in, i * 16)
                        project(ring)
                    if n == STEPS + 1:
                        project(ring)

            tiles(pe, body)

        def keep(eng, copy, ring, out, rows=P, cols=BANK):
            bank, count = ring.next()
            eng.wait_ge(t_done[bank], count)
            copy(out, t_ps[bank][0:rows, 0:cols]).then_inc(t_kept[bank], 1)

        def keep_hi(act, ring, out, rows=P, cols=BANK):
            bank, count = ring.next(True)
            act.wait_ge(t_done[bank], count)
            nc.scalar.activation(out, t_ps[bank][0:rows, 0:cols], ACT.Copy).then_inc(hi_kept, 1)

        def keep_lo(dve, ring, out, hi, rows=P, cols=BANK):
            bank, count = ring.next(True)
            dve.wait_ge(hi_kept, ring.split_count())
            nc.vector.tensor_tensor(out, t_ps[bank][0:rows, 0:cols], hi.bitcast(F32),
                                    ALU.subtract).then_inc(t_kept[bank], 1)

        def turned_part(pt, g):
            if g == 0:
                return pt[0:TXT, 0, :]
            return pt[0:IBLK, 4 * g - 3:4 * g + 1, :].rearrange("p j n -> p (j n)")

        def turned_size(g):
            return (TXT, P) if g == 0 else (IBLK, BANK)

        def flat(a):
            return a[:].rearrange("p k c n -> p (k c n)")

        def keep_queries(eng, copy, mine, ring):
            for half in range(2):
                bank, count = ring.next()
                if half == mine:
                    eng.wait_ge(t_done[bank], count)
                    for r in range(2):
                        rows = slice(r * HD1, (r + 1) * HD1)
                        last = copy(q[rows, 4 * half:4 * half + 4, r, :],
                                    t_ps[bank][rows, :].rearrange("p (j n) -> p j n", j=4))
                    last.then_inc(t_kept[bank], 1)

        @block.scalar
        def _(act):
            def copy(out, in_):
                return nc.scalar.activation(out, in_, ACT.Copy)

            act.wait_ge(q_zeroed, 1)
            start = Ring(0, USES, SPLITS, 0, 0)
            keep_queries(act, copy, 0, start)
            keep_hi(act, start, flat(a_hi))

            def body(i, ring, first_tile, last_tile):
                for n in range(STEPS + 2 if last_tile else STEPS):
                    s = n % 2
                    before, two_before = not first_tile or n >= 1, not first_tile or n >= 2
                    if n <= STEPS and before:
                        for g in range(4):
                            keep_hi(act, ring, turned_part(pt_hi, g), *turned_size(g))
                    if two_before:
                        keep(act, copy, ring, ot[:].rearrange("p j n -> p (j n)"))
                    if n < STEPS - 1:
                        keep_hi(act, ring, flat(a_hi))
                    if n < STEPS:
                        act.wait_ge(bias_done, i * STEPS + (n + 1))
                        nc.scalar.activation(prob[:, TXT:M].rearrange("p (j m) -> p j m", j=SB),
                                             s_ps[:, 1:4, 0:SBLK], ACT.Exp, bias=bias[s][:, 1:2], scale=SCALE,
                                             accum_out=total[s][:, 1:2])
                        nc.scalar.activation(prob[:, 0:TXT], s_ps[:, 0, 0:TXT], ACT.Exp, bias=bias[s][:, 0:1],
                                             scale=SCALE, accum_out=total[s][:, 0:1]).then_inc(exp_done, 1)
                    if n == STEPS - 1 and not last_tile:
                        keep_queries(act, copy, 0, ring)
                        keep_hi(act, ring, flat(a_hi))
                    if two_before:
                        b, p = divmod((n - 2) % STEPS, PAIRS1)
                        keep(act, copy, ring, head_out[:, p, b * S:(b + 1) * S], P, S)
                    if n == 1 and not first_tile or n == STEPS + 1:
                        ring.next()
                        ring.next()

            tiles(act, body)

        @block.vector
        def _(dve):
            def copy(out, in_):
                return nc.vector.tensor_copy(out, in_)

            nc.vector.memset(q[:], 0.0).then_inc(q_zeroed, 1)
            dve.wait_ge(q_zeroed, 1)
            start = Ring(0, USES, SPLITS, 0, 0)
            keep_queries(dve, copy, 1, start)
            dve.sem_inc(queried, 1)
            keep_lo(dve, start, flat(a_lo), flat(a_hi))

            def body(i, ring, first_tile, last_tile):
                base = i * STEPS
                for n in range(STEPS + 2 if last_tile else STEPS):
                    s = n % 2
                    before, two_before = not first_tile or n >= 1, not first_tile or n >= 2
                    if n <= STEPS and before:
                        for g in range(4):
                            keep_lo(dve, ring, turned_part(pt_lo, g), turned_part(pt_hi, g), *turned_size(g))
                    if n < STEPS:
                        dve.wait_ge(scored, base + (n + 1))
                        nc.vector.tensor_reduce(top[s][:, 0:1], s_ps[:, 0, 0:TXT], AX, ALU.max)
                        nc.vector.tensor_reduce(top[s][:, 1:2], s_ps[:, 1:4, 0:SBLK], mybir.AxisListType.XY,
                                                ALU.max).then_inc(topped, 1)
                        dve.wait_ge(topped, base + (n + 1))
                        nc.vector.tensor_scalar(bias[s][:], top[s][:], -SCALE, None, ALU.mult).then_inc(bias_done, 1)
                    if two_before:
                        ring.next()
                    if n == STEPS - 1 and not last_tile:
                        keep_queries(dve, copy, 1, ring)
                        dve.sem_inc(queried, 1)
                    if n < STEPS - 1 or n == STEPS - 1 and not last_tile:
                        keep_lo(dve, ring, flat(a_lo), flat(a_hi))
                    if n <= STEPS and before:
                        dve.wait_ge(exp_done, base + n)
                        nc.vector.reciprocal(inv[1 - s][:], total[1 - s][:]).then_inc(inv_done, 1)
                        dve.wait_ge(summed, base + n)
                        dve.wait_ge(inv_done, base + n)
                        nc.vector.tensor_scalar(o_part[:], img_ps[:, D:2 * D], inv[1 - s][:, 1:2], None,
                                                ALU.mult).then_inc(part_kept, 1)
                        nc.vector.tensor_scalar(o[:, 0, :], txt_ps[:, 0:D], inv[1 - s][:, 0:1], None, ALU.mult)
                        dve.wait_ge(part_kept, base + n)
                        nc.vector.scalar_tensor_tensor(out=o[:, 1, :], in0=img_ps[:, 0:D], scalar=inv[1 - s][:, 1:2],
                                                       in1=o_part[:], op0=ALU.mult, op1=ALU.add).then_inc(sums_kept, 1)
                    if two_before:
                        ring.next()
                    if n == 1 and not first_tile or n == STEPS + 1:
                        t = i if n == STEPS + 1 else i - 1
                        for half in range(2):
                            bank, count = ring.next()
                            dve.wait_ge(t_done[bank], count)
                            xt = k.x[:, bass.ds(t, 1), half * P:(half + 1) * P].rearrange("p a d -> p (a d)")
                            nc.vector.tensor_tensor(xt, xt, t_ps[bank][:, 0:P], ALU.add).then_inc(t_kept[bank], 1)
                        dve.sem_inc(projected, 1)

            tiles(dve, body)


def scan_layer(nc, k, src):
    HALF = T // 2
    HB = NB // 2
    with ExitStack() as outer:
        def keep(name, shape, dt=F32):
            return outer.enter_context(nc.sbuf_tensor(name, shape, dt))

        gate = keep("gate_z", [P, C, T])
        xc = keep("xc", [P, C, T])
        u = keep("u", [P, C, T])
        dt = keep("dt", [P, T])
        a_neg = keep("a_neg", [P, C * NS])
        par = keep("par", [NPAR, T])
        diag = keep("diag_d", [P, C, P])
        w_out = keep("w_out", [P, C, D])
        gated = keep("gated_y", [P, C, T])
        w_out_in = outer.enter_context(nc.semaphore("w_out_in"))

        with ExitStack() as ctx:
            w_in_proj = ctx.enter_context(nc.sbuf_tensor("w_in_proj", [P, C, 2 * D], F32))
            xpad = ctx.enter_context(nc.sbuf_tensor("xpad", [P, C, NB, S + KC - 1], F32))
            acc = [ctx.enter_context(nc.sbuf_tensor(f"conv_acc{c}", [P, NB, S], F32)) for c in range(C)]
            ps = ctx.enter_context(nc.psum_tensor("xz_ps", [P, 2 * C, 2, BANK], F32))
            proj_in = ctx.enter_context(nc.semaphore("proj_in"))
            projected = ctx.enter_context(nc.semaphore("projected"))
            x_kept = ctx.enter_context(nc.semaphore("x_kept"))
            pad_zeroed = ctx.enter_context(nc.semaphore("pad_zeroed"))
            tap_done = ctx.enter_context(nc.semaphore("tap_done"))
            block = ctx.enter_context(nc.Block())

            @block.sync
            def _(sp):
                sp.dma_start(w_in_proj[:], src["win"]).then_inc(proj_in, 16)
                sp.dma_start(w_out[:], src["wout"]).then_inc(w_out_in, 16)

            @block.tensor
            def _(pe):
                pe.wait_ge(proj_in, 16)
                for e in range(2 * C):
                    for g in range(2):
                        for c in range(C):
                            last = nc.tensor.matmul(ps[:, e, g, :], w_in_proj[:, c, e * P:(e + 1) * P],
                                                    k.h_t[:, c, g * HALF:(g + 1) * HALF],
                                                    start=c == 0, stop=c == C - 1)
                        last.then_inc(projected, 1)

            @block.scalar
            def _(act):
                for e in range(C):
                    for g in range(2):
                        act.wait_ge(projected, 2 * e + g + 1)
                        nc.scalar.activation(xpad[:, e, g * HB:(g + 1) * HB, KC - 1:],
                                             ps[:, e, g, :].rearrange("p (b l) -> p b l", l=S),
                                             ACT.Copy).then_inc(x_kept, 1)
                for e in range(C):
                    for g in range(2):
                        act.wait_ge(projected, 2 * (C + e) + g + 1)
                        nc.scalar.activation(gate[:, e, g * HALF:(g + 1) * HALF], ps[:, C + e, g, :], ACT.Silu)
                for c in range(C):
                    act.wait_ge(tap_done, KC * C - C + c + 1)
                    nc.scalar.activation(xc[:, c, :], acc[c][:].rearrange("p b l -> p (b l)"), ACT.Silu,
                                         bias=small(k, "convb")[:, c:c + 1])

            @block.vector
            def _(dve):
                nc.vector.memset(xpad[:, :, :, 0:KC - 1], 0.0).then_inc(pad_zeroed, 1)
                dve.wait_ge(pad_zeroed, 1)
                w = small(k, "convw")
                for tap in range(KC):
                    for c in range(C):
                        seen = xpad[:, c, :, tap:tap + S]
                        if tap == 0:
                            dve.wait_ge(x_kept, 2 * c + 2)
                            nc.vector.tensor_scalar(acc[c][:], seen, w[:, c * KC:c * KC + 1], None,
                                                    ALU.mult).then_inc(tap_done, 1)
                        else:
                            dve.wait_ge(tap_done, C * (tap - 1) + c + 1)
                            nc.vector.scalar_tensor_tensor(
                                out=acc[c][:], in0=seen, scalar=w[:, c * KC + tap:c * KC + tap + 1], in1=acc[c][:],
                                op0=ALU.mult, op1=ALU.add).then_inc(tap_done, 1)

        with ExitStack() as ctx:
            w_par = ctx.enter_context(nc.sbuf_tensor("w_par", [P, C, NPAR], F32))
            pick_dt = ctx.enter_context(nc.sbuf_tensor("pick_dt", [NPAR, P], F32))
            mag = ctx.enter_context(nc.sbuf_tensor("mag", [NPAR, T], F32))
            pos = ctx.enter_context(nc.sbuf_tensor("pos_part", [NPAR, T], F32))
            exp_a = ctx.enter_context(nc.sbuf_tensor("exp_a", [P, C * NS], F32))
            p_ps = ctx.enter_context(nc.psum_tensor("par_ps", [P, 2, BANK], F32))
            d_ps = ctx.enter_context(nc.psum_tensor("dt_ps", [P, 2, BANK], F32))
            par_in, par_done, par_kept = (ctx.enter_context(nc.semaphore(n)) for n in ("par_in", "par_done", "par_kept"))
            soft, soft_kept = (ctx.enter_context(nc.semaphore(n)) for n in ("softplus_step", "softplus_kept"))
            pos_done, pick_set, dt_done, dt_kept = (
                ctx.enter_context(nc.semaphore(n)) for n in ("pos_done", "pick_set", "dt_done", "dt_kept"))
            exp_done = ctx.enter_context(nc.semaphore("exp_a_done"))
            block = ctx.enter_context(nc.Block())
            row = slice(NPAR - 1, NPAR)

            @block.sync
            def _(sp):
                sp.dma_start(w_par[:], src["wpar"]).then_inc(par_in, 16)

            @block.tensor
            def _(pe):
                pe.wait_ge(par_in, 16)
                for g in range(2):
                    for c in range(C):
                        last = nc.tensor.matmul(p_ps[0:NPAR, g, :], w_par[:, c, :], xc[:, c, g * HALF:(g + 1) * HALF],
                                                start=c == 0, stop=c == C - 1)
                last.then_inc(par_done, 1)
                pe.wait_ge(soft_kept, 1)
                pe.wait_ge(pick_set, 2)
                for g in range(2):
                    last = nc.tensor.matmul(d_ps[:, g, :], pick_dt[:], par[:, g * HALF:(g + 1) * HALF],
                                            start=True, stop=True)
                last.then_inc(dt_done, 1)

            @block.scalar
            def _(act):
                nc.scalar.activation(exp_a[:], small(k, "alog"), ACT.Exp).then_inc(exp_done, 1)
                act.wait_ge(par_done, 1)
                nc.scalar.activation(par[:], p_ps[0:NPAR].rearrange("p g n -> p (g n)"), ACT.Copy).then_inc(par_kept, 1)
                act.wait_ge(par_kept, 1)
                nc.scalar.activation(mag[row], par[row], ACT.Abs).then_inc(soft, 1)
                act.wait_ge(soft, 1)
                nc.scalar.activation(mag[row], mag[row], ACT.Exp, scale=-1.0).then_inc(soft, 1)
                act.wait_ge(soft, 2)
                nc.scalar.activation(mag[row], mag[row], ACT.Ln, bias=1.0).then_inc(soft, 1)
                act.wait_ge(dt_done, 1)
                nc.scalar.activation(dt[:], d_ps[:].rearrange("p g n -> p (g n)"), ACT.Copy).then_inc(dt_kept, 1)

            @block.vector
            def _(dve):
                nc.vector.memset(pick_dt[:], 0.0).then_inc(pick_set, 1)
                dve.wait_ge(pick_set, 1)
                nc.vector.memset(pick_dt[row], 1.0).then_inc(pick_set, 1)
                dve.wait_ge(exp_done, 1)
                nc.vector.tensor_scalar(a_neg[:], exp_a[:], -1.0, None, ALU.mult)
                for c in range(C):
                    nc.vector.tensor_scalar(diag[:, c, :], k.ident, small(k, "dpar")[:, c:c + 1], None, ALU.mult)
                dve.wait_ge(par_kept, 1)
                nc.vector.tensor_scalar(pos[row], par[row], 0.0, None, ALU.max).then_inc(pos_done, 1)
                dve.wait_ge(pos_done, 1)
                dve.wait_ge(soft, 3)
                nc.vector.tensor_tensor(par[row], pos[row], mag[row], ALU.add).then_inc(soft_kept, 1)
                dve.wait_ge(dt_kept, 1)
                for c in range(C):
                    nc.vector.tensor_tensor(u[:, c, :], xc[:, c, :], dt[:], ALU.mult)

        with ExitStack() as ctx:
            def sb(name, shape):
                return ctx.enter_context(nc.sbuf_tensor(name, shape, F32))

            def sem(name):
                return ctx.enter_context(nc.semaphore(name))

            ones = sb("ones33", [NPAR, P])
            pick_b, pick_c, par_hi, par_lo = (
                ctx.enter_context(nc.sbuf_tensor(n, [NPAR, cols], F32R))
                for n, cols in (("pick_b", P), ("pick_c", P), ("par_hi", T), ("par_lo", T)))
            decay = [sb(f"decay{c}", [P, NB, S]) for c in range(C)]
            drive = [sb(f"drive{c}", [P, T]) for c in range(C)]
            state = [sb(f"state{c}", [P, T]) for c in range(C)]
            read = [sb(f"read{c}", [P, T]) for c in range(C)]
            c_row = sb("c_row", [P, T])
            b_ps = ctx.enter_context(nc.psum_tensor("b_ps", [P, 2, BANK], F32))
            c_ps = ctx.enter_context(nc.psum_tensor("c_ps", [P, 2, BANK], F32))
            y_ps = ctx.enter_context(nc.psum_tensor("scan_y_ps", [P, C, 2, BANK], F32))
            hi_kept, par_split, ones_set = sem("par_hi_kept"), sem("par_split"), sem("ones33_set")
            set_up, rows_picked, b_done, c_done = sem("scan_set_up"), sem("rows_picked"), sem("b_done"), sem("c_done")
            c_kept, decayed, driven, scanned = sem("c_kept"), sem("decayed"), sem("driven"), sem("scanned")
            read_done, y_added = sem("read_done"), sem("scan_y_added")
            block = ctx.enter_context(nc.Block())


            @block.scalar
            def _(act):
                def rows(n):
                    nc.scalar.activation(pick_b[:], ones[:], ACT.Identity, scale=small(k, "ident")[0:NPAR, bass.ds(n, 1)])
                    nc.scalar.activation(pick_c[:], ones[:], ACT.Identity,
                                         scale=small(k, "ident")[0:NPAR, bass.ds(n + NS, 1)]).then_inc(rows_picked, 1)

                def decays(n):
                    for c in range(C):
                        nc.scalar.activation(decay[c][:, :, 1:], dt[:].rearrange("p (b l) -> p b l", l=S)[:, :, 1:],
                                             ACT.Exp, scale=a_neg[:, bass.ds(n + c * NS, 1)]).then_inc(decayed, 1)

                nc.scalar.activation(par_hi[:], par[:], ACT.Copy).then_inc(hi_kept, 1)
                act.wait_ge(ones_set, 1)
                rows(0)
                act.wait_ge(set_up, 1)
                decays(0)
                act.wait_ge(c_done, 1)
                nc.scalar.activation(c_row[:], c_ps[:].rearrange("p g n -> p (g n)"), ACT.Copy).then_inc(c_kept, 1)
                with act.Fori(0, NS - 1) as n:
                    act.wait_ge(c_done, n + 1)
                    rows(n + 1)
                    for c in range(C):
                        act.wait_ge(scanned, n * 2 + (c + 3))
                        nc.scalar.activation(decay[c][:, :, 1:], dt[:].rearrange("p (b l) -> p b l", l=S)[:, :, 1:],
                                             ACT.Exp, scale=a_neg[:, bass.ds(n + (c * NS + 1), 1)]).then_inc(decayed, 1)
                    act.wait_ge(c_done, n + 2)
                    act.wait_ge(read_done, n * 2 + 4)
                    nc.scalar.activation(c_row[:], c_ps[:].rearrange("p g n -> p (g n)"), ACT.Copy).then_inc(c_kept, 1)

            @block.tensor
            def _(pe):
                def spread(out, pick):
                    for g in range(2):
                        cols = slice(g * HALF, (g + 1) * HALF)
                        nc.tensor.matmul(out[:, g, :], pick[:], par_hi[:, cols], start=True, stop=False)
                        last = nc.tensor.matmul(out[:, g, :], pick[:], par_lo[:, cols], start=False, stop=True)
                    return last

                def add(c, final):
                    for g in range(2):
                        last = nc.tensor.matmul(y_ps[:, c, g, :], k.ident, read[c][:, g * HALF:(g + 1) * HALF],
                                                start=False, stop=final, skip_group_check=True)
                    last.then_inc(y_added, 1)

                pe.sem_inc(y_added, 2)
                for c in range(C):
                    for g in range(2):
                        nc.tensor.matmul(y_ps[:, c, g, :], diag[:, c, :], xc[:, c, g * HALF:(g + 1) * HALF],
                                         start=True, stop=False, skip_group_check=True)
                pe.wait_ge(set_up, 1)
                pe.wait_ge(par_split, 1)
                pe.wait_ge(rows_picked, 1)
                spread(b_ps, pick_b).then_inc(b_done, 1)
                spread(c_ps, pick_c).then_inc(c_done, 1)
                with pe.Fori(0, NS - 1) as n:
                    pe.wait_ge(rows_picked, n + 2)
                    pe.wait_ge(driven, n * 2 + 2)
                    spread(b_ps, pick_b).then_inc(b_done, 1)
                    pe.wait_ge(c_kept, n + 1)
                    spread(c_ps, pick_c).then_inc(c_done, 1)
                    for c in range(C):
                        pe.wait_ge(read_done, n * 2 + (c + 3))
                        add(c, False)
                for c in range(C):
                    pe.wait_ge(read_done, (NS - 1) * 2 + c + 3)
                    add(c, True)

            @block.gpsimd
            def _(pool):
                pool.sem_inc(read_done, 2)
                with pool.Fori(0, NS) as n:
                    pool.wait_ge(c_kept, n + 1)
                    for c in range(C):
                        pool.wait_ge(scanned, n * 2 + (c + 3))
                        pool.wait_ge(y_added, n * 2 + (c + 1))
                        nc.gpsimd.tensor_tensor(read[c][:], state[c][:], c_row[:], ALU.mult).then_inc(read_done, 1)

            @block.vector
            def _(dve):
                dve.sem_inc(scanned, 2)
                nc.vector.memset(ones[:], 1.0).then_inc(ones_set, 1)
                dve.wait_ge(hi_kept, 1)
                nc.vector.tensor_tensor(par_lo[:], par[:], par_hi[:].bitcast(F32), ALU.subtract).then_inc(par_split, 1)
                for c in range(C):
                    last = nc.vector.memset(decay[c][:], 0.0)
                last.then_inc(set_up, 1)
                with dve.Fori(0, NS) as n:
                    dve.wait_ge(scanned, n * 2 + 2)
                    dve.wait_ge(b_done, n + 1)
                    for c in range(C):
                        nc.vector.tensor_tensor(drive[c][:], u[:, c, :], b_ps[:].rearrange("p g n -> p (g n)"),
                                                ALU.mult).then_inc(driven, 1)
                    for c in range(C):
                        dve.wait_ge(driven, n * 2 + (c + 1))
                        dve.wait_ge(decayed, n * 2 + (c + 1))
                        dve.wait_ge(read_done, n * 2 + (c + 1))
                        nc.vector.tensor_tensor_scan(state[c][:], decay[c][:].rearrange("p b l -> p (b l)"),
                                                     drive[c][:], 0.0, ALU.mult, ALU.add).then_inc(scanned, 1)
                for c in range(C):
                    dve.wait_ge(y_added, (NS - 1) * 2 + c + 3)
                    nc.vector.tensor_tensor(gated[:, c, :], y_ps[:, c].rearrange("p g n -> p (g n)"), gate[:, c, :],
                                            ALU.mult)

        with ExitStack() as ctx:
            o_ps = ctx.enter_context(nc.psum_tensor("scan_o_ps", [P, NT, BANK], F32))
            o_done = ctx.enter_context(nc.semaphore("scan_o_done"))
            block = ctx.enter_context(nc.Block())

            @block.tensor
            def _(pe):
                pe.wait_ge(w_out_in, 16)
                for t in range(NT):
                    for c in range(C):
                        last = nc.tensor.matmul(o_ps[:, t, 0:D], gated[:, c, t * P:(t + 1) * P], w_out[:, c, :],
                                                start=c == 0, stop=c == C - 1)
                    last.then_inc(o_done, 1)

            @block.vector
            def _(dve):
                for t in range(NT):
                    dve.wait_ge(o_done, t + 1)
                    nc.vector.tensor_tensor(k.x[:, t, :], k.x[:, t, :], o_ps[:, t, 0:D], ALU.add)


def perceiver_program(nc, src, out):
    with ExitStack() as ctx:
        k = Chip()

        def sb(name, shape, dt=F32, scope=ctx):
            return scope.enter_context(nc.sbuf_tensor(name, shape, dt))

        k.x = sb("x_sb", [P, NT, D])
        k.h_t = sb("h_t", [P, C, T])
        k.small = sb("small", [P, SMALL_N])
        k.ident = small(k, "ident")
        k.ones = sb("ones", [P, P])
        k.minus_half = sb("minus_half", [P, 1])
        k.log_s = sb("log_s", [P, 1])
        k.length = sb("length", [P, NB])
        k.far_count = sb("far_count", [1, 1], I32)
        k.combine = sb("combine", [P, NT, E1])
        k.bo1 = sb("bo1", [1, D])
        with ExitStack() as attentions:
            rows = k.rows = sb("rows", [1, len(ROWS), D], scope=attentions)
            k.early = sb("early", [P, EARLY_N], scope=attentions)
            k.row = lambda name: rows[:, ROWS[name], :]
            with ExitStack() as local:
                k.iota_all = sb("iota_all", [P, NWIN * WN], scope=local)
                k.q0 = sb("q0", [P, C, T], scope=local)
                k.pos = sb("pos", [P, NB + 1, PK], scope=local)
                k.ctx_t = sb("ctx_out_t", [P, C, T], scope=local)
                k.wq0, k.woff0 = sb("wq0", [P, C, D], scope=local), sb("woff0", [P, C, 2, PK], scope=local)
                k.wk0, k.wv0 = sb("wk0", [P, C, D], scope=local), sb("wv0", [P, C, D], scope=local)
                k.wq0_in, k.woff0_in, k.wkv0_in, k.iota_in = (
                    local.enter_context(nc.semaphore(n)) for n in ("wq0_in", "woff0_in", "wkv0_in", "iota_in"))

                def load_local(sp):
                    for buffer, name, loaded in ((k.wq0, "wq0", k.wq0_in), (k.woff0, "woff0", k.woff0_in),
                                                 (k.wk0, "wk0", k.wkv0_in), (k.wv0, "wv0", k.wkv0_in),
                                                 (k.iota_all, "iota_all", k.iota_in)):
                        sp.dma_start(buffer[:], src[name]).then_inc(loaded, 16)

                load_stage(nc, k, src)
                norm_stage(nc, k, "a", load=load_local)
                positions_stage(nc, k, src)
                local_attention(nc, k, src)
                after_local(nc, k, src)
            norm_stage(nc, k, "b")
            self_attention(nc, k, src)
        with ExitStack() as cross:
            first = CrossFirst(nc, cross, src)
            with ExitStack() as ffn:
                w = ExpertWeights(nc, ffn, 0, src["up0"], src["down0"])
                norm_stage(nc, k, "c", load=lambda sp: w.load(sp, 0))
                route(nc, k, 0, w)
                experts(nc, k, 0, w, ACT.Gelu_apprx_tanh, first)
            norm_stage(nc, k, "d", clear=True)
            cross_attention(nc, k, src, first)
        norm_stage(nc, k, "e")
        scan_layer(nc, k, src)
        w = ExpertWeights(nc, ctx, 1, src["up1"], src["down1"])
        norm_stage(nc, k, "f", load=lambda sp: w.load(sp, 0))
        route(nc, k, 1, w)
        experts(nc, k, 1, w, ACT.Silu)
        store_stage(nc, k, out)


def _small_arrays(np, a):
    part = np.arange(P)
    near = np.concatenate([np.arange(LOW), np.arange(HIGH, M)])
    loc = (part % S)[:, None]
    ref = np.tile(np.arange(NK) + (-NK // 2), PAIRS0)

    def rep(v):
        return np.broadcast_to(np.asarray(v).reshape(1, -1), (P, np.asarray(v).size))

    def cols(v):
        v = np.asarray(v).reshape(C, P, -1)
        return v.transpose(1, 0, 2).reshape(P, -1)

    boff = np.asarray(a["L0_xattn_boff"]).reshape(PAIRS0, 2, NK).transpose(1, 0, 2).reshape(2, PK)
    parts = dict(
        ident=np.eye(P), mask8=(part[:, None] // HD0 == np.arange(8)[None]) * 0.125,
        mask2=((part[:, None] % 32) // HD0 == np.arange(2)[None]), ref=rep(ref), loc=loc,
        boff=np.repeat(boff, S, axis=0), bq=cols(a["L0_xattn_bq"]), bk=cols(a["L0_xattn_bk"]),
        rscale=cols(a["L0_ffn_router_scale"]), pes=rep(a["L0_ffn_per_expert_scale"]),
        rw0=cols(a["L0_ffn_router_w"]), convw=cols(a["L1_attn_conv_w"]), convb=cols(a["L1_attn_conv_b"]),
        alog=cols(a["L1_attn_A_log"]), dpar=cols(a["L1_attn_D_param"]),
        rw1=cols(np.asarray(a["L1_ffn_router_w"]).T), rb1=rep(a["L1_ffn_router_bias"]),
    )
    early = dict(same=(part[:, None] // S == part[None] // S), iota=rep(near), ls=rep(a["L0_attn_layerscale"]))
    packed = []
    for arrays, places in ((parts, SMALL), (early, EARLY)):
        assert list(arrays) == list(places) and all(v.shape == (P, places[n][1]) for n, v in arrays.items())
        packed.append(np.concatenate([np.asarray(v, dtype=np.float32) for v in arrays.values()], axis=1))
    return packed


def _laid_out(np, a):
    def chunks(w):
        w = np.asarray(w)
        return w.reshape(w.shape[0] // P, P, -1).transpose(1, 0, 2)

    ctx = np.asarray(a["ctx_1024"])
    ctx_t = np.zeros((NB, P, C, MPAD), ctx.dtype)
    ctx_t[..., :M] = ctx.transpose(0, 2, 1).reshape(NB, C, P, M).transpose(0, 2, 1, 3)
    ctx_n = np.zeros((NB, NBLK, P, D), ctx.dtype)
    ctx_n[:, 0, :TXT] = ctx[:, :TXT]
    ctx_n[:, 1:, :IBLK] = ctx[:, TXT:].reshape(NB, IB, IBLK, D)
    woff = np.asarray(a["L0_xattn_Woff"]).reshape(PAIRS0, 2, NK, D).transpose(1, 0, 2, 3).reshape(2 * PK, D)
    up0 = np.asarray(a["L0_ffn_gating_w"]).reshape(E0, 2 * HID, C, P)
    up1 = np.stack([np.asarray(a["L1_ffn_gate_w"]).reshape(GROUPS, HID, D),
                    np.asarray(a["L1_ffn_up_w"]).reshape(GROUPS, HID, D)], axis=1)
    shared = np.stack([np.asarray(a["L1_ffn_sgate_w"]), np.asarray(a["L1_ffn_sup_w"])])[None]
    up1 = np.concatenate([up1, shared], axis=0).reshape(GROUPS + 1, 2 * HID, C, P)
    down1 = np.asarray(a["L1_ffn_down_w"]).reshape(GROUPS, HC, D, P).transpose(0, 3, 1, 2)
    sdown = np.asarray(a["L1_ffn_sdown_w"]).T.reshape(1, HC, P, D).transpose(0, 2, 1, 3)
    rows = np.arange(NWIN * WN)
    packed = _small_arrays(np, a)
    laid = dict(
        iota_all=np.broadcast_to(np.where(rows < M, rows, 1 << 20).astype(np.float32), (P, NWIN * WN)),
        x=np.asarray(a["x"]).reshape(T, D), mask=a["mask_BxS2_if0"], small=packed[0], early=packed[1],
        rows=np.stack([np.asarray(a[n]) for n in ("L0_xattn_bv", "L0_xattn_bo", "L0_attn_bq", "L0_attn_bk",
                                                  "L0_attn_bv", "L0_attn_bo")])[None],
        bo1=np.asarray(a["L1_xattn_bo"])[None],
        ctx_t=ctx_t, ctx_n=ctx_n.transpose(0, 2, 1, 3),
        wq0=chunks(np.asarray(a["L0_xattn_Wq"]).T), wk0=chunks(np.asarray(a["L0_xattn_Wk"]).T),
        wv0=chunks(np.asarray(a["L0_xattn_Wv"]).T), wo0=chunks(np.asarray(a["L0_xattn_Wo"]).T),
        woff0=chunks(woff.T).reshape(P, C, 2, PK),
        wqa=chunks(np.asarray(a["L0_attn_Wq"]).T), wka=chunks(np.asarray(a["L0_attn_Wk"]).T),
        wva=chunks(np.asarray(a["L0_attn_Wv"]).T), woa=chunks(np.asarray(a["L0_attn_Wo"]).T),
        up0=up0.transpose(0, 3, 2, 1), down0=np.asarray(a["L0_ffn_linear_w"]).reshape(E0, HC, P, D).transpose(0, 2, 1, 3),
        wq1=chunks(a["L1_xattn_Wq"]),
        wk1=np.stack([chunks(np.asarray(a[n]).T) for n in ("L1_xattn_Wk", "L1_xattn_Wk_ip")], axis=1),
        wv1=np.stack([chunks(a[n]) for n in ("L1_xattn_Wv", "L1_xattn_Wv_ip")], axis=1),
        wo1=chunks(a["L1_xattn_Wo"]),
        win=chunks(np.asarray(a["L1_attn_in_proj_w"]).T), wpar=chunks(np.asarray(a["L1_attn_x_proj_w"]).T),
        wout=chunks(np.asarray(a["L1_attn_out_proj_w"]).T),
        up1=up1.transpose(0, 3, 2, 1), down1=np.concatenate([down1, sdown], axis=0),
    )
    return {n: np.ascontiguousarray(v) for n, v in laid.items()}


def kernel(**inputs):
    import numpy as np
    import concourse.bacc as bacc
    from concourse.bass_utils import run_bass_kernel_spmd

    nc = bacc.Bacc("TRN2", target_bir_lowering=False, num_devices=1)
    laid = _laid_out(np, inputs)
    arrays = {f"in_{n}": v for n, v in laid.items()}
    aps = {n: nc.dram_tensor(f"in_{n}", v.shape, mybir.dt.from_np(v.dtype), kind="ExternalInput").ap()
           for n, v in laid.items()}
    out = nc.dram_tensor("out_x", (T, D), F32, kind="ExternalOutput").ap()
    perceiver_program(nc, aps, out)
    r = run_bass_kernel_spmd(nc, [arrays], core_ids=[0])
    return r.results[0]["out_x"].reshape(NB, S, D)
```
